# Optimizing a Trainium2 kernel written in Bass

```python
import numpy as np
import jax
import jax.numpy as jnp

def _softmax(x, axis=-1):
    return jax.nn.softmax(x, axis=axis)

def _gelu(x):
    return jax.nn.gelu(x, approximate=True)

def _silu(x):
    return jax.nn.silu(x)

def _sigmoid(x):
    return jax.nn.sigmoid(x)

def _layernorm(x, axis=-1, eps=1e-05):
    m = jnp.mean(x, axis=axis, keepdims=True)
    v = jnp.var(x, axis=axis, keepdims=True)
    return (x - m) / jnp.sqrt(v + eps)

def _scatter_add(tgt, idx, src, axis=0):
    return tgt.at[idx].add(src)

def _segment_sum(src, seg, n):
    return jax.ops.segment_sum(src, seg, n)
kernel_name = 'mk_decoder_preln_d2_seqx_r8_40bdb0'

def setup_inputs(seed: int=0):
    np.random.seed(seed)
    _w = jnp.asarray

    def _rec_inputs():
        import jax
        import jax.numpy as jnp
        _rk = jax.random.key(seed)
        x = -0.0002928 + 1 * jax.random.normal(jax.random.fold_in(_rk, 1), (64, 128, 128), jnp.float32)
        _lenS = 128 - jax.random.randint(jax.random.fold_in(_rk, 7), (64,), 0, max(1, 128 // 4) + 1, jnp.int32)
        _lenS2 = 120 - jax.random.randint(jax.random.fold_in(_rk, 8), (64,), 0, max(1, 120 // 4) + 1, jnp.int32)
        _ctx_1024P = jax.random.normal(jax.random.fold_in(_rk, 11), (64, 16, 128), jnp.float32)
        _ctx_1024c = jax.random.dirichlet(jax.random.fold_in(_rk, 511), 0.3 * jnp.ones((16,), jnp.float32), (64, 120))
        _ctx_1024t = jnp.einsum('bsk,bkd->bsd', _ctx_1024c, _ctx_1024P)
        _ctx_1024t = _ctx_1024t * jax.lax.rsqrt(jnp.mean(jnp.square(_ctx_1024t)) + 1e-12) * 0.953939
        ctx_1024 = -1.39393e-06 + 0.999914 * (_ctx_1024t + 0.3 * jax.random.normal(jax.random.fold_in(_rk, 611), (64, 120, 128), jnp.float32))
        _validS = jnp.arange(128)[None, :] < _lenS[:, None]
        _validS2 = jnp.arange(120)[None, :] < _lenS2[:, None]
        _causal = jnp.tril(jnp.ones((128, 128), dtype=bool))
        mask_1x1xSxS2_ik0 = jnp.where(jnp.broadcast_to(_validS2[0:1, None, None, :], (1, 1, 128, 120)), 0, 1).astype(jnp.int32)
        return (x, ctx_1024, mask_1x1xSxS2_ik0)
    x, ctx_1024, mask_1x1xSxS2_ik0 = _rec_inputs()

    def _L0_attn_setup():
        import jax, jax.numpy as jnp
        import numpy as np
        N_HEAD = 16
        NEG_BIG = -10000000000.0

        def _rope_cos_sin(T, head_dim, dtype):
            half = head_dim // 2
            i = jnp.arange(half, dtype=jnp.float32)
            theta = 1.0 / 10000.0 ** (2.0 * i / head_dim)
            t = jnp.arange(T, dtype=jnp.float32)[:, None]
            ang = t * theta[None, :]
            return (jnp.cos(ang).astype(dtype), jnp.sin(ang).astype(dtype))

        def _apply_rope(x, cos, sin):
            B, H, T, D = x.shape
            xr = x.reshape(B, H, T, D // 2, 2)
            x0, x1 = (xr[..., 0], xr[..., 1])
            c = cos[None, None, :, :]
            s = sin[None, None, :, :]
            out = jnp.stack((x0 * c - x1 * s, x0 * s + x1 * c), axis=-1)
            return out.reshape(B, H, T, D)
        key = jax.random.key(seed)
        ks = jax.random.split(key, 9)
        B, T, C = (4, 256, 128)
        sc = 1.0 / np.sqrt(C)
        return {'x': jax.random.normal(ks[0], (B, T, C), jnp.float32), 'wq': jax.random.normal(ks[1], (C, C), jnp.float32) * sc, 'bq': jax.random.normal(ks[2], (C,), jnp.float32) * 0.02, 'wk': jax.random.normal(ks[3], (C, C), jnp.float32) * sc, 'bk': jax.random.normal(ks[4], (C,), jnp.float32) * 0.02, 'wv': jax.random.normal(ks[5], (C, C), jnp.float32) * sc, 'bv': jax.random.normal(ks[6], (C,), jnp.float32) * 0.02, 'wp': jax.random.normal(ks[7], (C, C), jnp.float32) * sc, 'bp': jax.random.normal(ks[8], (C,), jnp.float32) * 0.02}
    _L0_attn_all = _L0_attn_setup()
    _L0_attn_in = {k: v for k, v in _L0_attn_all.items() if k in ('wq', 'bq', 'wk', 'bk', 'wv', 'bv', 'wp', 'bp')}
    del _L0_attn_all

    def _L0_xattn_setup():
        import jax, jax.numpy as jnp
        import numpy as np
        D_EMB = 128
        N_HEADS = 16
        D_HEAD = D_EMB // N_HEADS
        B, S = (2, 256)

        def _split_heads(x):
            b, s, _ = x.shape
            return x.reshape(b, s, N_HEADS, D_HEAD).transpose(0, 2, 1, 3)
        key = jax.random.key(seed)
        ks = jax.random.split(key, 10)
        s = 1.0 / np.sqrt(D_EMB)
        inp = {'queries': jax.random.normal(ks[0], (B, S, D_EMB), jnp.float32), 'values': jax.random.normal(ks[1], (B, S, D_EMB), jnp.float32), 'mask': jnp.tril(jnp.ones((S, S), jnp.int32))[None, None], 'Wq': jax.random.normal(ks[2], (D_EMB, D_EMB), jnp.float32) * s, 'bq': jnp.zeros((D_EMB,), jnp.float32), 'Wk': jax.random.normal(ks[3], (D_EMB, D_EMB), jnp.float32) * s, 'bk': jnp.zeros((D_EMB,), jnp.float32), 'Wv': jax.random.normal(ks[4], (D_EMB, D_EMB), jnp.float32) * s, 'bv': jnp.zeros((D_EMB,), jnp.float32), 'Wo': jax.random.normal(ks[5], (D_EMB, D_EMB), jnp.float32) * s, 'bo': jnp.zeros((D_EMB,), jnp.float32)}
        return inp
    _L0_xattn_all = _L0_xattn_setup()
    _L0_xattn_in = {k: v for k, v in _L0_xattn_all.items() if k in ('Wq', 'bq', 'Wk', 'bk', 'Wv', 'bv', 'Wo', 'bo')}
    del _L0_xattn_all

    def _L0_ffn_setup():
        import jax, jax.numpy as jnp
        import numpy as np
        key = jax.random.key(seed)
        kx, kw = jax.random.split(key)
        x = jax.random.normal(kx, (32, 512, 128), dtype=jnp.float32)
        weight = jax.random.normal(kw, (128, 128), dtype=jnp.float32) * 0.01
        return {'x': x, 'weight': weight}
    _L0_ffn_all = _L0_ffn_setup()
    _L0_ffn_in = {k: v for k, v in _L0_ffn_all.items() if k in ('weight',)}
    del _L0_ffn_all

    def _L1_attn_setup():
        import jax, jax.numpy as jnp
        import numpy as np
        import math
        EPS = 1e-06

        def favorplus_features(x, proj):
            xw = jnp.einsum('bhtd,hmd->bhtm', x, proj)
            xw = xw - jnp.max(xw, axis=-1, keepdims=True)
            x_norm_sq = jnp.sum(x * x, axis=-1, keepdims=True)
            return jnp.exp(xw) * jnp.exp(-0.5 * x_norm_sq) + EPS
        key = jax.random.key(seed)
        ks = jax.random.split(key, 6)
        B, T, d = (2, 512, 128)
        h, m = (16, 32)
        dk = d // h
        s = 1.0 / math.sqrt(d)
        return {'x': jax.random.normal(ks[0], (B, T, d), dtype=jnp.float32), 'Wq': jax.random.normal(ks[1], (d, d), dtype=jnp.float32) * s, 'Wk': jax.random.normal(ks[2], (d, d), dtype=jnp.float32) * s, 'Wv': jax.random.normal(ks[3], (d, d), dtype=jnp.float32) * s, 'Wo': jax.random.normal(ks[4], (d, d), dtype=jnp.float32) * s, 'bo': jnp.zeros((d,), dtype=jnp.float32), 'proj': jax.random.normal(ks[5], (h, m, dk), dtype=jnp.float32)}
    _L1_attn_all = _L1_attn_setup()
    _L1_attn_in = {k: v for k, v in _L1_attn_all.items() if k in ('Wq', 'Wk', 'Wv', 'Wo', 'bo', 'proj')}
    del _L1_attn_all

    def _L1_xattn_setup():
        import jax, jax.numpy as jnp
        import numpy as np
        B, N, F = (2, 256, 128)
        H = 16
        DH = F // H
        SCALE = 1.0 / np.sqrt(DH)
        key = jax.random.key(seed)
        ks = jax.random.split(key, 11)
        s = 0.02
        return {'q': jax.random.normal(ks[0], (B, N, F), dtype=jnp.float32), 'k': jax.random.normal(ks[1], (B, N, F), dtype=jnp.float32), 'v': jax.random.normal(ks[2], (B, N, F), dtype=jnp.float32), 'Wq': jax.random.normal(ks[3], (F, F), dtype=jnp.float32) * s, 'bq': jnp.zeros((F,), dtype=jnp.float32), 'Wk': jax.random.normal(ks[4], (F, F), dtype=jnp.float32) * s, 'bk': jnp.zeros((F,), dtype=jnp.float32), 'Wv': jax.random.normal(ks[5], (F, F), dtype=jnp.float32) * s, 'bv': jnp.zeros((F,), dtype=jnp.float32), 'Wo': jax.random.normal(ks[6], (F, F), dtype=jnp.float32) * s, 'bo': jnp.zeros((F,), dtype=jnp.float32)}
    _L1_xattn_all = _L1_xattn_setup()
    _L1_xattn_in = {k: v for k, v in _L1_xattn_all.items() if k in ('Wq', 'bq', 'Wk', 'bk', 'Wv', 'bv', 'Wo', 'bo')}
    del _L1_xattn_all

    def _L1_ffn_setup():
        import jax, jax.numpy as jnp
        import numpy as np
        H = 128
        I = 88
        E = 64
        TOP_K = 8
        NG = 8
        TOPK_GROUP = 4
        N_SHARED = 2
        ROUTED_SCALE = 2.5
        S_I = I * N_SHARED

        def _route(x, gate_w, gate_bias):
            T = x.shape[0]
            logits = x @ gate_w.T
            scores = jax.nn.sigmoid(logits)
            scores_for_choice = scores + gate_bias[None, :]
            grp = scores_for_choice.reshape(T, NG, E // NG)
            group_scores = jnp.sum(jax.lax.top_k(grp, 2)[0], axis=-1)
            _, gidx = jax.lax.top_k(group_scores, TOPK_GROUP)
            gmask = jnp.zeros((T, NG), dtype=scores.dtype).at[jnp.arange(T)[:, None], gidx].set(1.0)
            emask = jnp.repeat(gmask, E // NG, axis=1)
            masked = jnp.where(emask > 0, scores_for_choice, 0.0)
            _, topk_idx = jax.lax.top_k(masked, TOP_K)
            topk_w = jnp.take_along_axis(scores, topk_idx, axis=1)
            topk_w = topk_w / (jnp.sum(topk_w, axis=-1, keepdims=True) + 1e-20)
            topk_w = topk_w * ROUTED_SCALE
            rw = jnp.zeros((T, E), dtype=scores.dtype).at[jnp.arange(T)[:, None], topk_idx].add(topk_w)
            return rw

        def _mlp(x, gw, uw, dw):
            return jax.nn.silu(x @ gw.T) * (x @ uw.T) @ dw.T
        key = jax.random.key(seed)
        ks = jax.random.split(key, 10)
        sc = 0.02
        return {'hidden_states': jax.random.normal(ks[0], (1, 128, H), dtype=jnp.float32), 'gate_w': sc * jax.random.normal(ks[1], (E, H), dtype=jnp.float32), 'gate_bias': sc * jax.random.normal(ks[2], (E,), dtype=jnp.float32), 'Wg': sc * jax.random.normal(ks[3], (E, I, H), dtype=jnp.float32), 'Wu': sc * jax.random.normal(ks[4], (E, I, H), dtype=jnp.float32), 'Wd': sc * jax.random.normal(ks[5], (E, H, I), dtype=jnp.float32), 'Sg': sc * jax.random.normal(ks[6], (S_I, H), dtype=jnp.float32), 'Su': sc * jax.random.normal(ks[7], (S_I, H), dtype=jnp.float32), 'Sd': sc * jax.random.normal(ks[8], (H, S_I), dtype=jnp.float32)}
    _L1_ffn_all = _L1_ffn_setup()
    _L1_ffn_in = {k: v for k, v in _L1_ffn_all.items() if k in ('gate_w', 'gate_bias', 'Wg', 'Wu', 'Wd', 'Sg', 'Su', 'Sd')}
    del _L1_ffn_all
    return {'x': x, 'ctx_1024': ctx_1024, 'mask_1x1xSxS2_ik0': mask_1x1xSxS2_ik0, 'L0_attn_wq': _L0_attn_in['wq'], 'L0_attn_bq': _L0_attn_in['bq'], 'L0_attn_wk': _L0_attn_in['wk'], 'L0_attn_bk': _L0_attn_in['bk'], 'L0_attn_wv': _L0_attn_in['wv'], 'L0_attn_bv': _L0_attn_in['bv'], 'L0_attn_wp': _L0_attn_in['wp'], 'L0_attn_bp': _L0_attn_in['bp'], 'L0_xattn_Wq': _L0_xattn_in['Wq'], 'L0_xattn_bq': _L0_xattn_in['bq'], 'L0_xattn_Wk': _L0_xattn_in['Wk'], 'L0_xattn_bk': _L0_xattn_in['bk'], 'L0_xattn_Wv': _L0_xattn_in['Wv'], 'L0_xattn_bv': _L0_xattn_in['bv'], 'L0_xattn_Wo': _L0_xattn_in['Wo'], 'L0_xattn_bo': _L0_xattn_in['bo'], 'L0_ffn_weight': _L0_ffn_in['weight'], 'L1_attn_Wq': _L1_attn_in['Wq'], 'L1_attn_Wk': _L1_attn_in['Wk'], 'L1_attn_Wv': _L1_attn_in['Wv'], 'L1_attn_Wo': _L1_attn_in['Wo'], 'L1_attn_bo': _L1_attn_in['bo'], 'L1_attn_proj': _L1_attn_in['proj'], 'L1_xattn_Wq': _L1_xattn_in['Wq'], 'L1_xattn_bq': _L1_xattn_in['bq'], 'L1_xattn_Wk': _L1_xattn_in['Wk'], 'L1_xattn_bk': _L1_xattn_in['bk'], 'L1_xattn_Wv': _L1_xattn_in['Wv'], 'L1_xattn_bv': _L1_xattn_in['bv'], 'L1_xattn_Wo': _L1_xattn_in['Wo'], 'L1_xattn_bo': _L1_xattn_in['bo'], 'L1_ffn_gate_w': _L1_ffn_in['gate_w'], 'L1_ffn_gate_bias': _L1_ffn_in['gate_bias'], 'L1_ffn_Wg': _L1_ffn_in['Wg'], 'L1_ffn_Wu': _L1_ffn_in['Wu'], 'L1_ffn_Wd': _L1_ffn_in['Wd'], 'L1_ffn_Sg': _L1_ffn_in['Sg'], 'L1_ffn_Su': _L1_ffn_in['Su'], 'L1_ffn_Sd': _L1_ffn_in['Sd']}

def reference(x, ctx_1024, mask_1x1xSxS2_ik0, L0_attn_wq, L0_attn_bq, L0_attn_wk, L0_attn_bk, L0_attn_wv, L0_attn_bv, L0_attn_wp, L0_attn_bp, L0_xattn_Wq, L0_xattn_bq, L0_xattn_Wk, L0_xattn_bk, L0_xattn_Wv, L0_xattn_bv, L0_xattn_Wo, L0_xattn_bo, L0_ffn_weight, L1_attn_Wq, L1_attn_Wk, L1_attn_Wv, L1_attn_Wo, L1_attn_bo, L1_attn_proj, L1_xattn_Wq, L1_xattn_bq, L1_xattn_Wk, L1_xattn_bk, L1_xattn_Wv, L1_xattn_bv, L1_xattn_Wo, L1_xattn_bo, L1_ffn_gate_w, L1_ffn_gate_bias, L1_ffn_Wg, L1_ffn_Wu, L1_ffn_Wd, L1_ffn_Sg, L1_ffn_Su, L1_ffn_Sd):
    import jax
    import jax.numpy as jnp

    def _L0_attn_ref(x, wq, bq, wk, bk, wv, bv, wp, bp):
        import jax, jax.numpy as jnp
        import numpy as np
        N_HEAD = 16
        NEG_BIG = -10000000000.0

        def _rope_cos_sin(T, head_dim, dtype):
            half = head_dim // 2
            i = jnp.arange(half, dtype=jnp.float32)
            theta = 1.0 / 10000.0 ** (2.0 * i / head_dim)
            t = jnp.arange(T, dtype=jnp.float32)[:, None]
            ang = t * theta[None, :]
            return (jnp.cos(ang).astype(dtype), jnp.sin(ang).astype(dtype))

        def _apply_rope(x, cos, sin):
            B, H, T, D = x.shape
            xr = x.reshape(B, H, T, D // 2, 2)
            x0, x1 = (xr[..., 0], xr[..., 1])
            c = cos[None, None, :, :]
            s = sin[None, None, :, :]
            out = jnp.stack((x0 * c - x1 * s, x0 * s + x1 * c), axis=-1)
            return out.reshape(B, H, T, D)
        B, T, C = x.shape
        H = N_HEAD
        D = C // H

        def proj(w, b):
            return (jnp.einsum('btc,oc->bto', x, w) + b).reshape(B, T, H, D).transpose(0, 2, 1, 3)
        q = proj(wq, bq)
        k = proj(wk, bk)
        v = proj(wv, bv)
        cos, sin = _rope_cos_sin(T, D, x.dtype)
        q = _apply_rope(q, cos, sin)
        k = _apply_rope(k, cos, sin)
        att = jnp.einsum('bhtd,bhsd->bhts', q, k) * (1.0 / np.sqrt(D))
        causal = jnp.tril(jnp.ones((T, T), bool))
        att = jnp.where(causal[None, None], att, jnp.asarray(NEG_BIG, att.dtype))
        att = jax.nn.softmax(att, axis=-1)
        y = jnp.einsum('bhts,bhsd->bhtd', att, v)
        y = y.transpose(0, 2, 1, 3).reshape(B, T, C)
        return jnp.einsum('btc,oc->bto', y, wp) + bp

    def _L0_xattn_ref(queries, values, mask, Wq, bq, Wk, bk, Wv, bv, Wo, bo):
        import jax, jax.numpy as jnp
        import numpy as np
        D_EMB = 128
        N_HEADS = 16
        D_HEAD = D_EMB // N_HEADS
        B, S = (2, 256)

        def _split_heads(x):
            b, s, _ = x.shape
            return x.reshape(b, s, N_HEADS, D_HEAD).transpose(0, 2, 1, 3)
        q = _split_heads(queries @ Wq.T + bq)
        k = _split_heads(values @ Wk.T + bk)
        v = _split_heads(values @ Wv.T + bv)
        logits = jnp.einsum('bhqd,bhkd->bhqk', q, k) / np.sqrt(D_HEAD)
        logits = jnp.where(mask == 0, jnp.float32(-1000000000.0), logits)
        probs = jax.nn.softmax(logits, axis=-1)
        ctx = jnp.einsum('bhqk,bhkd->bhqd', probs, v)
        ctx = ctx.transpose(0, 2, 1, 3).reshape(queries.shape[0], queries.shape[1], D_EMB)
        return ctx @ Wo.T + bo

    def _L0_ffn_ref(x, weight):
        import jax, jax.numpy as jnp
        import numpy as np
        b_weight = jnp.sign(weight)
        return jnp.einsum('bsi,oi->bso', x, b_weight)

    def _L1_attn_ref(x, Wq, Wk, Wv, Wo, bo, proj):
        import jax, jax.numpy as jnp
        import numpy as np
        import math
        EPS = 1e-06

        def favorplus_features(x, proj):
            xw = jnp.einsum('bhtd,hmd->bhtm', x, proj)
            xw = xw - jnp.max(xw, axis=-1, keepdims=True)
            x_norm_sq = jnp.sum(x * x, axis=-1, keepdims=True)
            return jnp.exp(xw) * jnp.exp(-0.5 * x_norm_sq) + EPS
        B, T, d = x.shape
        h, m, dk = proj.shape

        def heads(W):
            y = jnp.einsum('btd,ed->bte', x, W)
            return y.reshape(B, T, h, dk).transpose(0, 2, 1, 3)
        Q = heads(Wq) / math.sqrt(dk)
        K = heads(Wk) / math.sqrt(dk)
        V = heads(Wv)
        inv_sqrt_m = 1.0 / math.sqrt(m)
        phiQ = favorplus_features(Q, proj) * inv_sqrt_m
        phiK = favorplus_features(K, proj) * inv_sqrt_m
        KV = jnp.einsum('bhtm,bhtd->bhmd', phiK, V)
        Ksum = jnp.sum(phiK, axis=2)
        num = jnp.einsum('bhtm,bhmd->bhtd', phiQ, KV)
        den = jnp.einsum('bhtm,bhm->bht', phiQ, Ksum)[..., None] + EPS
        out_heads = num / den
        merged = out_heads.transpose(0, 2, 1, 3).reshape(B, T, d)
        return jnp.einsum('btd,ed->bte', merged, Wo) + bo

    def _L1_xattn_ref(q, k, v, Wq, bq, Wk, bk, Wv, bv, Wo, bo):
        import jax, jax.numpy as jnp
        import numpy as np
        B, N, F = (2, 256, 128)
        H = 16
        DH = F // H
        SCALE = 1.0 / np.sqrt(DH)
        b = q.shape[0]
        qh = (q @ Wq + bq).reshape(b, -1, H, DH).transpose(0, 2, 1, 3)
        kh = (k @ Wk + bk).reshape(b, -1, H, DH).transpose(0, 2, 1, 3)
        vh = (v @ Wv + bv).reshape(b, -1, H, DH).transpose(0, 2, 1, 3)
        attn = jnp.einsum('bhqd,bhkd->bhqk', qh * SCALE, kh)
        attn = jax.nn.softmax(attn, axis=-1)
        out = jnp.einsum('bhqk,bhkd->bhqd', attn, vh)
        out = out.transpose(0, 2, 1, 3).reshape(b, -1, H * DH)
        return out @ Wo + bo

    def _L1_ffn_ref(hidden_states, gate_w, gate_bias, Wg, Wu, Wd, Sg, Su, Sd):
        import jax, jax.numpy as jnp
        import numpy as np
        H = 128
        I = 88
        E = 64
        TOP_K = 8
        NG = 8
        TOPK_GROUP = 4
        N_SHARED = 2
        ROUTED_SCALE = 2.5
        S_I = I * N_SHARED

        def _route(x, gate_w, gate_bias):
            T = x.shape[0]
            logits = x @ gate_w.T
            scores = jax.nn.sigmoid(logits)
            scores_for_choice = scores + gate_bias[None, :]
            grp = scores_for_choice.reshape(T, NG, E // NG)
            group_scores = jnp.sum(jax.lax.top_k(grp, 2)[0], axis=-1)
            _, gidx = jax.lax.top_k(group_scores, TOPK_GROUP)
            gmask = jnp.zeros((T, NG), dtype=scores.dtype).at[jnp.arange(T)[:, None], gidx].set(1.0)
            emask = jnp.repeat(gmask, E // NG, axis=1)
            masked = jnp.where(emask > 0, scores_for_choice, 0.0)
            _, topk_idx = jax.lax.top_k(masked, TOP_K)
            topk_w = jnp.take_along_axis(scores, topk_idx, axis=1)
            topk_w = topk_w / (jnp.sum(topk_w, axis=-1, keepdims=True) + 1e-20)
            topk_w = topk_w * ROUTED_SCALE
            rw = jnp.zeros((T, E), dtype=scores.dtype).at[jnp.arange(T)[:, None], topk_idx].add(topk_w)
            return rw

        def _mlp(x, gw, uw, dw):
            return jax.nn.silu(x @ gw.T) * (x @ uw.T) @ dw.T
        B, S, _ = hidden_states.shape
        x = hidden_states.reshape(B * S, H)
        rw = _route(x, gate_w, gate_bias)
        expert_out = jax.vmap(lambda gw_, uw_, dw_: _mlp(x, gw_, uw_, dw_))(Wg, Wu, Wd)
        routed = jnp.einsum('eth,te->th', expert_out, rw)
        shared = _mlp(x, Sg, Su, Sd)
        out = (routed + shared).reshape(B, S, H)
        return out
    x = x + _L0_attn_ref(_layernorm(x, axis=-1), L0_attn_wq, L0_attn_bq, L0_attn_wk, L0_attn_bk, L0_attn_wv, L0_attn_bv, L0_attn_wp, L0_attn_bp)
    x = x + _L0_xattn_ref(_layernorm(x, axis=-1), ctx_1024, mask_1x1xSxS2_ik0, L0_xattn_Wq, L0_xattn_bq, L0_xattn_Wk, L0_xattn_bk, L0_xattn_Wv, L0_xattn_bv, L0_xattn_Wo, L0_xattn_bo)
    x = x + _L0_ffn_ref(_layernorm(x, axis=-1), L0_ffn_weight)
    x = x + _L1_attn_ref(_layernorm(x, axis=-1), L1_attn_Wq, L1_attn_Wk, L1_attn_Wv, L1_attn_Wo, L1_attn_bo, L1_attn_proj)
    x = x + _L1_xattn_ref(_layernorm(x, axis=-1), ctx_1024, ctx_1024, L1_xattn_Wq, L1_xattn_bq, L1_xattn_Wk, L1_xattn_bk, L1_xattn_Wv, L1_xattn_bv, L1_xattn_Wo, L1_xattn_bo)
    x = x + _L1_ffn_ref(_layernorm(x, axis=-1), L1_ffn_gate_w, L1_ffn_gate_bias, L1_ffn_Wg, L1_ffn_Wu, L1_ffn_Wd, L1_ffn_Sg, L1_ffn_Su, L1_ffn_Sd)
    return x

_drawn_inputs = setup_inputs


def setup_inputs(seed=0):
    import zlib

    import numpy as np

    out = dict(_drawn_inputs(seed))
    spreads = {'L0_xattn_bq': (0.0, 0.314),
     'L0_xattn_bk': (0.0, 2.0),
     'L0_xattn_bv': (0.0, 0.1),
     'L0_xattn_bo': (0.0, 0.1),
     'L1_attn_bo': (0.0, 0.8),
     'L1_xattn_bq': (0.0, 0.8),
     'L1_xattn_bk': (0.0, 2.0),
     'L1_xattn_bv': (0.0, 0.8),
     'L1_xattn_bo': (0.0, 0.8)}
    factors = {'L0_attn_bq': 8.0,
     'L0_attn_bk': 8.0,
     'L0_attn_bv': 3.239,
     'L0_attn_bp': 3.442,
     'L1_attn_Wq': 64.0,
     'L1_attn_Wk': 200.0,
     'L1_attn_proj': 64.0,
     'L1_xattn_Wq': 8.0,
     'L1_xattn_Wk': 8.0,
     'L1_xattn_Wv': 8.0,
     'L1_xattn_Wo': 8.0,
     'L1_ffn_gate_w': 8.0,
     'L1_ffn_gate_bias': 8.0,
     'L1_ffn_Wg': 8.0,
     'L1_ffn_Wu': 8.0,
     'L1_ffn_Wd': 8.0,
     'L1_ffn_Sg': 8.0,
     'L1_ffn_Su': 8.0,
     'L1_ffn_Sd': 8.0,
     'L1_attn_Wv': 64.0,
     'L1_attn_Wo': 64.0}
    for name, (base, spread) in spreads.items():
        noise = np.random.default_rng([zlib.crc32(name.encode()), seed]).standard_normal(out[name].shape)
        drawn = base * np.exp(spread * noise) if base else spread * noise
        out[name] = jnp.asarray(drawn.astype(out[name].dtype))
    for name, factor in factors.items():
        out[name] = (out[name] * factor).astype(out[name].dtype)
    return out
```

```python
from contextlib import ExitStack

import concourse.bass as bass
import numpy as np
from concourse import mybir
from concourse.alu_op_type import AluOpType as ALU

ACT = mybir.ActivationFunctionType
F32 = mybir.dt.float32
BF16 = mybir.dt.bfloat16
I32 = mybir.dt.int32
AX = mybir.AxisListType.X

P = 128
NSEQ = 64
SK = 120
H, DH = 16, 8
DA = DH + 1
PAD = 32
G = 4
TURNS = NSEQ // G
M = 32
E, I, TOPK, NG, TOPG = 64, 88, 8, 8, 4
REGION = NSEQ * P
NT = NSEQ * P * TOPK // P + E
TCOLS = -(-NT // P)
ROWS = E * REGION
LAST = REGION - P
SCALE = DH ** -0.5
LN_EPS, FAV_EPS = 1e-5, 1e-6
ROUTED = 2.5
GONE = -3.0e38

CONSTS = [("ident", P), ("causal", P), ("causal_t", P), ("upper", P), ("rope_c", 2 * P), ("rope_s", 2 * P),
          ("blocks", H * DA), ("first_slot", E), ("last_tile", E), ("tile_no", TCOLS), ("expert", E), ("before", NG * NG)]
BIASES = [("qkv0", 3 * P), ("o0", P), ("q_x0", P), ("ctx", 4 * P), ("o_x0", P), ("o_f", P), ("q_x1", P), ("o_x1", P),
          ("gate", E)]
WEIGHTS = [("qkv0", 3 * P), ("o0", P), ("q_x0", P), ("ctx", 4 * P), ("o_x0", P), ("ffn", P), ("qkv_f", 3 * P),
           ("proj_f", H * M), ("o_f", P), ("q_x1", P), ("o_x1", P), ("gate", E), ("shared_gu", 4 * I)]


def columns(parts):
    at, n = {}, 0
    for name, w in parts:
        at[name] = (n, n + w)
        n += w
    return at, n


def build(nc, x_d, ctx_d, mask_d, const_d, bias_d, weight_d, wgu_d, wdown_d, sdown_d, out_d,
          xs_d, ys_d, ln_d, res_d, tab_d):
    const_at, n_const = columns(CONSTS)
    bias_at, n_bias = columns(BIASES)
    w_at, n_w = columns(WEIGHTS)
    with ExitStack() as ctx:
        def sb(name, shape, dt=F32):
            return ctx.enter_context(nc.sbuf_tensor(name, shape, dt))

        def sem(name):
            return ctx.enter_context(nc.semaphore(name))

        wide = ctx.enter_context(nc.psum_tensor("wide", [P, 2, 2, 4, P], F32))
        bank = ctx.enter_context(nc.psum_tensor("bank", [P, G, 512], F32))

        consts = sb("consts", [P, n_const])
        biases = sb("biases", [P, n_bias])
        w = sb("w", [P, n_w])
        w_gu = sb("w_gu", [P, E * 2 * I])
        s_down = sb("s_down", [I, 2 * P])

        def const(name):
            return consts[:, const_at[name][0]:const_at[name][1]]

        def bias(name):
            return biases[:, bias_at[name][0]:bias_at[name][1]]

        def wt(name):
            return w[:, w_at[name][0]:w_at[name][1]]

        ident = const("ident")
        identb = sb("identb", [P, P], BF16)
        upperb = sb("upperb", [P, P], BF16)
        onesb = sb("onesb", [P, P], BF16)
        causal4 = sb("causal4", [P, 4, P], BF16)
        causal4_t = sb("causal4_t", [P, 4, P], BF16)
        mask_i = sb("mask_i", [P, SK], I32)
        maskb = sb("maskb", [P, SK], BF16)
        mask4 = sb("mask4", [P, 4, SK], BF16)
        mask4_t = sb("mask4_t", [SK, 4, P], BF16)
        seen = sb("seen", [P, SK])
        q_scale = sb("q_scale", [P, 1])
        q_bias0 = sb("q_bias0", [P, P])
        q_bias1 = sb("q_bias1", [P, P])
        sign_a = sb("sign_a", [P, P])
        sign_w = sb("sign_w", [P, P])

        idx_all = sb("idx_all", [P, NSEQ * 8], I32)
        w_all = sb("w_all", [P, NSEQ * 8])
        ones_e = sb("ones_e", [P, E])
        zeros = sb("zeros", [P, P])
        w_f = sb("w_f", [P, 2, 8])
        total = sb("total", [P, E])
        totalb = sb("totalb", [P, E], BF16)
        eps = sb("eps", [P, 1])

        first = ExitStack()

        def sa(name, shape, dt=F32):
            return first.enter_context(nc.sbuf_tensor(name, shape, dt))

        x_in = sa("x_in", [P, G, P])
        ctx_in = sa("ctx_in", [SK, G, P])
        x = sa("x", [P, G, P])
        xb = sa("xb", [P, G, P])
        stats = sa("stats", [P, G, 6])
        mv = sa("mv", [P, G, 2])
        lnv = sa("lnv", [P, G])
        rstd = sa("rstd", [P, G])
        ln = sa("ln", [P, G, P])
        ln_r = sa("ln_r", [P, G, P])
        ln_t = sa("ln_t", [P, G, P])
        ctx_t = sa("ctx_t", [P, G, SK])
        kpad_x = sa("kpad_x", [SK, G, H, PAD])
        kt_x = [sa(f"kt_x{i}", [P, G, 4, SK]) for i in range(2)]
        v_x = [sa(f"v_x{i}", [SK, G, H, DA]) for i in range(2)]
        qkv = sa("qkv", [P, G, 3 * P])
        rot = sa("rot", [P, 2, 2 * P])
        kpad = sa("kpad", [P, G, H, PAD])
        kt = sa("kt", [P, G, 4, P])
        v = sa("v", [P, G, H, DA])
        qpad = sa("qpad", [P, G, H, PAD])
        qt = sa("qt", [P, G, 4, P])
        pt = sa("pt", [P, 2, H, P])
        pt_flat = pt[:, :, :, :].rearrange("p a h c -> p (a h c)")
        ckv = pt_flat[0:SK, 0:G * 4 * P].rearrange("p (b a c) -> p b a c", b=G, a=4)
        phi = pt_flat.rearrange("p (b i c) -> p b i c", b=G, i=2)
        pq_t = qt[:, :, :, :].rearrange("p b g c -> p b (g c)")
        fqk_t = kt[:, :, :, :].rearrange("p b g c -> p (b g c)")[:, 0:G * 2 * P].rearrange("p (b c) -> p b c", b=G)
        rden = sa("rden", [P, G, H])
        o = sa("o", [P, G, P])
        o_t = sa("o_t", [P, G, P])
        sq = sa("sq", [P, G, 2 * P])
        norm2 = sa("norm2", [P, G, 2 * H])
        fmax = sa("fmax", [P, G, 2 * H])
        kvb = sa("kvb", [P, G, H * DA])

        sc = sa("sc", [P, G, E])
        sfc = sa("sfc", [P, G, E])
        top8 = sa("top8", [P, G, NG, 8])
        gsum = sa("gsum", [P, G, NG])
        more = sa("more", [P, G, NG, NG])
        least = sa("least", [P, G, NG, NG])
        glead = sa("glead", [P, G, NG])
        masked = sa("masked", [P, G, E])
        best = sa("best", [P, G, 8])
        taken = sa("taken", [P, G, E])
        chosen = sa("chosen", [P, G, E])
        chosenb = sa("chosenb", [P, G, E], BF16)
        gw = sa("gw", [P, G, E])
        wsum = sa("wsum", [P, G])
        slot = sa("slot", [P, G, E])
        slot8 = sa("slot8", [P, G, 8])
        pick = sq[:, 0:2, :].rearrange("p b c -> p (b c)").rearrange("p (j e) -> p j e", j=8)
        w8 = sa("w8", [P, G, 8])
        idx = sa("idx", [P, G, 8], I32)

        first.close()
        w_down = sb("w_down", [I, E * P])
        tok = sb("tok", [P, G, P])
        tok_t = sb("tok_t", [P, G, P])
        act_g = sb("act_g", [P, G, I])
        hid = sb("hid", [P, G, I])
        hid_t = sb("hid_t", [I, G, P])
        y = sb("y", [P, G, P])
        n_tiles = sb("n_tiles", [P, E])
        n_int = sb("n_int", [P, E], I32)
        upto = sb("upto", [P, E])
        past = sb("past", [P, E])
        which = sb("which", [P, TCOLS])
        skipped = sb("skipped", [P, TCOLS])
        rowf = sb("rowf", [P, 2 * TCOLS])
        rowi = sb("rowi", [P, 2 * TCOLS], I32)
        rows = sb("rows", [1, 2 * TCOLS * P], I32)
        tail_f = sb("tail_f", [P, E])
        tail_i = sb("tail_i", [P, E], I32)
        room = sb("room", [P, E])
        empty = sb("empty", [P, E])
        spare = sb("spare", [P, 1])
        idx_f = sb("idx_f", [P, 2, 8], I32)
        idx_old = sb("idx_old", [P, 2, 8])
        of_all = sb("of_all", [P, NSEQ * 8], I32)
        of = sb("of", [P, 2, 8])
        shift = sb("shift", [P, E])
        same = sb("same", [P, 2, TOPK, E])
        moved = sb("moved", [P, 2, TOPK])
        own = sb("own", [P, 2, P])
        res = sb("res", [P, 2, P])
        own_t = sb("own_t", [P, 2, P])
        s_act = sb("s_act", [P, 2, 2 * I])
        s_hid = sb("s_hid", [P, 2, 2 * I])
        s_hid_t = sb("s_hid_t", [I, 2, 2 * P])
        got = sb("got", [P, 2, TOPK, P])
        acc = sb("acc", [P, 2, P])

        ahead = {
            "dve": ["mv", "ln", "ckv", "qkv", "qpad", "max0", "max1", "o", "res", "norm2", "fsub", "kvb"],
            "act": ["ctx_t", "kt_x0", "kt_x1", "ln_t", "kt", "qt", "exp0", "exp1", "o_t", "fqkv", "fqk_t", "fexp",
                    "pq_t"],
            "pool": ["xb", "kv_x", "rope", "sq", "fphi"],
            "pe": ["pe_t", "ctx_mm", "kt_mm", "lnt_mm", "qkv_mm", "qt_mm", "s0", "s1", "st0", "st1", "pv", "ot_mm",
                   "proj", "fqkt_mm", "xw", "kv_mm", "pqt_mm", "num_mm"],
        }
        S = {n: sem(n) for part in ahead.values() for n in part}
        carried = sem("carried")
        cleared, down_in = sem("cleared"), sem("down_in")
        loads, setup, setup_pe, mask_t = sem("loads"), sem("setup"), sem("setup_pe"), sem("mask_t")
        x_loaded, c_loaded = sem("x_loaded"), sem("c_loaded")
        lnv_done, rstd_done = sem("lnv_done"), sem("rstd_done")
        gate_done, gate_exp = sem("gate_done"), sem("gate_exp")
        chosen_done, rank_done, slots_done = sem("chosen_done"), sem("rank_done"), sem("slots_done")
        res_out, ln_out, scattered = sem("res_out"), sem("ln_out"), sem("scattered")
        dve_step, pool_step = sem("dve_step"), sem("pool_step")
        counted, tables, table_out, table_in, tails = (sem("counted"), sem("tables"), sem("table_out"),
                                                       sem("table_in"), sem("tails"))
        tok_in, y_out = ([sem(f"{n}{u}") for u in range(G)] for n in ("tok_in", "y_out"))
        own_in, res_in, gathered, out_done = ([sem(f"{n}{u}") for u in range(2)]
                                              for n in ("own_in", "res_in", "gathered", "out_done"))
        xt_mm, xt_ev, gu_mm, g_act, h_done = ( sem("xt_mm"), sem("xt_ev"), sem("gu_mm"),
                                                      sem("g_act"), sem("h_done"))
        ht_mm, ht_ev, y_mm, y_ev, picks = sem("ht_mm"), sem("ht_ev"), sem("y_mm"), sem("y_ev"), sem("picks")
        pick_step = sem("pick_step")
        ct_mm, ct_ev, cg_mm, cg_act, ch_done = (sem("ct_mm"), sem("ct_ev"), sem("cg_mm"), sem("cg_act"),
                                                sem("ch_done"))
        cht_mm, cht_ev, cy_mm, acc_step, summed = (sem("cht_mm"), sem("cht_ev"), sem("cy_mm"),
                                                             sem("acc_step"), sem("summed"))

        def at(it, b=G - 1, k=0, K=1):
            return (it * K + k) * G + b + 1 + G

        def before(it, b, k=0, K=1):
            return (it * K + k) * G + b + 1

        def plain(eng):
            eng.sem_inc(carried, 1)

        block = ctx.enter_context(nc.Block())
        wide4 = wide[:, :, :, :, :].rearrange("p a j g c -> p (a j g c)").rearrange("p (u c) -> p u c", u=G)
        N_LOADS = 6

        @block.sync
        def _(sp):
            def load(turn):
                sp.dma_start(x_in[:, :, :], x_d[bass.ds(turn * G, G)].rearrange("s t f -> t s f")).then_inc(x_loaded, 16)
                sp.dma_start(ctx_in[:, :, :], ctx_d[bass.ds(turn * G, G)].rearrange("s t f -> t s f")
                             ).then_inc(c_loaded, 16)

            def store(it):
                sp.wait_ge(S["res"], at(it, G - 1, 4, 5))
                plain(sp)
                sp.dma_start(res_d[bass.ds(it * G, G)].rearrange("s t f -> t s f"), x[:, :, :]).then_inc(res_out, 16)
                sp.wait_ge(S["ln"], at(it, G - 1, 5, 6))
                plain(sp)
                sp.dma_start(ln_d[bass.ds(it * G, G)].rearrange("s t f -> t s f"), ln_r[:, :, :]).then_inc(ln_out, 16)

            sp.dma_start(consts[:, :], const_d).then_inc(loads, 16)
            load(0)
            sp.dma_start(mask_i[:, :], mask_d).then_inc(loads, 16)
            sp.dma_start(w[:, :], weight_d).then_inc(loads, 16)
            sp.dma_start(biases[:, :], bias_d).then_inc(loads, 16)
            sp.dma_start(w_gu[:, :], wgu_d).then_inc(loads, 16)
            sp.dma_start(s_down[:, :], sdown_d).then_inc(loads, 16)
            sp.wait_ge(setup_pe, 1)
            plain(sp)
            for e in range(E):
                sp.dma_start(xs_d[e * REGION + LAST:(e + 1) * REGION], zeros[:, :]).then_inc(cleared, 16)
            with sp.Fori(0, TURNS - 1) as it:
                sp.wait_ge(S["ln"], at(it, G - 1, 0, 6))
                plain(sp)
                sp.wait_ge(S["xb"], at(it, G - 1, 0, 4))
                plain(sp)
                sp.wait_ge(S["ctx_t"], at(it))
                plain(sp)
                load(it + 1)
                store(it)
            store(TURNS - 1)

            sp.wait_ge(tables, 1)
            plain(sp)
            sp.wait_ge(scattered, 16 * NSEQ * TOPK)
            plain(sp)
            sp.wait_ge(res_out, 16 * TURNS)
            plain(sp)
            sp.wait_ge(ln_out, 16 * TURNS)
            plain(sp)
            sp.dma_start(w_down[:, :], wdown_d).then_inc(down_in, 16)
            with sp.Fori(0, E) as e:
                row = sp.value_load(tail_i[0:1, bass.ds(e, 1)], min_val=0, max_val=ROWS - P)
                sp.dma_start(xs_d[bass.ds(row, P)], zeros[:, :]).then_inc(tails, 16)
            sp.wait_ge(tables, 2)
            plain(sp)
            sp.dma_start(tab_d.rearrange("(c p) -> p c", p=P), rowi[:, :], allow_slow_non_contiguous=True
                         ).then_inc(table_out, 16)
            sp.wait_ge(table_out, 16)
            plain(sp)
            sp.dma_start(rows[:, :], tab_d.rearrange("(a n) -> a n", a=1)).then_inc(table_in, 16)
            sp.wait_ge(table_in, 16)
            plain(sp)
            sp.wait_ge(tails, 16 * E)
            plain(sp)
            with sp.Fori(0, NT // G) as it:
                for u in range(G):
                    row = sp.value_load(rows[0:1, bass.ds(it * G + u, 1)], min_val=0, max_val=ROWS - P)
                    sp.wait_ge(xt_ev, it * G)
                    plain(sp)
                    sp.dma_start(tok[:, u, :], xs_d[bass.ds(row, P)]).then_inc(tok_in[u], 16)

            with sp.Fori(0, NSEQ // 2) as it:
                for u in range(2):
                    sp.wait_ge(ct_ev, it * 2)
                    plain(sp)
                    sp.wait_ge(summed, it * 2)
                    plain(sp)
                    sp.dma_start(own[:, u, :], ln_d[it * 2 + u]).then_inc(own_in[u], 16)
                    sp.dma_start(res[:, u, :], res_d[it * 2 + u]).then_inc(res_in[u], 16)
                for u in range(2):
                    sp.wait_ge(summed, it * 2 + u + 1)
                    plain(sp)
                    sp.dma_start(out_d[it * 2 + u], acc[:, u, :]).then_inc(out_done[u], 16)
            for u in range(2):
                sp.wait_ge(out_done[u], 16 * (NSEQ // 2))
            plain(sp)

        @block.tensor
        def _(pe):
            for n in ahead["pe"]:
                pe.sem_inc(S[n], G)
            pe.wait_ge(setup, 1)
            pe.transpose(bank[0:SK, 0, 0:P // 2].bitcast(BF16), maskb[:, :], identb[:, :]).then_inc(mask_t, 1)
            pe.wait_ge(setup, 2)

            def turn(out, in_, n_in, width):
                return pe.transpose(out, in_, ident[0:n_in, 0:n_in])

            with pe.Fori(0, TURNS) as it:
                def norm_t(k, reader, src=ln):
                    for b in range(G):
                        pe.wait_ge(S["ln"], at(it, b, k, 6))
                        pe.wait_ge(S[reader[0]], at(it, b, reader[1], reader[2]))
                        turn(bank[:, b, 0:P], src[:, b, :], P, P).then_inc(S["lnt_mm"], 1)

                def queries_t(k, ready, n_ready, free, n_free, b):
                    pe.wait_ge(S[ready], n_ready)
                    pe.wait_ge(S[free], n_free)
                    for g in range(4):
                        mm = turn(bank[:, b, g * P:(g + 1) * P], qpad[:, b, 4 * g:4 * g + 4, :].rearrange(
                            "p h c -> p (h c)"), P, P)
                    mm.then_inc(S["qt_mm"], 1)

                def scores(a, keys, sk, mask, mask_turned):
                    for b in range(G):
                        pe.wait_ge(S["qt"], at(it, b, 2 * a, 6))
                        for half in range(2):
                            if b:
                                pe.wait_ge(S[f"max{half}"], at(it, b - 1, a, 3))
                            else:
                                pe.wait_ge(S[f"exp{half}"], before(it, G - 1, a, 3))
                            if mask is not None:
                                for q in range(2):
                                    pe.matmul(wide[:, half, q, :, 0:sk], identb[:, :], mask, start=True,
                                              stop=False, skip_group_check=True)
                            for g in range(4):
                                for q in range(2):
                                    at_j = 32 * (2 * half + q)
                                    mm = pe.matmul(wide[:, half, q, g, 0:sk], qt[at_j:at_j + DH, b, g, :],
                                                   keys[at_j:at_j + DH, b, g, 0:sk], start=mask is None,
                                                   stop=True, skip_group_check=True)
                            mm.then_inc(S[f"s{half}"], 1)
                    for b in range(G):
                        pe.wait_ge(S["max0"], at(it, b, a, 3))
                        queries_t(2 * a + 1, "max1", at(it, b, a, 3), "qt", at(it, b, 2 * a, 6), b)

                def weights_and_values(a, keys, values, sk, mask_turned):
                    for b in range(G):
                        pe.wait_ge(S["qt"], at(it, b, 2 * a + 1, 6))
                        for half in range(2):
                            if b:
                                pe.wait_ge(S[f"exp{half}"], at(it, b - 1, a, 3))
                            else:
                                pe.wait_ge(S[f"max{half}"], at(it, G - 1, a, 3))
                            if mask_turned is not None:
                                for q in range(2):
                                    pe.matmul(wide[0:sk, half, q, :, :], identb[0:sk, 0:sk], mask_turned,
                                              start=True, stop=False, skip_group_check=True)
                            for g in range(4):
                                for q in range(2):
                                    at_j = 32 * (2 * half + q)
                                    mm = pe.matmul(wide[0:sk, half, q, g, :], keys[at_j:at_j + DH + 1, b, g, 0:sk],
                                                   qt[at_j:at_j + DH + 1, b, g, :], start=mask_turned is None,
                                                   stop=True, skip_group_check=True)
                            mm.then_inc(S[f"st{half}"], 1)
                        if b:
                            values_of(a, b - 1, values, sk)
                    values_of(a, G - 1, values, sk)

                def values_of(a, b, values, sk):
                    pe.wait_ge(S["exp0"], at(it, b, a, 3))
                    pe.wait_ge(S["exp1"], at(it, b, a, 3))
                    pe.wait_ge(S["qt"], at(it, b, 2 * a + 1, 6))
                    for h in range(H):
                        mm = pe.matmul(bank[:, b, h * DA:(h + 1) * DA], pt[0:sk, b % 2, 4 * (h % 4) + h // 4, :], values[:, b, h, :],
                                       start=True, stop=True)
                    mm.then_inc(S["pv"], 1)

                def project(k, weight):
                    for b in range(G):
                        pe.wait_ge(S["o"], at(it, b, k, 4))
                        turn(bank[:, b, 0:P], o[:, b, :], P, P).then_inc(S["ot_mm"], 1)
                    for b in range(G):
                        pe.wait_ge(S["o_t"], at(it, b, k, 4))
                        pe.matmul(bank[:, b, 0:P], o_t[:, b, :], weight, start=True, stop=True).then_inc(S["proj"], 1)

                for b in range(G):
                    pe.wait_ge(c_loaded, 16 * it + 16)
                    pe.wait_ge(slots_done, 2 * it)
                    turn(bank[:, b, 0:SK], ctx_in[:, b, :], SK, P).then_inc(S["pe_t"], 1)
                for b in range(G):
                    pe.wait_ge(S["ctx_t"], at(it, b))
                    pe.matmul(bank[0:SK, b, :], ctx_t[:, b, :], wt("ctx"), start=True, stop=True
                              ).then_inc(S["ctx_mm"], 1)
                for i in range(2):
                    for b in range(G):
                        pe.wait_ge(S["kv_x"], at(it, b, i, 2))
                        pe.wait_ge(S["kt_x0" if i else "ckv"], at(it, b))
                        for g in range(4):
                            mm = turn(bank[:, b, g * SK:(g + 1) * SK],
                                      kpad_x[:, b, 4 * g:4 * g + 4, :].rearrange("p h c -> p (h c)"), SK, P)
                        mm.then_inc(S["kt_mm"], 1)

                norm_t(0, ("kt_x1", 0, 1))
                for b in range(G):
                    pe.wait_ge(S["ln_t"], at(it, b, 0, 6))
                    pe.matmul(bank[:, b, 0:3 * P], ln_t[:, b, :], wt("qkv0"), start=True, stop=True
                              ).then_inc(S["qkv_mm"], 1)
                for b in range(G):
                    pe.wait_ge(S["rope"], at(it, b))
                    pe.wait_ge(S["qkv"], at(it, b))
                    for g in range(4):
                        mm = turn(bank[:, b, g * P:(g + 1) * P],
                                  kpad[:, b, 4 * g:4 * g + 4, :].rearrange("p h c -> p (h c)"), P, P)
                    mm.then_inc(S["kt_mm"], 1)
                for b in range(G):
                    queries_t(0, "rope", at(it, b), "kt", at(it, b), b)
                scores(0, kt, P, causal4[:, :, :], causal4_t[:, :, :])
                weights_and_values(0, kt, v, P, causal4_t[:, :, :])
                project(0, wt("o0"))

                norm_t(1, ("res", 0, 5))
                for b in range(G):
                    pe.wait_ge(S["ln_t"], at(it, b, 1, 6))
                    pe.matmul(bank[:, b, 0:P], ln_t[:, b, :], wt("q_x0"), start=True, stop=True
                              ).then_inc(S["qkv_mm"], 1)
                for b in range(G):
                    queries_t(2, "qpad", at(it, b, 0, 2), "qpad", at(it, b, 0, 2), b)
                scores(1, kt_x[0], SK, mask4[:, :, :], mask4_t[:, :, :])
                weights_and_values(1, kt_x[0], v_x[0], SK, mask4_t[:, :, :])
                project(1, wt("o_x0"))

                norm_t(2, ("res", 1, 5))
                for b in range(G):
                    pe.wait_ge(S["ln_t"], at(it, b, 2, 6))
                    pe.matmul(bank[:, b, 0:P], ln_t[:, b, :], sign_w[:, :], start=True, stop=True
                              ).then_inc(S["proj"], 1)

                norm_t(3, ("res", 2, 5))
                for b in range(G):
                    pe.wait_ge(S["ln_t"], at(it, b, 3, 6))
                    pe.matmul(bank[:, b, 0:3 * P], ln_t[:, b, :], wt("qkv_f"), start=True, stop=True
                              ).then_inc(S["qkv_mm"], 1)
                for b in range(G):
                    pe.wait_ge(S["fqkv"], at(it, b))
                    for i in range(2):
                        mm = turn(bank[:, b, i * P:(i + 1) * P], qkv[:, b, i * P:(i + 1) * P], P, P)
                    mm.then_inc(S["fqkt_mm"], 1)
                for i in range(2):
                    for b in range(G):
                        if i:
                            pe.wait_ge(S["fsub"], at(it, b, 0, 2))
                        else:
                            pe.wait_ge(S["fqk_t"], at(it, b))
                        pe.matmul(bank[:, b, :], fqk_t[:, b, i * P:(i + 1) * P], wt("proj_f"), start=True, stop=True
                                  ).then_inc(S["xw"], 1)
                for b in range(G):
                    pe.wait_ge(S["fphi"], at(it, b, 0, 2))
                    pe.wait_ge(S["fsub"], at(it, b, 1, 2))
                    for g in range(4):
                        mm = turn(bank[:, b, g * P:(g + 1) * P], phi[:, b, 0, g * P:(g + 1) * P], P, P)
                    mm.then_inc(S["pqt_mm"], 1)
                for b in range(G):
                    pe.wait_ge(S["fphi"], at(it, b, 1, 2))
                    pe.wait_ge(S["pq_t"], at(it, b))
                    for g in range(4):
                        mm = pe.matmul(bank[:, b, g * 4 * DA:(g + 1) * 4 * DA], phi[:, b, 1, g * P:(g + 1) * P],
                                       v[:, b, 4 * g:4 * g + 4, :].rearrange("p h c -> p (h c)"), start=True, stop=True)
                    mm.then_inc(S["kv_mm"], 1)
                for b in range(G):
                    pe.wait_ge(S["kvb"], at(it, b))
                    for g in range(4):
                        mm = pe.matmul(bank[:, b, g * 4 * DA:(g + 1) * 4 * DA], pq_t[:, b, g * P:(g + 1) * P],
                                       kvb[:, b, g * 4 * DA:(g + 1) * 4 * DA], start=True, stop=True)
                    mm.then_inc(S["num_mm"], 1)
                project(2, wt("o_f"))

                norm_t(4, ("res", 3, 5))
                for b in range(G):
                    pe.wait_ge(S["ln_t"], at(it, b, 4, 6))
                    pe.matmul(bank[:, b, 0:P], ln_t[:, b, :], wt("q_x1"), start=True, stop=True
                              ).then_inc(S["qkv_mm"], 1)
                for b in range(G):
                    queries_t(4, "qpad", at(it, b, 1, 2), "qpad", at(it, b, 1, 2), b)
                scores(2, kt_x[1], SK, None, None)
                weights_and_values(2, kt_x[1], v_x[1], SK, None)
                project(3, wt("o_x1"))

                norm_t(5, ("res", 4, 5), ln_r)
                for b in range(G):
                    pe.wait_ge(S["ln_t"], at(it, b, 5, 6))
                    mm = pe.matmul(bank[:, 0, b * E:(b + 1) * E], ln_t[:, b, :], wt("gate"), start=True, stop=True)
                mm.then_inc(gate_done, 1)
                pe.wait_ge(chosen_done, it + 1)
                pe.matmul(bank[:, 1, 0:G * E].rearrange("p (b e) -> p b e", b=G), onesb[:, :],
                          totalb[:, :].rearrange("p (a e) -> p a e", a=1).to_broadcast((P, G, E)), start=True, stop=False,
                          skip_group_check=True)
                for b in range(G):
                    mm = pe.matmul(bank[:, 1, b * E:(b + 1) * E], upperb[:, :], chosenb[:, b, :], start=False,
                                   stop=b == G - 1, skip_group_check=True)
                    for earlier in range(b):
                        mm = pe.matmul(bank[:, 1, b * E:(b + 1) * E], onesb[:, :], chosenb[:, earlier, :],
                                       start=False, stop=False, skip_group_check=True)
                mm.then_inc(rank_done, 1)

            pe.wait_ge(slots_done, 2 * TURNS)
            pe.matmul(bank[:, 0, 0:E], onesb[:, :], totalb[:, :], start=True, stop=True).then_inc(counted, 1)

            pe.wait_ge(table_in, 16)
            pe.wait_ge(down_in, 16)
            with pe.Fori(0, NT // G) as it:
                for u in range(G):
                    pe.wait_ge(tok_in[u], 16 * it + 16)
                    pe.wait_ge(ht_ev, it * G)
                    turn(bank[:, u, 0:P], tok[:, u, :], P, P).then_inc(xt_mm, 1)
                experts = [pe.value_load(rows[0:1, bass.ds(it * G + u + TCOLS * P, 1)], min_val=0, max_val=E - 1)
                           for u in range(G)]
                for u in range(G):
                    pe.wait_ge(xt_ev, it * G + u + 1)
                    pe.wait_ge(y_ev, it * G)
                    pe.matmul(wide4[:, u, 0:2 * I], tok_t[:, u, :], w_gu[:, bass.ds(experts[u] * (2 * I), 2 * I)],
                              start=True, stop=True).then_inc(gu_mm, 1)
                for u in range(G):
                    pe.wait_ge(h_done, it * G + u + 1)
                    turn(bank[0:I, u, P:2 * P], hid[:, u, :], P, P).then_inc(ht_mm, 1)
                for u in range(G):
                    pe.wait_ge(ht_ev, it * G + u + 1)
                    pe.matmul(wide4[:, u, 256:256 + P], hid_t[:, u, :], w_down[:, bass.ds(experts[u] * P, P)],
                              start=True, stop=True).then_inc(y_mm, 1)

            pe.wait_ge(y_ev, NT)
            pe.wait_ge(ht_ev, NT)
            with pe.Fori(0, NSEQ // 2) as it:
                for u in range(2):
                    pe.wait_ge(own_in[u], 16 * it + 16)
                    pe.wait_ge(cht_ev, it * 2)
                    turn(bank[:, u, 0:P], own[:, u, :], P, P).then_inc(ct_mm, 1)
                for u in range(2):
                    pe.wait_ge(ct_ev, it * 2 + u + 1)
                    pe.wait_ge(summed, it * 2)
                    pe.matmul(wide4[:, u, 0:4 * I], own_t[:, u, :], wt("shared_gu"), start=True, stop=True
                              ).then_inc(cg_mm, 1)
                for u in range(2):
                    pe.wait_ge(ch_done, it * 2 + u + 1)
                    for c in range(2):
                        mm = turn(bank[0:I, u, (1 + c) * P:(2 + c) * P], s_hid[:, u, c * I:(c + 1) * I], P, P)
                    mm.then_inc(cht_mm, 1)
                for u in range(2):
                    pe.wait_ge(cht_ev, it * 2 + u + 1)
                    for c in range(2):
                        mm = pe.matmul(wide4[:, 2 + u, 0:P], s_hid_t[:, u, c * P:(c + 1) * P], s_down[:, c * P:(c + 1) * P],
                                       start=c == 0, stop=c == 1)
                    mm.then_inc(cy_mm, 1)

        @block.scalar
        def _(act):
            for n in ahead["act"]:
                act.sem_inc(S[n], G)
            nc.scalar.preload_act_table_set("natural_log_exp_and_others")
            act.wait_ge(setup, 2)
            with act.Fori(0, TURNS) as it:
                def rstd_of(k):
                    act.wait_ge(S["mv"], at(it, G - 1, k, 6))
                    nc.scalar.activation(lnv[:, :], mv[:, :, 1], ACT.Ln, bias=eps[:, 0:1]).then_inc(lnv_done, 1)
                    act.wait_ge(lnv_done, it * 6 + k + 1)
                    nc.scalar.activation(rstd[:, :], lnv[:, :], ACT.Exp, scale=-0.5).then_inc(rstd_done, 1)

                def copies(made, n_made, name, out, in_):
                    for b in range(G):
                        act.wait_ge(S[made], n_made(b))
                        nc.scalar.copy(out(b), in_(b)).then_inc(S[name], 1)

                def norm_t(k):
                    copies("lnt_mm", lambda b: at(it, b, k, 6), "ln_t", lambda b: ln_t[:, b, :],
                           lambda b: bank[:, b, 0:P])

                def queries_t(k):
                    copies("qt_mm", lambda b: at(it, b, k, 6), "qt", lambda b: qt[:, b, :, :],
                           lambda b: bank[:, b, :].rearrange("p (g c) -> p g c", g=4))

                def exps(a, sk):
                    for b in range(G):
                        act.wait_ge(S["pv"], at(it, b, a, 3) - 2)
                        for half in range(2):
                            act.wait_ge(S[f"st{half}"], at(it, b, a, 3))
                            nc.scalar.activation(pt[0:sk, b % 2, 8 * half:8 * half + 8, :], wide[0:sk, half, :, :, :].rearrange("p j g c -> p (j g) c"),
                                                 ACT.Exp).then_inc(S[f"exp{half}"], 1)

                def heads_t(k):
                    copies("ot_mm", lambda b: at(it, b, k, 4), "o_t", lambda b: o_t[:, b, :], lambda b: bank[:, b, 0:P])

                copies("pe_t", lambda b: at(it, b), "ctx_t", lambda b: ctx_t[:, b, :], lambda b: bank[:, b, 0:SK])
                rstd_of(0)
                for i in range(2):
                    copies("kt_mm", lambda b: at(it, b, i, 3), f"kt_x{i}", lambda b: kt_x[i][:, b, :, :],
                           lambda b: bank[:, b, 0:4 * SK].rearrange("p (g c) -> p g c", g=4))
                norm_t(0)
                copies("kt_mm", lambda b: at(it, b, 2, 3), "kt", lambda b: kt[:, b, :, :],
                       lambda b: bank[:, b, :].rearrange("p (g c) -> p g c", g=4))
                queries_t(0)
                queries_t(1)
                exps(0, P)
                heads_t(0)
                rstd_of(1)
                norm_t(1)
                queries_t(2)
                queries_t(3)
                exps(1, SK)
                heads_t(1)
                rstd_of(2)
                norm_t(2)
                rstd_of(3)
                norm_t(3)
                for b in range(G):
                    act.wait_ge(S["qkv_mm"], at(it, b, 2, 4))
                    nc.scalar.mul(qkv[:, b, 0:2 * P], bank[:, b, 0:2 * P], SCALE)
                    nc.scalar.copy(v[:, b, :, 0:DH], bank[:, b, 2 * P:3 * P].rearrange("p (h c) -> p h c", h=H)
                                   ).then_inc(S["fqkv"], 1)
                copies("fqkt_mm", lambda b: at(it, b), "fqk_t", lambda b: fqk_t[:, b, :], lambda b: bank[:, b, 0:2 * P])
                for i in range(2):
                    for b in range(G):
                        act.wait_ge(S["fsub"], at(it, b, i, 2))
                        nc.scalar.activation(phi[:, b, i, :], phi[:, b, i, :], ACT.Exp).then_inc(S["fexp"], 1)
                copies("pqt_mm", lambda b: at(it, b), "pq_t", lambda b: pq_t[:, b, :], lambda b: bank[:, b, :])
                heads_t(2)
                rstd_of(4)
                norm_t(4)
                queries_t(4)
                queries_t(5)
                exps(2, SK)
                heads_t(3)
                rstd_of(5)
                norm_t(5)
                act.wait_ge(gate_done, it + 1)
                nc.scalar.activation(sc[:, :, :], bank[:, 0, 0:G * E].rearrange("p (b e) -> p b e", b=G), ACT.Exp,
                                     scale=-1.0).then_inc(gate_exp, 1)

            act.wait_ge(table_in, 16)
            with act.Fori(0, NT // G) as it:
                for u in range(G):
                    act.wait_ge(xt_mm, it * G + u + 1)
                    nc.scalar.copy(tok_t[:, u, :], bank[:, u, 0:P]).then_inc(xt_ev, 1)
                for u in range(G):
                    act.wait_ge(gu_mm, it * G + u + 1)
                    act.wait_ge(h_done, it * G)
                    nc.scalar.activation(act_g[:, u, :], wide4[:, u, 0:I], ACT.Silu).then_inc(g_act, 1)
                for u in range(G):
                    act.wait_ge(y_mm, it * G + u + 1)
                    act.wait_ge(y_out[u], 16 * it)
                    nc.scalar.copy(y[:, u, :], wide4[:, u, 256:256 + P]).then_inc(y_ev, 1)
                for u in range(G):
                    act.wait_ge(y_ev, it * G + u + 1)
                    act.dma_start(ys_d[it * G + u], y[:, u, :]).then_inc(y_out[u], 16)
            with act.Fori(0, NSEQ // 2) as it:
                for u in range(2):
                    act.wait_ge(ct_mm, it * 2 + u + 1)
                    nc.scalar.copy(own_t[:, u, :], bank[:, u, 0:P]).then_inc(ct_ev, 1)
                for u in range(2):
                    act.wait_ge(cg_mm, it * 2 + u + 1)
                    nc.scalar.activation(s_act[:, u, :], wide4[:, u, 0:2 * I], ACT.Silu).then_inc(cg_act, 1)
                for u in range(2):
                    act.wait_ge(cht_mm, it * 2 + u + 1)
                    nc.scalar.copy(s_hid_t[:, u, :], bank[0:I, u, P:3 * P]).then_inc(cht_ev, 1)

        @block.gpsimd
        def _(pool):
            for n in ahead["pool"]:
                pool.sem_inc(S[n], G)
            for t in [qpad, kpad, kpad_x]:
                nc.gpsimd.memset(t[:, :, :, :], 0.0)
            nc.gpsimd.memset(zeros[:, :], 0.0)
            nc.gpsimd.memset(onesb[:, :], 1.0)
            nc.gpsimd.memset(totalb[:, :], 0.0)
            nc.gpsimd.memset(total[:, :], 0.0)
            nc.gpsimd.memset(ones_e[:, :], 1.0)
            nc.gpsimd.memset(eps[:, :], LN_EPS).then_inc(pool_step, 1)
            pool.wait_ge(pool_step, 1)
            for t in [kpad, kpad_x]:
                nc.gpsimd.memset(t[:, :, :, DH:DH + 1], 1.0)
            for t in [v] + v_x:
                nc.gpsimd.memset(t[:, :, :, DH:DH + 1], 1.0)
            nc.gpsimd.memset(w_f[:, :, :], 0.0).then_inc(setup_pe, 1)
            pool.wait_ge(setup, 2)
            pool.wait_ge(loads, 16 * N_LOADS)
            pool.wait_ge(cleared, 16 * E)
            ROPE = 3
            with pool.Fori(0, TURNS) as it:
                def with_bias(k, name, src):
                    for b in range(G):
                        if k:
                            pool.wait_ge(S["res"], at(it, b, {1: 0, 2: 2, 3: 3}[k], 5))
                        else:
                            pool.wait_ge(x_loaded, 16 * it + 16)
                            pool.wait_ge(S["res"], before(it, b, 0, 5))
                        nc.gpsimd.tensor_tensor(xb[:, b, :], src[:, b, :], bias(name), ALU.add).then_inc(S["xb"], 1)

                with_bias(0, "o0", x_in)
                for i in range(2):
                    for b in range(G):
                        pool.wait_ge(S["ckv"], at(it, b))
                        if i:
                            pool.wait_ge(S["kt_mm"], at(it, b, 0, 3))
                        plain(pool)
                        nc.gpsimd.tensor_copy(kpad_x[:, b, :, 0:DH],
                                              ckv[:, b, 2 * i, :].rearrange("p (h c) -> p h c", h=H))
                        nc.gpsimd.tensor_copy(v_x[i][:, b, :, 0:DH],
                                              ckv[:, b, 2 * i + 1, :].rearrange("p (h c) -> p h c", h=H)
                                              ).then_inc(S["kv_x"], 1)
                for b in range(G):
                    n = (it * G + b) * ROPE + 1
                    pool.wait_ge(S["qkv"], at(it, b))
                    qk = qkv[:, b, 0:2 * P].rearrange("p (n c) -> p n c", c=2)
                    sin = const("rope_s").rearrange("p (n c) -> p n c", c=2)
                    crossed = rot[:, 1, :].rearrange("p (n c) -> p n c", c=2)
                    nc.gpsimd.tensor_tensor(rot[:, 0, :], qkv[:, b, 0:2 * P], const("rope_c"), ALU.mult)
                    nc.gpsimd.tensor_tensor(crossed[:, :, 0], qk[:, :, 1], sin[:, :, 0], ALU.mult)
                    nc.gpsimd.tensor_tensor(crossed[:, :, 1], qk[:, :, 0], sin[:, :, 1], ALU.mult
                                            ).then_inc(pool_step, 1)
                    nc.gpsimd.tensor_copy(v[:, b, :, 0:DH], qkv[:, b, 2 * P:3 * P].rearrange("p (h c) -> p h c", h=H))
                    pool.wait_ge(pool_step, n + 1)
                    nc.gpsimd.tensor_tensor(qpad[:, b, :, 0:DH], rot[:, 0, 0:P].rearrange("p (h c) -> p h c", h=H),
                                            rot[:, 1, 0:P].rearrange("p (h c) -> p h c", h=H), ALU.add
                                            ).then_inc(pool_step, 1)
                    nc.gpsimd.tensor_tensor(kpad[:, b, :, 0:DH], rot[:, 0, P:2 * P].rearrange("p (h c) -> p h c", h=H),
                                            rot[:, 1, P:2 * P].rearrange("p (h c) -> p h c", h=H), ALU.add
                                            ).then_inc(pool_step, 1)
                    pool.wait_ge(pool_step, n + ROPE)
                    plain(pool)
                    pool.sem_inc(S["rope"], 1)
                with_bias(1, "o_x0", x)
                with_bias(2, "o_f", x)
                for b in range(G):
                    pool.wait_ge(S["fqkv"], at(it, b))
                    nc.gpsimd.tensor_tensor(sq[:, b, :], qkv[:, b, 0:2 * P], qkv[:, b, 0:2 * P], ALU.mult
                                            ).then_inc(S["sq"], 1)
                for i in range(2):
                    for b in range(G):
                        pool.wait_ge(S["fexp"], at(it, b, i, 2))
                        plain(pool)
                        nc.gpsimd.tensor_scalar(phi[:, b, i, :], phi[:, b, i, :], FAV_EPS, None, ALU.add
                                                ).then_inc(S["fphi"], 1)
                with_bias(3, "o_x1", x)
                pool.wait_ge(slots_done, 2 * it + 2)
                pool.wait_ge(S["ln"], at(it, G - 1, 5, 6))
                plain(pool)
                for b in range(G):
                    for j in range(TOPK):
                        nc.gpsimd.indirect_dma_start(
                            out=xs_d, out_offset=bass.IndirectOffsetOnAxis(ap=idx[:, b, j:j + 1], axis=0),
                            in_=ln_r[:, b, :], in_offset=None).then_inc(scattered, 16)

            y_rows = ys_d.rearrange("t p f -> (t p) f")
            for u in range(G):
                pool.wait_ge(y_out[u], 16 * (NT // G))
            with pool.Fori(0, NSEQ // 2) as it:
                for u in range(2):
                    pool.wait_ge(picks, it * 2 + u + 1)
                    pool.wait_ge(summed, it * 2)
                    plain(pool)
                    for j in range(TOPK):
                        nc.gpsimd.indirect_dma_start(
                            out=got[:, u, j, :], out_offset=None, in_=y_rows,
                            in_offset=bass.IndirectOffsetOnAxis(ap=idx_f[:, u, j:j + 1], axis=0)).then_inc(gathered[u], 16)

        @block.vector
        def _(dve):
            for n in ahead["dve"]:
                dve.sem_inc(S[n], G)
            dve.wait_ge(loads, 16 * N_LOADS)
            dve.wait_ge(setup_pe, 1)
            nc.vector.tensor_copy(identb[:, :], ident)
            nc.vector.tensor_copy(upperb[:, :], const("upper"))
            for j in range(4):
                nc.vector.tensor_copy(causal4[:, j, :], const("causal"))
                nc.vector.tensor_copy(causal4_t[:, j, :], const("causal_t"))
            nc.vector.tensor_scalar(sign_a[:, :], wt("ffn"), 0.0, None, ALU.is_gt)
            nc.vector.tensor_scalar(sign_w[:, :], wt("ffn"), 0.0, None, ALU.is_lt)
            nc.vector.tensor_scalar(maskb[:, :], mask_i[:, :], 0, -1.0e9, ALU.is_equal, ALU.mult)
            nc.vector.tensor_scalar(seen[:, :], mask_i[:, :], 0, None, ALU.not_equal).then_inc(setup, 1)
            dve.wait_ge(setup, 1)
            nc.vector.tensor_tensor(sign_w[:, :], sign_a[:, :], sign_w[:, :], ALU.subtract)
            for j in range(4):
                nc.vector.tensor_copy(mask4[:, j, :], maskb[:, :])
            nc.vector.tensor_reduce(q_scale[:, :], seen[:, :], AX, ALU.max).then_inc(dve_step, 1)
            dve.wait_ge(dve_step, 1)
            nc.vector.tensor_scalar(q_scale[:, :], q_scale[:, :], SCALE, None, ALU.mult)
            nc.vector.tensor_scalar(q_bias1[:, :], bias("q_x1"), SCALE, None, ALU.mult).then_inc(dve_step, 1)
            dve.wait_ge(dve_step, 2)
            nc.vector.tensor_scalar(q_bias0[:, :], bias("q_x0"), q_scale[:, 0:1], None, ALU.mult)
            dve.wait_ge(mask_t, 1)
            for j in range(4):
                cp = nc.vector.tensor_copy(mask4_t[:, j, :], bank[0:SK, 0, 0:P // 2].bitcast(BF16))
            cp.then_inc(setup, 1)
            dve.wait_ge(setup, 2)
            FIRST, STEPS = 2, DVE_STEPS
            with dve.Fori(0, TURNS) as it:
                taken_steps = [0]

                def own_step(ins, alone=False):
                    taken_steps[0] += 1
                    ins.then_inc(dve_step, 1)
                    dve.wait_ge(dve_step, it * STEPS + FIRST + taken_steps[0])
                    if alone:
                        plain(dve)

                def norm(k, src, out):
                    for b in range(G):
                        if k:
                            dve.wait_ge(S["res"], at(it, b, k - 1, 5))
                        else:
                            dve.wait_ge(x_loaded, 16 * it + 16)
                        st = nc.vector.bn_stats(stats[:, b, :], src[:, b, :])
                        if b < G - 1:
                            st.then_inc(dve_step, 1)
                            taken_steps[0] += 1
                        else:
                            own_step(st, alone=True)
                    for b in range(G):
                        nc.vector.bn_aggr(mv[:, b, :], stats[:, b, :]).then_inc(S["mv"], 1)
                    dve.wait_ge(rstd_done, it * 6 + k + 1)
                    dve.wait_ge(S["mv"], at(it, G - 1, k, 6))
                    if k == 5:
                        dve.wait_ge(scattered, 16 * G * TOPK * it)
                        dve.wait_ge(ln_out, 16 * it)
                    for b in range(G):
                        nc.vector.tensor_scalar(out[:, b, :], src[:, b, :], mv[:, b, 0:1], rstd[:, b:b + 1],
                                                ALU.subtract, ALU.mult).then_inc(S["ln"], 1)

                def maxima(a, sk):
                    for b in range(G):
                        for half in range(2):
                            dve.wait_ge(S[f"s{half}"], at(it, b, a, 3))
                            ninth = qpad[:, b, :, DH].rearrange("p (g j) -> p j g", j=4)
                            nc.vector.tensor_reduce(ninth[:, 2 * half:2 * half + 2, :], wide[:, half, :, :, 0:sk], AX,
                                                    ALU.max, negate=True).then_inc(S[f"max{half}"], 1)

                def heads_out(made, n_made):
                    for b in range(G):
                        dve.wait_ge(S[made], n_made(b))
                        heads = bank[:, b, 0:H * DA].rearrange("p (h c) -> p h c", h=H)
                        if made == "num_mm":
                            own_step(nc.vector.tensor_scalar(rden[:, b, :], heads[:, :, DH], M * FAV_EPS, None, ALU.add))
                            own_step(nc.vector.reciprocal(rden[:, b, :], rden[:, b, :]))
                        else:
                            own_step(nc.vector.reciprocal(rden[:, b, :], heads[:, :, DH]))
                        nc.vector.tensor_tensor(o[:, b, :].rearrange("p (h c) -> p h c", h=H), heads[:, :, 0:DH],
                                                rden[:, b, :].rearrange("p (h a) -> p h a", a=1).to_broadcast((P, H, DH)),
                                                ALU.mult).then_inc(S["o"], 1)

                def residual(k, n_proj, n_xb):
                    for b in range(G):
                        dve.wait_ge(S["proj"], at(it, b, n_proj, 5))
                        if k == 0:
                            dve.wait_ge(res_out, 16 * it)
                        if n_xb is None:
                            base = x
                        else:
                            base = xb
                            dve.wait_ge(S["xb"], at(it, b, n_xb, 4))
                        nc.vector.tensor_tensor(x[:, b, :], base[:, b, :], bank[:, b, 0:P], ALU.add
                                                ).then_inc(S["res"], 1)

                def queries(k, a, scale, bias_tile):
                    for b in range(G):
                        dve.wait_ge(S["qkv_mm"], at(it, b, k, 4))
                        nc.vector.scalar_tensor_tensor(
                            qpad[:, b, :, 0:DH], bank[:, b, 0:P].rearrange("p (h c) -> p h c", h=H), scale,
                            bias_tile.rearrange("p (h c) -> p h c", h=H), ALU.mult, ALU.add).then_inc(S["qpad"], 1)

                norm(0, x_in, ln)
                for b in range(G):
                    dve.wait_ge(S["ctx_mm"], at(it, b))
                    nc.vector.tensor_tensor(ckv[:, b, :, :].rearrange("p a c -> p (a c)"), bank[0:SK, b, :],
                                            bias("ctx")[0:SK, :], ALU.add).then_inc(S["ckv"], 1)
                for b in range(G):
                    dve.wait_ge(S["qkv_mm"], at(it, b, 0, 4))
                    nc.vector.tensor_tensor(qkv[:, b, :], bank[:, b, 0:3 * P], bias("qkv0"), ALU.add
                                            ).then_inc(S["qkv"], 1)
                maxima(0, P)
                heads_out("pv", lambda b: at(it, b, 0, 3))
                residual(0, 0, 0)

                norm(1, x, ln)
                queries(1, 1, q_scale[:, 0:1], q_bias0[:, :])
                maxima(1, SK)
                heads_out("pv", lambda b: at(it, b, 1, 3))
                residual(1, 1, 1)

                norm(2, x, ln)
                residual(2, 2, None)

                norm(3, x, ln)
                for b in range(G):
                    dve.wait_ge(S["sq"], at(it, b))
                    nc.vector.tensor_reduce(norm2[:, b, :], sq[:, b, :].rearrange("p (h c) -> p h c", c=DH), AX, ALU.add
                                            ).then_inc(S["norm2"], 1)
                for i in range(2):
                    for b in range(G):
                        dve.wait_ge(S["xw"], at(it, b, i, 2))
                        feats = bank[:, b, :].rearrange("p (h m) -> p h m", h=H)
                        cut = fmax[:, b, i * H:(i + 1) * H]
                        own_step(nc.vector.tensor_reduce(cut, feats, AX, ALU.max))
                        dve.wait_ge(S["norm2"], at(it, b))
                        own_step(nc.vector.scalar_tensor_tensor(cut, norm2[:, b, i * H:(i + 1) * H], 0.5, cut, ALU.mult,
                                                                ALU.add))
                        nc.vector.tensor_tensor(phi[:, b, i, :].rearrange("p (h m) -> p h m", h=H), feats,
                                                cut.rearrange("p (h a) -> p h a", a=1).to_broadcast((P, H, M)),
                                                ALU.subtract).then_inc(S["fsub"], 1)
                for b in range(G):
                    dve.wait_ge(S["kv_mm"], at(it, b))
                    nc.vector.tensor_tensor(kvb[:, b, :], bank[:, b, 0:H * DA], const("blocks"), ALU.mult
                                            ).then_inc(S["kvb"], 1)
                heads_out("num_mm", lambda b: at(it, b))
                residual(3, 3, 2)

                norm(4, x, ln)
                queries(3, 2, SCALE, q_bias1[:, :])
                maxima(2, SK)
                heads_out("pv", lambda b: at(it, b, 2, 3))
                residual(4, 4, 3)

                norm(5, x, ln_r)
                dve.wait_ge(gate_exp, it + 1)
                own_step(nc.vector.tensor_scalar(sc[:, :, :], sc[:, :, :], 1.0, None, ALU.add))
                own_step(nc.vector.reciprocal(sc[:, :, :], sc[:, :, :]))
                for b in range(G):
                    ins = nc.vector.tensor_tensor(sfc[:, b, :], sc[:, b, :], bias("gate"), ALU.add)
                own_step(ins, alone=True)
                for b in range(G):
                    for g in range(NG):
                        ins = nc.vector.max(top8[:, b, g, :], sfc[:, b, g * 8:(g + 1) * 8])
                own_step(ins)
                own_step(nc.vector.tensor_tensor(gsum[:, :, :], top8[:, :, :, 0], top8[:, :, :, 1], ALU.add))
                for b in range(G):
                    mine = gsum[:, b, :].rearrange("p (g a) -> p g a", a=1).to_broadcast((P, NG, NG))
                    theirs = gsum[:, b, :].rearrange("p (a g) -> p a g", a=1).to_broadcast((P, NG, NG))
                    nc.vector.tensor_tensor(more[:, b, :, :], theirs, mine, ALU.is_gt)
                    ins = nc.vector.tensor_tensor(least[:, b, :, :], theirs, mine, ALU.is_ge)
                own_step(ins)
                for b in range(G):
                    ins = nc.vector.tensor_tensor(least[:, b, :, :].rearrange("p a g -> p (a g)"),
                                                  least[:, b, :, :].rearrange("p a g -> p (a g)"), const("before"),
                                                  ALU.mult)
                own_step(ins)
                flat = "p b a g -> p (b a g)"
                own_step(nc.vector.tensor_tensor(more[:, :, :, :].rearrange(flat), more[:, :, :, :].rearrange(flat),
                                                 least[:, :, :, :].rearrange(flat), ALU.max))
                own_step(nc.vector.tensor_reduce(glead[:, :, :], more[:, :, :, :], AX, ALU.add))
                own_step(nc.vector.tensor_scalar(glead[:, :, :], glead[:, :, :], TOPG - 0.5, None, ALU.is_lt))
                own_step(nc.vector.tensor_tensor(
                    masked[:, :, :].rearrange("p b (g c) -> p (b g) c", c=8),
                    sfc[:, :, :].rearrange("p b (g c) -> p (b g) c", c=8),
                    glead[:, :, :].rearrange("p b g -> p (b g)").rearrange("p (n a) -> p n a", a=1
                                                                           ).to_broadcast((P, G * NG, 8)), ALU.mult), alone=True)
                for b in range(G):
                    ins = nc.vector.max(best[:, b, :], masked[:, b, :])
                own_step(ins, alone=True)
                for b in range(G):
                    ins = nc.vector.match_replace(taken[:, b, :], best[:, b, :], masked[:, b, :], GONE)
                own_step(ins)
                nc.vector.tensor_scalar(chosenb[:, :, :], taken[:, :, :], GONE / 2, None, ALU.is_lt)
                own_step(nc.vector.tensor_scalar(chosen[:, :, :], taken[:, :, :], GONE / 2, None, ALU.is_lt))
                dve.sem_inc(chosen_done, 1)
                own_step(nc.vector.tensor_tensor(gw[:, :, :], chosen[:, :, :], sc[:, :, :], ALU.mult))
                own_step(nc.vector.tensor_reduce(wsum[:, :], gw[:, :, :], AX, ALU.add))
                own_step(nc.vector.tensor_scalar(wsum[:, :], wsum[:, :], 1e-20, None, ALU.add))
                own_step(nc.vector.reciprocal(wsum[:, :], wsum[:, :]))
                own_step(nc.vector.tensor_scalar(wsum[:, :], wsum[:, :], ROUTED, None, ALU.mult))
                own_step(nc.vector.tensor_tensor(gw[:, :, :], gw[:, :, :],
                                                 wsum[:, :].rearrange("p (b a) -> p b a", a=1).to_broadcast((P, G, E)),
                                                 ALU.mult))
                dve.wait_ge(rank_done, it + 1)
                for b in range(G):
                    ins = nc.vector.tensor_tensor(slot[:, b, :], bank[:, 1, b * E:(b + 1) * E], const("first_slot"),
                                                  ALU.add)
                own_step(ins)
                dve.sem_inc(slots_done, 1)
                own_step(nc.vector.tensor_tensor(slot[:, :, :], slot[:, :, :], chosen[:, :, :], ALU.mult), alone=True)
                for b in range(G):
                    ins = nc.vector.max(slot8[:, b, :], slot[:, b, :])
                own_step(ins)
                own_step(nc.vector.tensor_scalar(idx[:, :, :], slot8[:, :, :], -1.0, None, ALU.add))
                for b in range(G):
                    for j in range(TOPK):
                        ins = nc.vector.scalar_tensor_tensor(pick[:, j, :], slot[:, b, :], slot8[:, b, j:j + 1],
                                                             gw[:, b, :], ALU.is_equal, ALU.mult,
                                                             accum_out=w8[:, b, j:j + 1])
                    own_step(ins)
                for b in range(G):
                    own_step(nc.vector.tensor_tensor(total[:, :], total[:, :], chosen[:, b, :], ALU.add))
                nc.vector.tensor_copy(totalb[:, :], total[:, :])
                nc.vector.tensor_copy(idx_all[:, bass.ds(it * (G * 8), G * 8)], idx[:, :, :].rearrange("p b j -> p (b j)"))
                own_step(nc.vector.tensor_copy(w_all[:, bass.ds(it * (G * 8), G * 8)],
                                               w8[:, :, :].rearrange("p b j -> p (b j)")))
                dve.sem_inc(slots_done, 1)
            assert taken_steps[0] == STEPS, taken_steps

            done = TURNS * STEPS + FIRST
            def late(ins):
                nonlocal done
                done += 1
                ins.then_inc(dve_step, 1)
                dve.wait_ge(dve_step, done)

            dve.wait_ge(counted, 1)
            late(nc.vector.tensor_scalar(room[:, :], bank[:, 0, 0:E], float(LAST), None, ALU.is_le))
            late(nc.vector.tensor_tensor(empty[:, :], room[:, :], const("last_tile"), ALU.mult))
            late(nc.vector.tensor_reduce(spare[:, :], empty[:, :], AX, ALU.max))
            late(nc.vector.tensor_tensor(tail_f[:, :], bank[:, 0, 0:E], const("first_slot"), ALU.add))
            late(nc.vector.tensor_scalar(tail_f[:, :], tail_f[:, :], -1.0, spare[:, 0:1], ALU.add, ALU.subtract))
            late(nc.vector.tensor_tensor(tail_f[:, :], tail_f[:, :], room[:, :], ALU.mult))
            nc.vector.tensor_scalar(tail_i[:, :], tail_f[:, :], spare[:, 0:1], None, ALU.add).then_inc(tables, 1)
            late(nc.vector.tensor_scalar(n_int[:, :], bank[:, 0, 0:E], float(P - 1), None, ALU.add))
            late(nc.vector.tensor_scalar(n_int[:, :], n_int[:, :], 7, None, ALU.arith_shift_right))
            late(nc.vector.tensor_copy(n_tiles[:, :], n_int[:, :]))
            late(nc.vector.tensor_tensor_scan(upto[:, :], ones_e[:, :], n_tiles[:, :], 0.0, ALU.mult, ALU.add))
            for c in range(TCOLS):
                tile_no = const("tile_no")[:, c:c + 1]
                late(nc.vector.scalar_tensor_tensor(past[:, :], upto[:, :], tile_no, ones_e[:, :], ALU.is_le, ALU.mult,
                                                    accum_out=which[:, c:c + 1]))
                late(nc.vector.scalar_tensor_tensor(past[:, :], upto[:, :], tile_no, n_tiles[:, :], ALU.is_le, ALU.mult,
                                                    accum_out=skipped[:, c:c + 1]))
            late(nc.vector.tensor_tensor(skipped[:, :], const("tile_no"), skipped[:, :], ALU.subtract))
            late(nc.vector.tensor_scalar(skipped[:, :], skipped[:, :], float(P), None, ALU.mult))
            late(nc.vector.scalar_tensor_tensor(skipped[:, :], which[:, :], float(REGION), skipped[:, :], ALU.mult,
                                                ALU.add))
            late(nc.vector.tensor_scalar(skipped[:, :], skipped[:, :], spare[:, 0:1], None, ALU.subtract))
            late(nc.vector.scalar_tensor_tensor(skipped[:, :], which[:, :], E - 0.5, skipped[:, :], ALU.is_lt,
                                                ALU.mult))
            late(nc.vector.tensor_scalar(rowf[:, 0:TCOLS], skipped[:, :], spare[:, 0:1], None, ALU.add))
            late(nc.vector.tensor_scalar(rowf[:, TCOLS:], which[:, :], float(E - 1), None, ALU.min))
            nc.vector.tensor_copy(rowi[:, :], rowf[:, :]).then_inc(tables, 1)
            late(nc.vector.tensor_tensor(shift[:, :], upto[:, :], n_tiles[:, :], ALU.subtract))
            late(nc.vector.tensor_scalar(shift[:, :], shift[:, :], float(P), 1.0, ALU.mult, ALU.add))
            late(nc.vector.tensor_tensor(shift[:, :], shift[:, :], const("first_slot"), ALU.subtract))
            late(nc.vector.tensor_scalar(of_all[:, :], idx_all[:, :], 13, None, ALU.arith_shift_right))

            dve.wait_ge(table_in, 16)
            with dve.Fori(0, NT // G) as it:
                for u in range(G):
                    dve.wait_ge(g_act, it * G + u + 1)
                    dve.wait_ge(ht_mm, it * G)
                    nc.vector.tensor_tensor(hid[:, u, :], act_g[:, u, :], wide4[:, u, I:2 * I], ALU.mult
                                            ).then_inc(h_done, 1)
                for u in range(G):
                    dve.wait_ge(ht_mm, it * G + u + 1)
                    dve.wait_ge(y_mm, it * G)
                    nc.vector.tensor_copy(hid_t[:, u, :], bank[0:I, u, P:2 * P]).then_inc(ht_ev, 1)

            with dve.Fori(0, NSEQ // 2) as it:
                for u in range(2):
                    dve.wait_ge(gathered[u], 16 * TOPK * it)
                    in_turn = [0]

                    def pair_step(ins):
                        in_turn[0] += 1
                        ins.then_inc(pick_step, 1)
                        dve.wait_ge(pick_step, (it * 2 + u) * 4 + in_turn[0])

                    nc.vector.tensor_copy(w_f[:, u, :], w_all[:, bass.ds(it * 16 + u * 8, 8)])
                    nc.vector.tensor_copy(idx_old[:, u, :], idx_all[:, bass.ds(it * 16 + u * 8, 8)])
                    pair_step(nc.vector.tensor_copy(of[:, u, :], of_all[:, bass.ds(it * 16 + u * 8, 8)]))
                    mine = of[:, u, :].rearrange("p (j a) -> p j a", a=1).to_broadcast((P, TOPK, E))
                    every = const("expert").rearrange("p (a e) -> p a e", a=1).to_broadcast((P, TOPK, E))
                    pair_step(nc.vector.tensor_tensor(same[:, u, :, :], every, mine, ALU.is_equal))
                    pair_step(nc.vector.tensor_tensor(
                        same[:, u, :, :], same[:, u, :, :],
                        shift[:, :].rearrange("p (a e) -> p a e", a=1).to_broadcast((P, TOPK, E)), ALU.mult))
                    pair_step(nc.vector.tensor_reduce(moved[:, u, :], same[:, u, :, :], AX, ALU.add))
                    nc.vector.tensor_tensor(idx_f[:, u, :], moved[:, u, :], idx_old[:, u, :], ALU.add
                                            ).then_inc(picks, 1)
                for u in range(2):
                    dve.wait_ge(cg_act, it * 2 + u + 1)
                    nc.vector.tensor_tensor(s_hid[:, u, :], s_act[:, u, :], wide4[:, u, 2 * I:4 * I], ALU.mult
                                            ).then_inc(ch_done, 1)
                for u in range(2):
                    dve.wait_ge(cy_mm, it * 2 + u + 1)
                    dve.wait_ge(res_in[u], 16 * it + 16)
                    dve.wait_ge(out_done[u], 16 * it)
                    nc.vector.tensor_tensor(acc[:, u, :], res[:, u, :], wide4[:, 2 + u, 0:P], ALU.add
                                            ).then_inc(acc_step, 1)
                for u in range(2):
                    dve.wait_ge(gathered[u], 16 * TOPK * (it + 1))
                    for j in range(TOPK):
                        dve.wait_ge(acc_step, it * 2 * TOPK + 2 + (u * (TOPK - 1)) + j if j else
                                    it * 2 * TOPK + 2 + u * (TOPK - 1))
                        ins = nc.vector.scalar_tensor_tensor(acc[:, u, :], got[:, u, j, :], w_f[:, u, j:j + 1],
                                                             acc[:, u, :], ALU.mult, ALU.add)
                        ins.then_inc(acc_step if j < TOPK - 1 else summed, 1)


DVE_STEPS = 93



def shape_tables():
    at, n = columns(CONSTS)
    c = np.zeros((P, n), np.float32)

    def put(name, value):
        c[:, at[name][0]:at[name][1]] = value

    i = np.arange(P)
    put("ident", np.eye(P))
    put("causal", np.where(i[None, :] > i[:, None], -1e10, 0.0))
    put("causal_t", np.where(i[:, None] > i[None, :], -1e10, 0.0))
    put("upper", i[:, None] < i[None, :])
    theta = 1.0 / 10000.0 ** (2.0 * np.arange(DH // 2, dtype=np.float32) / DH)
    ang = (i[:, None].astype(np.float32) * theta[None, :].astype(np.float32)).astype(np.float32)
    cos = np.repeat(np.cos(ang)[:, None, :, None], 2, 3).reshape(P, 1, DH)
    sin = np.stack([-np.sin(ang), np.sin(ang)], -1).reshape(P, 1, DH)
    both = np.repeat(np.array([SCALE, 1.0]), H)[None, :, None]
    put("rope_c", (both * cos).reshape(P, -1))
    put("rope_s", (both * sin).reshape(P, -1))
    put("blocks", np.tile(np.repeat(i[:, None] // M == np.arange(4)[None, :], DA, 1), (1, 4)))
    put("first_slot", np.arange(E)[None, :] * REGION + 1)
    put("last_tile", np.arange(E)[None, :] * REGION + LAST)
    put("tile_no", i[:, None] + P * np.arange(TCOLS)[None, :])
    put("expert", np.arange(E)[None, :])
    g = np.arange(NG)
    put("before", (g[None, :] < g[:, None]).reshape(1, -1))
    return c


def kernel(**inputs):
    import concourse.bacc as bacc
    from concourse.bass_utils import run_bass_kernel_spmd

    a = {k: np.asarray(v) for k, v in inputs.items()}
    t = lambda name: a[name].T
    c0, c1, f = "L0_xattn_", "L1_xattn_", "L1_attn_"
    proj = np.zeros((H, DH, H, M), np.float32)
    proj[np.arange(H), :, np.arange(H), :] = a["L1_attn_proj"].transpose(0, 2, 1)
    shared_gu = np.concatenate([t("L1_ffn_Sg"), t("L1_ffn_Su")], 1)
    weight = np.concatenate([
        t("L0_attn_wq"), t("L0_attn_wk"), t("L0_attn_wv"), t("L0_attn_wp"), t(c0 + "Wq"),
        t(c0 + "Wk"), t(c0 + "Wv"), a[c1 + "Wk"], a[c1 + "Wv"], t(c0 + "Wo"), t("L0_ffn_weight"),
        t(f + "Wq"), t(f + "Wk"), t(f + "Wv"), proj.reshape(P, H * M), t(f + "Wo"), a[c1 + "Wq"], a[c1 + "Wo"],
        t("L1_ffn_gate_w"), shared_gu], 1)
    bias = np.concatenate([
        a["L0_attn_bq"], a["L0_attn_bk"], a["L0_attn_bv"], a["L0_attn_bp"], a[c0 + "bq"], a[c0 + "bk"], a[c0 + "bv"],
        a[c1 + "bk"], a[c1 + "bv"], a[c0 + "bo"], a[f + "bo"], a[c1 + "bq"], a[c1 + "bo"], a["L1_ffn_gate_bias"]])
    w_gu = np.stack([a["L1_ffn_Wg"], a["L1_ffn_Wu"]], 1).transpose(3, 0, 1, 2).reshape(P, E * 2 * I)
    arrays = {
        "x_d": a["x"], "ctx_d": a["ctx_1024"], "mask_d": a["mask_1x1xSxS2_ik0"].reshape(P, SK),
        "const_d": shape_tables(), "bias_d": np.broadcast_to(bias[None, :], (P, bias.size)), "weight_d": weight,
        "wgu_d": w_gu, "wdown_d": a["L1_ffn_Wd"].transpose(2, 0, 1).reshape(I, E * P),
        "sdown_d": a["L1_ffn_Sd"].T.reshape(2, I, P).transpose(1, 0, 2).reshape(I, 2 * P)}
    arrays = {k: np.ascontiguousarray(v) for k, v in arrays.items()}
    nc = bacc.Bacc("TRN2", target_bir_lowering=False, num_devices=1)
    args = [nc.dram_tensor(k, v.shape, mybir.dt.from_np(v.dtype), kind="ExternalInput").ap() for k, v in arrays.items()]
    args.append(nc.dram_tensor("out_d", (NSEQ, P, P), F32, kind="ExternalOutput").ap())
    for name, shape, dt in [("xs_d", (ROWS, P), F32), ("ys_d", (NT, P, P), F32), ("ln_d", (NSEQ, P, P), F32),
                            ("res_d", (NSEQ, P, P), F32), ("tab_d", (2 * TCOLS * P,), I32)]:
        args.append(nc.dram_tensor(name, shape, dt).ap())
    build(nc, *args)
    r = run_bass_kernel_spmd(nc, [arrays], core_ids=[0])
    return r.results[0]["out_d"]
```

```python
from contextlib import ExitStack

import concourse.bass as bass
import numpy as np
from concourse import mybir
from concourse.alu_op_type import AluOpType as ALU

ACT = mybir.ActivationFunctionType
F32 = mybir.dt.float32
F32R = mybir.dt.float32r
BF16 = mybir.dt.bfloat16
I32 = mybir.dt.int32
AX = mybir.AxisListType.X

P = 128
NSEQ = 64
SK = 120
H, DH = 16, 8
DA = DH + 1
PAD = 32
G = 4
B2 = 2
TURNS = NSEQ // G
M = 32
E, I, TOPK, NG, TOPG = 64, 88, 8, 8, 4
REGION = NSEQ * P
NT = NSEQ * P * TOPK // P + E
TCOLS = -(-NT // P)
TU = 8
ROWS = E * REGION
LAST = REGION - P
SCALE = DH ** -0.5
LN_EPS, FAV_EPS = 1e-5, 1e-6
ROUTED = 2.5
GONE = -3.0e38

CONSTS = [("ident", P), ("causal", P), ("causal_t", P), ("upper", P), ("rope_c", 2 * P), ("rope_s", 2 * P),
          ("blocks", H * DA), ("first_slot", E), ("last_tile", E), ("tile_no", TCOLS), ("expert", E), ("before", NG * NG)]
BIASES = [("qkv0", 3 * P), ("o0", P), ("q_x0", P), ("ctx", 4 * P), ("o_x0", P), ("o_f", P), ("q_x1", P), ("o_x1", P),
          ("gate", E)]
WEIGHTS = [("qkv0", 3 * P), ("o0", P), ("q_x0", P), ("ctx", 4 * P), ("o_x0", P), ("ffn", P), ("qkv_f", 3 * P),
           ("proj_f", H * M), ("o_f", P), ("q_x1", P), ("o_x1", P), ("gate", E), ("shared_gu", 4 * I)]


def columns(parts):
    at, n = {}, 0
    for name, w in parts:
        at[name] = (n, n + w)
        n += w
    return at, n


def build(nc, x_d, ctx_d, mask_d, const_d, bias_d, weight_d, wgu_d, wdown_d, sdown_d, out_d,
          xs_d, ys_d, ln_d, res_d, tab_d):
    const_at, n_const = columns(CONSTS)
    bias_at, n_bias = columns(BIASES)
    w_at, n_w = columns(WEIGHTS)
    with ExitStack() as ctx:
        def sb(name, shape, dt=F32):
            return ctx.enter_context(nc.sbuf_tensor(name, shape, dt))

        def sem(name):
            return ctx.enter_context(nc.semaphore(name))

        wide = ctx.enter_context(nc.psum_tensor("wide", [P, 2, 2, 4, P], F32))
        bank = ctx.enter_context(nc.psum_tensor("bank", [P, G, 512], F32))

        consts = sb("consts", [P, n_const])
        biases = sb("biases", [P, n_bias])
        w = sb("w", [P, n_w])
        w_gu = sb("w_gu", [P, E * 2 * I])
        s_down = sb("s_down", [I, 2 * P])

        def const(name):
            return consts[:, const_at[name][0]:const_at[name][1]]

        def bias(name):
            return biases[:, bias_at[name][0]:bias_at[name][1]]

        def wt(name):
            return w[:, w_at[name][0]:w_at[name][1]]

        ident = const("ident")
        identb = sb("identb", [P, P], BF16)
        upperb = sb("upperb", [P, P], BF16)
        onesb = sb("onesb", [P, P], BF16)
        causal4 = sb("causal4", [P, 4, P], BF16)
        causal4_t = sb("causal4_t", [P, 4, P], BF16)
        mask_i = sb("mask_i", [P, SK], I32)
        maskb = sb("maskb", [P, SK], BF16)
        mask4 = sb("mask4", [P, 4, SK], BF16)
        mask4_t = sb("mask4_t", [SK, 4, P], BF16)
        seen = sb("seen", [P, SK])
        q_scale = sb("q_scale", [P, 1])
        q_bias0 = sb("q_bias0", [P, P])
        q_bias1 = sb("q_bias1", [P, P])
        sign_a = sb("sign_a", [P, P])
        sign_w = sb("sign_w", [P, P])

        idx_all = sb("idx_all", [P, (NT // TU + 1) * 8], I32)
        w_all = sb("w_all", [P, NSEQ * 8])
        ones_e = sb("ones_e", [P, E])
        zeros = sb("zeros", [P, P])
        total = sb("total", [P, E])
        totalb = sb("totalb", [P, E], BF16)
        eps = sb("eps", [P, 1])

        first = ExitStack()

        def sa(name, shape, dt=F32):
            return first.enter_context(nc.sbuf_tensor(name, shape, dt))

        x_in = sa("x_in", [P, G, P])
        ctx_in = sa("ctx_in", [SK, G, P])
        x = sa("x", [P, G, P])
        xb = sa("xb", [P, G, P])
        stats = sa("stats", [P, G, 6])
        mv = sa("mv", [P, G, 2])
        lnv = sa("lnv", [P, G])
        rstd = sa("rstd", [P, G])
        ln = sa("ln", [P, G, P])
        ln_r = sa("ln_r", [P, G, P])
        ln_t = sa("ln_t", [P, G, P])
        ctx_t = sa("ctx_t", [P, G, SK])
        kt_x = [sa(f"kt_x{i}", [P, G, 4, SK], F32R) for i in range(2)]
        v_x = [sa(f"v_x{i}", [SK, G, H, DA]) for i in range(2)]
        qkv = sa("qkv", [P, G, 3 * P])
        rot = sa("rot", [P, 2, 2 * P])
        kpad = sa("kpad", [P, G, H, PAD])
        kt = sa("kt", [P, G, 4, P], F32R)
        v = sa("v", [P, G, H, DA])
        qpad = sa("qpad", [P, G, H, PAD])
        qt = sa("qt", [P, G, 4, P], F32R)
        pt = sa("pt", [P, 2, H, P])
        pt_flat = pt[:, :, :, :].rearrange("p a h c -> p (a h c)")
        phi = pt_flat.rearrange("p (b i c) -> p b i c", b=G, i=2)
        ckv = phi[0:SK, :, 0, :].rearrange("p b (a c) -> p b a c", a=4)
        pq_t = phi[:, :, 0, :]
        fqk_t = phi[:, :, 1, 0:2 * P]
        rden = sa("rden", [P, G, H])
        o = sa("o", [P, G, P])
        o_t = sa("o_t", [P, G, P])
        sq = sa("sq", [P, G, 2 * P])
        norm2 = sa("norm2", [P, G, 2 * H])
        fmax = sa("fmax", [P, G, 2 * H])
        kvb = sa("kvb", [P, G, H * DA])

        sc = sa("sc", [P, G, E])
        sfc = sa("sfc", [P, G, E])
        top8 = sa("top8", [P, G, NG, 8])
        gsum = sa("gsum", [P, G, NG])
        more = sa("more", [P, G, NG, NG])
        least = sa("least", [P, G, NG, NG])
        glead = sa("glead", [P, G, NG])
        masked = sa("masked", [P, G, E])
        best = sa("best", [P, G, 8])
        taken = sa("taken", [P, G, E])
        chosen = sa("chosen", [P, G, E])
        chosenb = sa("chosenb", [P, G, E], BF16)
        gw = sa("gw", [P, G, E])
        wsum = sa("wsum", [P, G])
        slot = sa("slot", [P, G, E])
        slot8 = sa("slot8", [P, G, 8])
        picks_of = [sq[:, 2 * st:2 * st + 2, :].rearrange("p b c -> p (b c)").rearrange("p (j e) -> p j e", j=8)
                    for st in range(2)]
        w8 = sa("w8", [P, G, 8])
        idx = sa("idx", [P, G, 8], I32)

        first.close()
        w_down = sb("w_down", [I, E * P])
        tok = sb("tok", [P, TU, P])
        tok_t = sb("tok_t", [P, 4, P])
        act_g = sb("act_g", [P, 4, I])
        hid = sb("hid", [P, 4, I])
        hid_t = sb("hid_t", [I, 4, P])
        y = sb("y", [P, TU, P])
        n_tiles = sb("n_tiles", [P, E])
        n_int = sb("n_int", [P, E], I32)
        upto = sb("upto", [P, E])
        past = sb("past", [P, E])
        which = sb("which", [P, TCOLS])
        skipped = sb("skipped", [P, TCOLS])
        rowf = sb("rowf", [P, 2 * TCOLS])
        rowi = sb("rowi", [P, 2 * TCOLS], I32)
        rows = sb("rows", [1, 2 * TCOLS * P], I32)
        tail_f = sb("tail_f", [P, E])
        tail_i = sb("tail_i", [P, E], I32)
        room = sb("room", [P, E])
        empty = sb("empty", [P, E])
        spare = sb("spare", [P, 1])
        of_all = sb("of_all", [P, (NT // TU + 1) * 8], I32)
        row_all = sb("row_all", [P, (NT // TU + 1) * 8], I32)
        of = sb("of", [P, 8])
        same = sb("same", [P, TOPK, E])
        moved = sb("moved", [P, TOPK])
        shift = sb("shift", [P, E])
        idx_f = sb("idx_f", [P, 2, 8], I32)
        own = sb("own", [P, 2, P])
        res = sb("res", [P, 2, P])
        own_t = sb("own_t", [P, 2, P])
        s_act = sb("s_act", [P, 2, 2 * I])
        s_hid = sb("s_hid", [P, 2, 2 * I])
        s_hid_t = sb("s_hid_t", [I, 2, 2 * P])
        got = sb("got", [P, 2, TOPK, P])
        acc = sb("acc", [P, 2, P])

        names = {
            "dve": "mv ln ckv qkv max o res norm2 fsub fphi kvb",
            "act": "ctx_t khi qhi kt ln_t qt exp o_t fqkv fqk_t fexp pq_t",
            "pool": "xb rope klo qlo sq",
            "pe": "ctx_mm0 ctx_mm kt_mm lnt_mm qkv_mm qt_mm sc_mm st_mm pv ot_mm proj fqkt_mm xw kv_mm pqt_mm num_mm",
        }
        S = [{n: sem(f"{n}_{st}") for part in names.values() for n in part.split()} for st in range(2)]

        def per_stream(name):
            return [sem(f"{name}_{st}") for st in range(2)]

        loads, setup, setup_pe, mask_t = sem("loads"), sem("setup"), sem("setup_pe"), sem("mask_t")
        cleared, down_in, carried = sem("cleared"), sem("down_in"), sem("carried")
        x_loaded, c_loaded, lnv_done, rstd_done = (per_stream(n) for n in ("x_loaded", "c_loaded", "lnv", "rstd"))
        route_mm, gate_exp, routed = (per_stream(n) for n in ("route_mm", "gate_exp", "routed"))
        res_out, ln_out, scattered = (per_stream(n) for n in ("res_out", "ln_out", "scattered"))
        dve_own, pool_own = per_stream("dve_own"), per_stream("pool_own")
        dve_step, pool_step = sem("dve_step"), sem("pool_step")
        counted, tables, table_in, tails = (sem(n) for n in ("counted", "tables", "table_in", "tails"))
        tok_in = [sem(f"tok_in{u}") for u in range(TU)]
        y_out = [sem(f"y_out{u}") for u in range(2)]
        FETCHES = 16 * (NT // TU)
        xt_mm, xt_ev, gu_mm, g_act, h_done = (sem(n) for n in ("xt_mm", "xt_ev", "gu_mm", "g_act", "h_done"))
        ht_mm, ht_ev, y_mm, y_ev, moving = (sem(n) for n in ("ht_mm", "ht_ev", "y_mm", "y_ev", "moving"))
        gathered = [sem(f"gathered{u}") for u in range(2)]
        acc_step, summed, picked = (sem(n) for n in ("acc_step", "summed", "picked"))

        def at(it, b=B2 - 1, k=0, K=1):
            return (it * K + k) * B2 + b + 1 + B2

        def before(it, b, k=0, K=1):
            return (it * K + k) * B2 + b + 1

        def half_at(it, a, b, half):
            return ((it * 3 + a) * B2 + b) * 2 + half + 1 + 2 * B2

        def half_made(it, a, b, half):
            return half_at(it, a, b, half) - B2

        def ahead(eng, part):
            for st in range(2):
                for n in names[part].split():
                    eng.sem_inc(S[st][n], 2 * B2 if n in ("max", "exp") else B2)

        def plain(eng):
            eng.sem_inc(carried, 1)

        def opening(it):
            return isinstance(it, int) and it == 0

        def weave(one, other):
            i = j = 0
            while i < one[1] or j < other[1]:
                if j >= other[1] or (i < one[1] and i * other[1] <= j * one[1]):
                    next(one[0])
                    i += 1
                else:
                    next(other[0])
                    j += 1

        def turns(eng, layer0, layer1):
            def turn(it):
                weave((layer0(0, it), BEATS0), (layer1(1, it - 1), BEATS1))
                weave((layer1(0, it), BEATS1), (layer0(1, it), BEATS0))

            weave((layer0(0, 0), BEATS0), (iter(()), 0))
            weave((layer1(0, 0), BEATS1), (layer0(1, 0), BEATS0))
            turn(1)
            with eng.Fori(2, TURNS) as it:
                turn(it)
            weave((layer1(1, TURNS - 1), BEATS1), (iter(()), 0))

        block = ctx.enter_context(nc.Block())
        bank8 = [wide[:, i // 2, i % 2, :, :].rearrange("p g c -> p (g c)") for i in range(4)] + \
                [bank[:, i, :] for i in range(4)]
        N_LOADS = 6

        @block.sync
        def _(sp):
            def load(st, turn):
                src = bass.ds(turn * G + st * B2, B2)
                dst = slice(st * B2, st * B2 + B2)
                sp.dma_start(x_in[:, dst, :], x_d[src].rearrange("s t f -> t s f")).then_inc(x_loaded[st], 16)
                sp.dma_start(ctx_in[:, dst, :], ctx_d[src].rearrange("s t f -> t s f")).then_inc(c_loaded[st], 16)

            def load_next(st, it):
                sp.wait_ge(S[st]["ln"], at(it, B2 - 1, 0, 6))
                plain(sp)
                sp.wait_ge(S[st]["xb"], at(it, B2 - 1, 0, 4))
                plain(sp)
                sp.wait_ge(S[st]["ctx_t"], at(it))
                plain(sp)
                load(st, it + 1)

            def store(st, it):
                dst = bass.ds(it * G + st * B2, B2)
                src = slice(st * B2, st * B2 + B2)
                sp.wait_ge(S[st]["res"], at(it, B2 - 1, 4, 5))
                plain(sp)
                sp.dma_start(res_d[dst].rearrange("s t f -> t s f"), x[:, src, :]).then_inc(res_out[st], 16)
                sp.wait_ge(S[st]["ln"], at(it, B2 - 1, 5, 6))
                plain(sp)
                sp.dma_start(ln_d[dst].rearrange("s t f -> t s f"), ln_r[:, src, :]).then_inc(ln_out[st], 16)

            sp.dma_start(consts[:, :], const_d).then_inc(loads, 16)
            load(0, 0)
            sp.dma_start(mask_i[:, :], mask_d).then_inc(loads, 16)
            sp.dma_start(w[:, :], weight_d).then_inc(loads, 16)
            sp.dma_start(biases[:, :], bias_d).then_inc(loads, 16)
            load(1, 0)
            sp.dma_start(s_down[:, :], sdown_d).then_inc(loads, 16)
            sp.dma_start(w_gu[:, :], wgu_d).then_inc(loads, 16)
            sp.wait_ge(setup_pe, 1)
            for e in range(E):
                sp.dma_start(xs_d[e * REGION + LAST:(e + 1) * REGION], zeros[:, :]).then_inc(cleared, 16)
            load_next(0, 0)
            load_next(1, 0)
            store(0, 0)
            with sp.Fori(1, TURNS - 1) as it:
                load_next(0, it)
                store(1, it - 1)
                load_next(1, it)
                store(0, it)
            store(1, TURNS - 2)
            store(0, TURNS - 1)
            store(1, TURNS - 1)

            sp.wait_ge(tables, 1)
            for st in range(2):
                sp.wait_ge(scattered[st], 16 * B2 * TOPK * TURNS)
                sp.wait_ge(res_out[st], 16 * TURNS)
                sp.wait_ge(ln_out[st], 16 * TURNS)
            sp.dma_start(w_down[:, :], wdown_d).then_inc(down_in, 16)
            with sp.Fori(0, E) as e:
                row = sp.value_load(tail_i[0:1, bass.ds(e, 1)], min_val=0, max_val=ROWS - P)
                sp.dma_start(xs_d[bass.ds(row, P)], zeros[:, :]).then_inc(tails, 16)
            sp.wait_ge(tables, 2)
            sp.dma_start(tab_d.rearrange("(c p) -> p c", p=P), rowi[:, :], allow_slow_non_contiguous=True
                         ).then_inc(table_in, 16)
            sp.wait_ge(table_in, 16)
            sp.dma_start(rows[:, :], tab_d.rearrange("(a n) -> a n", a=1)).then_inc(table_in, 16)
            sp.wait_ge(table_in, 32)
            sp.wait_ge(tails, 16 * E)

            def fetch(it):
                for u in range(TU):
                    row = sp.value_load(rows[0:1, bass.ds(it * TU + u, 1)], min_val=0, max_val=ROWS - P)
                    if not opening(it):
                        sp.wait_ge(xt_mm, it * TU + u + 1 - TU)
                        plain(sp)
                    sp.dma_start(tok[:, u, :], xs_d[bass.ds(row, P)]).then_inc(tok_in[u], 16)

            fetch(0)
            with sp.Fori(1, NT // TU) as it:
                fetch(it)

            def rows_in(it, u):
                if not opening(it):
                    sp.wait_ge(xt_ev, NT + it * 2 + u - 1)
                    plain(sp)
                    sp.wait_ge(acc_step, ((it - 1) * 2 + u) * TOPK + 1)
                    plain(sp)
                sp.dma_start(own[:, u, :], ln_d[it * 2 + u]).then_inc(tok_in[u], 16)
                sp.dma_start(res[:, u, :], res_d[it * 2 + u]).then_inc(tok_in[2 + u], 16)

            def rows_out(it, u):
                sp.wait_ge(summed, it * 2 + u + 1)
                plain(sp)
                sp.dma_start(out_d[it * 2 + u], acc[:, u, :]).then_inc(tok_in[4 + u], 16)

            sp.wait_ge(xt_mm, NT)
            rows_in(0, 0)
            rows_in(0, 1)
            with sp.Fori(1, NSEQ // 2) as it:
                for u in range(2):
                    rows_in(it, u)
                    rows_out(it - 1, u)
            for u in range(2):
                rows_out(NSEQ // 2 - 1, u)
            for u in range(2):
                sp.wait_ge(tok_in[4 + u], FETCHES + 16 * (NSEQ // 2))

        @block.tensor
        def _(pe):
            ahead(pe, "pe")
            pe.wait_ge(setup, 1)
            pe.transpose(bank[0:SK, 0, 0:P // 2].bitcast(BF16), maskb[:, :], identb[:, :]).then_inc(mask_t, 1)
            pe.wait_ge(setup, 2)

            def turn(out, in_, n_in):
                return pe.transpose(out, in_, ident[0:n_in, 0:n_in])

            def norm_t(st, it, k, freed, src=ln):
                for b in range(B2):
                    q = st * B2 + b
                    pe.wait_ge(S[st]["ln"], at(it, b, k, 6))
                    pe.wait_ge(S[st][freed[0]], at(it, b, freed[1], freed[2]))
                    turn(bank[:, q, 0:P], src[:, q, :], P).then_inc(S[st]["lnt_mm"], 1)

            def through(st, it, k, weight, width, name):
                for b in range(B2):
                    q = st * B2 + b
                    pe.wait_ge(S[st]["ln_t"], at(it, b, k, 6))
                    pe.matmul(bank[:, q, 0:width], ln_t[:, q, :], weight, start=True, stop=True).then_inc(S[st][name], 1)

            def keys_t(st, it, k, sk, freed, n_freed):
                for b in range(B2):
                    q = st * B2 + b
                    pe.wait_ge(S[st]["klo"], at(it, b, k, 3))
                    pe.wait_ge(S[st][freed], n_freed(b))
                    for g in range(4):
                        mm = turn(bank[:, q, g * sk:(g + 1) * sk],
                                  kpad[0:sk, q, 4 * g:4 * g + 4, :].rearrange("p h c -> p (h c)"), sk)
                    mm.then_inc(S[st]["kt_mm"], 1)

            def queries_t(st, it, ready, n_ready, free, n_free):
                for b in range(B2):
                    q = st * B2 + b
                    pe.wait_ge(S[st][ready], n_ready(b))
                    pe.wait_ge(S[st][free], n_free(b))
                    for g in range(4):
                        mm = turn(bank[:, q, g * P:(g + 1) * P],
                                  qpad[:, q, 4 * g:4 * g + 4, :].rearrange("p h c -> p (h c)"), P)
                    mm.then_inc(S[st]["qt_mm"], 1)

            def attention(st, it, a, keys, values, sk, mask, mask_turned):
                sems = S[st]
                for b in range(B2):
                    q = st * B2 + b
                    for half in range(2):
                        if not half:
                            pe.wait_ge(sems["qt"], at(it, b, 2 * a, 6))
                        if b or half:
                            pe.wait_ge(sems["max"], half_at(it, a, b, half) - 1)
                        else:
                            pe.wait_ge(sems["exp"], half_at(it, a, 0, 0) - 1)
                        for c in range(2):
                            if mask is not None:
                                pe.matmul(wide[:, st, c, :, 0:sk], identb[:, :], mask, start=True, stop=False,
                                          skip_group_check=True)
                        for g in range(4):
                            for c in range(2):
                                j = 32 * (2 * half + c)
                                mm = pe.matmul(wide[:, st, c, g, 0:sk], qt[j:j + 3 * DH, q, g, :],
                                               keys[j:j + 3 * DH, q, g, 0:sk], start=mask is None, stop=True,
                                               skip_group_check=True)
                        mm.then_inc(sems["sc_mm"], 1)
                        yield
                queries_t(st, it, "max", lambda b: half_at(it, a, b, 1), "qt", lambda b: at(it, b, 2 * a, 6))
                yield
                for b in range(B2):
                    q = st * B2 + b
                    for half in range(2):
                        if not half:
                            pe.wait_ge(sems["qt"], at(it, b, 2 * a + 1, 6))
                        if b or half:
                            pe.wait_ge(sems["exp"], half_at(it, a, b, half) - 1)
                        else:
                            pe.wait_ge(sems["max"], half_at(it, a, 1, 1))
                        for c in range(2):
                            if mask_turned is not None:
                                pe.matmul(wide[0:sk, st, c, :, :], identb[0:sk, 0:sk], mask_turned, start=True,
                                          stop=False, skip_group_check=True)
                        for g in range(4):
                            for c in range(2):
                                j = 32 * (2 * half + c)
                                mm = pe.matmul(wide[0:sk, st, c, g, :], keys[j:j + 3 * DH + 1, q, g, 0:sk],
                                               qt[j:j + 3 * DH + 1, q, g, :], start=mask_turned is None, stop=True,
                                               skip_group_check=True)
                        mm.then_inc(sems["st_mm"], 1)
                        yield
                    pe.wait_ge(sems["exp"], half_at(it, a, b, 1))
                    for h in range(H):
                        mm = pe.matmul(bank[:, q, h * DA:(h + 1) * DA], pt[0:sk, st, 4 * (h % 4) + h // 4, :],
                                       values[:, q, h, :], start=True, stop=True)
                    mm.then_inc(sems["pv"], 1)
                    yield

            def project(st, it, k, weight):
                for b in range(B2):
                    q = st * B2 + b
                    pe.wait_ge(S[st]["o"], at(it, b, k, 4))
                    turn(bank[:, q, 0:P], o[:, q, :], P).then_inc(S[st]["ot_mm"], 1)
                yield
                for b in range(B2):
                    q = st * B2 + b
                    pe.wait_ge(S[st]["o_t"], at(it, b, k, 4))
                    pe.matmul(bank[:, q, 0:P], o_t[:, q, :], weight, start=True, stop=True).then_inc(S[st]["proj"], 1)
                yield

            def layer0(st, it):
                sems = S[st]
                if not opening(it):
                    pe.wait_ge(routed[st], 3 * it - 1)
                for b in range(B2):
                    q = st * B2 + b
                    pe.wait_ge(c_loaded[st], 16 * it + 16)
                    turn(bank[:, q, 0:SK], ctx_in[:, q, :], SK).then_inc(sems["ctx_mm0"], 1)
                yield
                for b in range(B2):
                    q = st * B2 + b
                    pe.wait_ge(sems["ctx_t"], at(it, b))
                    pe.matmul(bank[0:SK, q, :], ctx_t[:, q, :], wt("ctx"), start=True, stop=True
                              ).then_inc(sems["ctx_mm"], 1)
                yield
                yield
                norm_t(st, it, 0, ("ckv", 0, 1))
                yield
                through(st, it, 0, wt("qkv0"), 3 * P, "qkv_mm")
                yield
                keys_t(st, it, 0, SK, "qkv", lambda b: at(it, b, 0, 3))
                yield
                yield
                keys_t(st, it, 1, SK, "kt", lambda b: at(it, b, 0, 3))
                yield
                yield
                keys_t(st, it, 2, P, "kt", lambda b: at(it, b, 1, 3))
                yield
                queries_t(st, it, "qlo", lambda b: at(it, b, 0, 3), "kt", lambda b: at(it, b, 2, 3))
                yield
                yield from attention(st, it, 0, kt, v, P, causal4[:, :, :], causal4_t[:, :, :])
                yield from project(st, it, 0, wt("o0"))
                yield
                yield
                norm_t(st, it, 1, ("res", 0, 5))
                yield
                through(st, it, 1, wt("q_x0"), P, "qkv_mm")
                yield
                yield
                queries_t(st, it, "qlo", lambda b: at(it, b, 1, 3), "qkv", lambda b: at(it, b, 1, 3))
                yield
                yield from attention(st, it, 1, kt_x[0], v_x[0], SK, mask4[:, :, :], mask4_t[:, :, :])
                yield from project(st, it, 1, wt("o_x0"))
                yield
                yield
                norm_t(st, it, 2, ("res", 1, 5))
                yield
                through(st, it, 2, sign_w[:, :], P, "proj")
                yield

            def layer1(st, it):
                sems = S[st]
                yield
                yield
                norm_t(st, it, 3, ("res", 2, 5))
                yield
                through(st, it, 3, wt("qkv_f"), 3 * P, "qkv_mm")
                yield
                for b in range(B2):
                    q = st * B2 + b
                    pe.wait_ge(sems["fqkv"], at(it, b))
                    for i in range(2):
                        mm = turn(bank[:, q, i * P:(i + 1) * P], qkv[:, q, i * P:(i + 1) * P], P)
                    mm.then_inc(sems["fqkt_mm"], 1)
                yield
                for i in range(2):
                    for b in range(B2):
                        q = st * B2 + b
                        if i:
                            pe.wait_ge(sems["fsub"], at(it, b, 0, 2))
                        else:
                            pe.wait_ge(sems["fqk_t"], at(it, b))
                        pe.matmul(bank[:, q, :], fqk_t[:, q, i * P:(i + 1) * P], wt("proj_f"), start=True, stop=True
                                  ).then_inc(sems["xw"], 1)
                    yield
                yield
                for b in range(B2):
                    q = st * B2 + b
                    pe.wait_ge(sems["fphi"], at(it, b, 0, 2))
                    pe.wait_ge(sems["fsub"], at(it, b, 1, 2))
                    for g in range(4):
                        mm = turn(bank[:, q, g * P:(g + 1) * P], phi[:, q, 0, g * P:(g + 1) * P], P)
                    mm.then_inc(sems["pqt_mm"], 1)
                yield
                for b in range(B2):
                    q = st * B2 + b
                    pe.wait_ge(sems["fphi"], at(it, b, 1, 2))
                    pe.wait_ge(sems["pq_t"], at(it, b))
                    for g in range(4):
                        mm = pe.matmul(bank[:, q, g * 4 * DA:(g + 1) * 4 * DA], phi[:, q, 1, g * P:(g + 1) * P],
                                       v[:, q, 4 * g:4 * g + 4, :].rearrange("p h c -> p (h c)"), start=True, stop=True)
                    mm.then_inc(sems["kv_mm"], 1)
                yield
                for b in range(B2):
                    q = st * B2 + b
                    pe.wait_ge(sems["kvb"], at(it, b))
                    for g in range(4):
                        mm = pe.matmul(bank[:, q, g * 4 * DA:(g + 1) * 4 * DA], pq_t[:, q, g * P:(g + 1) * P],
                                       kvb[:, q, g * 4 * DA:(g + 1) * 4 * DA], start=True, stop=True)
                    mm.then_inc(sems["num_mm"], 1)
                yield
                yield from project(st, it, 2, wt("o_f"))
                yield
                yield
                norm_t(st, it, 4, ("res", 3, 5))
                yield
                through(st, it, 4, wt("q_x1"), P, "qkv_mm")
                yield
                yield
                queries_t(st, it, "qlo", lambda b: at(it, b, 2, 3), "qkv", lambda b: at(it, b, 2, 3))
                yield
                yield from attention(st, it, 2, kt_x[1], v_x[1], SK, None, None)
                yield from project(st, it, 3, wt("o_x1"))
                yield
                yield
                norm_t(st, it, 5, ("res", 4, 5), ln_r)
                yield
                for b in range(B2):
                    pe.wait_ge(sems["ln_t"], at(it, b, 5, 6))
                    mm = pe.matmul(bank[:, st * B2, b * E:(b + 1) * E], ln_t[:, st * B2 + b, :], wt("gate"), start=True,
                                   stop=True)
                mm.then_inc(route_mm[st], 1)
                yield
                yield
                yield
                pe.wait_ge(routed[st], 3 * it + 1)
                ranks = bank[:, st * B2 + 1, 0:B2 * E]
                pe.matmul(ranks.rearrange("p (b e) -> p b e", b=B2), onesb[:, :],
                          totalb[:, :].rearrange("p (a e) -> p a e", a=1).to_broadcast((P, B2, E)), start=True,
                          stop=False, skip_group_check=True)
                for b in range(B2):
                    pe.matmul(ranks[:, b * E:(b + 1) * E], upperb[:, :], chosenb[:, st * B2 + b, :], start=False,
                              stop=False, skip_group_check=True)
                pe.matmul(ranks[:, E:2 * E], onesb[:, :], chosenb[:, st * B2, :], start=False, stop=True,
                          skip_group_check=True).then_inc(route_mm[st], 1)
                yield
                yield

            turns(pe, layer0, layer1)

            for st in range(2):
                pe.wait_ge(routed[st], 3 * TURNS)
            pe.matmul(bank[:, 0, 0:E], onesb[:, :], totalb[:, :], start=True, stop=True).then_inc(counted, 1)
            pe.wait_ge(table_in, 32)
            pe.wait_ge(down_in, 16)

            def expert_of(it, u, lag):
                return pe.value_load(rows[0:1, bass.ds(it * TU + u - lag + TCOLS * P, 1)], min_val=0, max_val=E - 1)

            def experts_turn(it, first, last):
                for u in range(TU):
                    t = it * TU + u
                    if not last:
                        pe.wait_ge(tok_in[u], 16 * it + 16)
                        if not (first and u < 2):
                            pe.wait_ge(xt_ev, t - 1)
                        turn(bank8[u % 2][:, 0:P], tok[:, u, :], P).then_inc(xt_mm, 1)
                    if not (first and u < 2) and not (last and u >= 2):
                        e = expert_of(it, u, 2)
                        pe.wait_ge(xt_ev, t - 1)
                        if not (first and u < 4):
                            pe.wait_ge(h_done, t - 3)
                        pe.matmul(bank8[2 + u % 2][:, 0:2 * I], tok_t[:, (u - 2) % 4, :],
                                  w_gu[:, bass.ds(e * (2 * I), 2 * I)], start=True, stop=True).then_inc(gu_mm, 1)
                    if not (first and u < 4) and not (last and u >= 4):
                        pe.wait_ge(h_done, t - 3)
                        if not (first and u < 6):
                            pe.wait_ge(ht_ev, t - 5)
                        turn(bank8[4 + u % 2][0:I, 0:P], hid[:, (u - 4) % 4, :], P).then_inc(ht_mm, 1)
                    if not (first and u < 6) and not (last and u >= 6):
                        e = expert_of(it, u, 6)
                        pe.wait_ge(ht_ev, t - 5)
                        if not first:
                            pe.wait_ge(y_ev, t - 7)
                        pe.matmul(bank8[6 + u % 2][:, 0:P], hid_t[:, (u - 6) % 4, :], w_down[:, bass.ds(e * P, P)],
                                  start=True, stop=True).then_inc(y_mm, 1)

            experts_turn(0, True, False)
            with pe.Fori(1, NT // TU) as it:
                experts_turn(it, False, False)
            experts_turn(NT // TU, False, True)

            pe.wait_ge(y_ev, NT)

            def shared_turn(it):
                for u in range(2):
                    pe.wait_ge(tok_in[u], FETCHES + 16 * it + 16)
                    if not opening(it):
                        pe.wait_ge(ht_ev, NT + it * 2 + u - 1)
                    turn(bank8[u][:, 0:P], own[:, u, :], P).then_inc(xt_mm, 1)
                for u in range(2):
                    pe.wait_ge(xt_ev, NT + it * 2 + u + 1)
                    pe.matmul(bank8[2 + u][:, 0:4 * I], own_t[:, u, :], wt("shared_gu"), start=True, stop=True
                              ).then_inc(gu_mm, 1)
                for u in range(2):
                    pe.wait_ge(h_done, NT + it * 2 + u + 1)
                    for c in range(2):
                        mm = turn(bank8[u][0:I, (1 + c) * P:(2 + c) * P], s_hid[:, u, c * I:(c + 1) * I], P)
                    mm.then_inc(ht_mm, 1)
                for u in range(2):
                    pe.wait_ge(ht_ev, NT + it * 2 + u + 1)
                    if not opening(it):
                        pe.wait_ge(acc_step, ((it - 1) * 2 + u) * TOPK + 1)
                    for c in range(2):
                        mm = pe.matmul(bank8[4 + u][:, 0:P], s_hid_t[:, u, c * P:(c + 1) * P],
                                       s_down[:, c * P:(c + 1) * P], start=c == 0, stop=c == 1)
                    mm.then_inc(y_mm, 1)

            shared_turn(0)
            with pe.Fori(1, NSEQ // 2) as it:
                shared_turn(it)

        @block.scalar
        def _(act):
            ahead(act, "act")
            nc.scalar.preload_act_table_set("natural_log_exp_and_others")
            act.wait_ge(setup, 2)

            def rstd_of(st, it, k):
                two = slice(st * B2, st * B2 + B2)
                act.wait_ge(S[st]["mv"], at(it, B2 - 1, k, 6))
                nc.scalar.activation(lnv[:, two], mv[:, two, 1], ACT.Ln, bias=eps[:, 0:1]).then_inc(lnv_done[st], 1)
                act.wait_ge(lnv_done[st], it * 6 + k + 1)
                nc.scalar.activation(rstd[:, two], lnv[:, two], ACT.Exp, scale=-0.5).then_inc(rstd_done[st], 1)

            def copies(st, made, n_made, name, out, in_):
                for b in range(B2):
                    act.wait_ge(S[st][made], n_made(b))
                    nc.scalar.copy(out(st * B2 + b), in_(st * B2 + b)).then_inc(S[st][name], 1)

            def norm_t(st, it, k):
                copies(st, "lnt_mm", lambda b: at(it, b, k, 6), "ln_t", lambda q: ln_t[:, q, :], lambda q: bank[:, q, 0:P])

            def keys_t(st, it, k, out, sk):
                copies(st, "kt_mm", lambda b: at(it, b, k, 3), "kt", lambda q: out[:, q, :, :],
                       lambda q: bank[:, q, 0:4 * sk].rearrange("p (g c) -> p g c", g=4))

            def queries_t(st, it, k):
                copies(st, "qt_mm", lambda b: at(it, b, k, 6), "qt", lambda q: qt[:, q, :, :],
                       lambda q: bank[:, q, :].rearrange("p (g c) -> p g c", g=4))

            def high_parts(dst, src, sk, step):
                out = dst[0:sk, :, 0:2 * step].rearrange("p h (c e) -> p h c e", c=2)[:, :, :, 0:DH].bitcast(F32R)
                heads = src.rearrange("p (h a c) -> p h a c", h=H, a=1)
                return nc.scalar.copy(out, heads.to_broadcast((sk, H, 2, DH)))

            def attention(st, it, a, sk):
                for _ in range(4):
                    yield
                queries_t(st, it, 2 * a + 1)
                yield
                for b in range(B2):
                    for half in range(2):
                        act.wait_ge(S[st]["st_mm"], half_made(it, a, b, half))
                        if not half:
                            act.wait_ge(S[st]["pv"], at(it, b, a, 3) - 1)
                        nc.scalar.activation(pt[0:sk, st, 8 * half:8 * half + 8, :],
                                             wide[0:sk, st, :, :, :].rearrange("p j g c -> p (j g) c"), ACT.Exp
                                             ).then_inc(S[st]["exp"], 1)
                        yield
                    yield

            def project(st, it, k):
                copies(st, "ot_mm", lambda b: at(it, b, k, 4), "o_t", lambda q: o_t[:, q, :], lambda q: bank[:, q, 0:P])
                yield
                yield

            def norm(st, it, k):
                rstd_of(st, it, k)
                yield
                yield
                norm_t(st, it, k)
                yield

            def cross_queries(st, it, k):
                yield
                for b in range(B2):
                    act.wait_ge(S[st]["qkv"], at(it, b, k, 3))
                    high_parts(qpad[:, st * B2 + b, :, :], qkv[:, st * B2 + b, 0:P], P, 16).then_inc(S[st]["qhi"], 1)
                yield
                queries_t(st, it, 2 * k)
                yield

            def layer0(st, it):
                copies(st, "ctx_mm0", lambda b: at(it, b), "ctx_t", lambda q: ctx_t[:, q, :], lambda q: bank[:, q, 0:SK])
                yield
                rstd_of(st, it, 0)
                yield
                for b in range(B2):
                    act.wait_ge(S[st]["ckv"], at(it, b))
                    high_parts(kpad[:, st * B2 + b, :, :], ckv[:, st * B2 + b, 0, :], SK, DH).then_inc(S[st]["khi"], 1)
                yield
                norm_t(st, it, 0)
                yield
                yield
                keys_t(st, it, 0, kt_x[0], SK)
                yield
                for b in range(B2):
                    high_parts(kpad[:, st * B2 + b, :, :], ckv[:, st * B2 + b, 2, :], SK, DH).then_inc(S[st]["khi"], 1)
                yield
                keys_t(st, it, 1, kt_x[1], SK)
                yield
                for b in range(B2):
                    q = st * B2 + b
                    act.wait_ge(S[st]["rope"], at(it, b))
                    high_parts(kpad[:, q, :, :], qkv[:, q, P:2 * P], P, DH).then_inc(S[st]["khi"], 1)
                    high_parts(qpad[:, q, :, :], qkv[:, q, 0:P], P, 16).then_inc(S[st]["qhi"], 1)
                yield
                keys_t(st, it, 2, kt, P)
                yield
                queries_t(st, it, 0)
                yield
                yield from attention(st, it, 0, P)
                yield from project(st, it, 0)
                yield from norm(st, it, 1)
                yield from cross_queries(st, it, 1)
                yield from attention(st, it, 1, SK)
                yield from project(st, it, 1)
                yield from norm(st, it, 2)
                yield

            def layer1(st, it):
                yield from norm(st, it, 3)
                for b in range(B2):
                    q = st * B2 + b
                    act.wait_ge(S[st]["qkv_mm"], at(it, b, 2, 4))
                    nc.scalar.mul(qkv[:, q, 0:2 * P], bank[:, q, 0:2 * P], SCALE)
                    nc.scalar.copy(v[:, q, :, 0:DH], bank[:, q, 2 * P:3 * P].rearrange("p (h c) -> p h c", h=H)
                                   ).then_inc(S[st]["fqkv"], 1)
                yield
                copies(st, "fqkt_mm", lambda b: at(it, b), "fqk_t", lambda q: fqk_t[:, q, :],
                       lambda q: bank[:, q, 0:2 * P])
                yield
                yield
                for i in range(2):
                    for b in range(B2):
                        q = st * B2 + b
                        act.wait_ge(S[st]["fsub"], at(it, b, i, 2))
                        nc.scalar.activation(phi[:, q, i, :], phi[:, q, i, :], ACT.Exp).then_inc(S[st]["fexp"], 1)
                    yield
                copies(st, "pqt_mm", lambda b: at(it, b), "pq_t", lambda q: pq_t[:, q, :], lambda q: bank[:, q, :])
                yield
                yield
                yield
                yield from project(st, it, 2)
                yield from norm(st, it, 4)
                yield from cross_queries(st, it, 2)
                yield from attention(st, it, 2, SK)
                yield from project(st, it, 3)
                yield from norm(st, it, 5)
                act.wait_ge(route_mm[st], 2 * it + 1)
                nc.scalar.activation(sc[:, st * B2:st * B2 + B2, :],
                                     bank[:, st * B2, 0:B2 * E].rearrange("p (b e) -> p b e", b=B2), ACT.Exp,
                                     scale=-1.0).then_inc(gate_exp[st], 1)
                for _ in range(5):
                    yield

            turns(act, layer0, layer1)

            act.wait_ge(table_in, 32)

            def experts_turn(it, first, last):
                for u in range(TU):
                    t = it * TU + u
                    if not last:
                        act.wait_ge(xt_mm, t + 1)
                        nc.scalar.copy(tok_t[:, u % 4, :], bank8[u % 2][:, 0:P]).then_inc(xt_ev, 1)
                    if not (first and u < 2) and not (last and u >= 2):
                        act.wait_ge(gu_mm, t - 1)
                        if not (first and u < 6):
                            act.wait_ge(h_done, t - 5)
                        nc.scalar.activation(act_g[:, (u - 2) % 4, :], bank8[2 + u % 2][:, 0:I], ACT.Silu
                                             ).then_inc(g_act, 1)
                    if not (first and u < 6) and not (last and u >= 6):
                        act.wait_ge(y_mm, t - 5)
                        lane = (u - 6) % TU
                        if lane == 0 and not first:
                            act.wait_ge(y_out[0], 16 * it)
                        if lane == 4 and not opening(it - 1):
                            act.wait_ge(y_out[1], 16 * (it - 1))
                        nc.scalar.copy(y[:, lane, :], bank8[6 + u % 2][:, 0:P]).then_inc(y_ev, 1)

            experts_turn(0, True, False)
            experts_turn(1, False, False)
            with act.Fori(2, NT // TU) as it:
                experts_turn(it, False, False)
            experts_turn(NT // TU, False, True)

            def shared_turn(it):
                for u in range(2):
                    act.wait_ge(xt_mm, NT + it * 2 + u + 1)
                    nc.scalar.copy(own_t[:, u, :], bank8[u][:, 0:P]).then_inc(xt_ev, 1)
                for u in range(2):
                    act.wait_ge(gu_mm, NT + it * 2 + u + 1)
                    nc.scalar.activation(s_act[:, u, :], bank8[2 + u][:, 0:2 * I], ACT.Silu).then_inc(g_act, 1)
                for u in range(2):
                    act.wait_ge(ht_mm, NT + it * 2 + u + 1)
                    nc.scalar.copy(s_hid_t[:, u, :], bank8[u][0:I, P:3 * P]).then_inc(ht_ev, 1)

            shared_turn(0)
            with act.Fori(1, NSEQ // 2) as it:
                shared_turn(it)

        @block.gpsimd
        def _(pool):
            ahead(pool, "pool")
            for t in [qpad, kpad]:
                nc.gpsimd.memset(t[:, :, :, :], 0.0)
            nc.gpsimd.memset(zeros[:, :], 0.0)
            nc.gpsimd.memset(onesb[:, :], 1.0)
            nc.gpsimd.memset(totalb[:, :], 0.0)
            nc.gpsimd.memset(total[:, :], 0.0)
            nc.gpsimd.memset(ones_e[:, :], 1.0)
            nc.gpsimd.memset(idx_all[:, :], 0)
            nc.gpsimd.memset(eps[:, :], LN_EPS).then_inc(pool_step, 1)
            pool.wait_ge(pool_step, 1)
            nc.gpsimd.memset(kpad[:, :, :, 3 * DH:3 * DH + 1], 1.0)
            for t in [v] + v_x:
                last = nc.gpsimd.memset(t[:, :, :, DH:DH + 1], 1.0)
            last.then_inc(setup_pe, 1)
            pool.wait_ge(setup, 2)
            pool.wait_ge(loads, 16 * N_LOADS)
            ROPE = 3

            def with_bias(st, it, k, name, src):
                for b in range(B2):
                    q = st * B2 + b
                    if k:
                        pool.wait_ge(S[st]["res"], at(it, b, {1: 0, 2: 2, 3: 3}[k], 5))
                    else:
                        pool.wait_ge(S[st]["res"], before(it, b, 0, 5))
                        pool.wait_ge(x_loaded[st], 16 * it + 16)
                    nc.gpsimd.tensor_tensor(xb[:, q, :], src[:, q, :], bias(name), ALU.add).then_inc(S[st]["xb"], 1)

            def low_part(dst, src, sk, place, hi_place=0):
                return nc.gpsimd.tensor_tensor(dst[0:sk, :, place:place + DH].bitcast(F32R),
                                               src.rearrange("p (h c) -> p h c", h=H), dst[0:sk, :, 0:DH], ALU.subtract)

            def values_x(st, it, i, ready):
                for b in range(B2):
                    q = st * B2 + b
                    pool.wait_ge(S[st]["ckv"], at(it, b))
                    plain(pool)
                    nc.gpsimd.tensor_copy(v_x[i][:, q, :, 0:DH], ckv[:, q, 2 * i + 1, :].rearrange("p (h c) -> p h c", h=H))

            def keys_low(st, it, i):
                for b in range(B2):
                    q = st * B2 + b
                    pool.wait_ge(S[st]["khi"], at(it, b, i, 3))
                    low_part(kpad[:, q, :, :], ckv[:, q, 2 * i, :], SK, 2 * DH).then_inc(S[st]["klo"], 1)

            def send(st, turn, n):
                q, j = st * B2 + n // TOPK, n % TOPK
                if n == 0:
                    pool.wait_ge(routed[st], 3 * turn + 3)
                    plain(pool)
                    if isinstance(turn, int) and turn == 0:
                        pool.wait_ge(cleared, 16 * E)
                nc.gpsimd.indirect_dma_start(
                    out=xs_d, out_offset=bass.IndirectOffsetOnAxis(ap=idx[:, q, j:j + 1], axis=0),
                    in_=ln_r[:, q, :], in_offset=None).then_inc(scattered[st], 16)

            def attention(st, it, sends):
                for _ in range(11):
                    if sends and sends[0] < B2 * TOPK:
                        send(st, it - 1, sends[0])
                        sends[0] += 1
                    yield

            def norm(st, it, k=None, name=None):
                yield
                if k:
                    with_bias(st, it, k, name, x)
                yield
                yield

            def cross_queries(st, it, k):
                yield
                for b in range(B2):
                    q = st * B2 + b
                    pool.wait_ge(S[st]["qhi"], at(it, b, k, 3))
                    low_part(qpad[:, q, :, :], qkv[:, q, 0:P], P, DH).then_inc(S[st]["qlo"], 1)
                yield
                yield

            def layer0(st, it):
                sends = None if opening(it) else [0]
                with_bias(st, it, 0, "o0", x_in)
                yield
                yield
                values_x(st, it, 0, None)
                yield
                keys_low(st, it, 0)
                yield
                yield
                for b in range(B2):
                    q = st * B2 + b
                    own = it * (B2 * ROPE) + b * ROPE
                    pool.wait_ge(S[st]["qkv"], at(it, b, 0, 3))
                    qk = qkv[:, q, 0:2 * P].rearrange("p (n c) -> p n c", c=2)
                    sin = const("rope_s").rearrange("p (n c) -> p n c", c=2)
                    crossed = rot[:, 1, :].rearrange("p (n c) -> p n c", c=2)
                    nc.gpsimd.tensor_tensor(rot[:, 0, :], qkv[:, q, 0:2 * P], const("rope_c"), ALU.mult)
                    nc.gpsimd.tensor_tensor(crossed[:, :, 0], qk[:, :, 1], sin[:, :, 0], ALU.mult
                                            ).then_inc(pool_own[st], 1)
                    nc.gpsimd.tensor_tensor(crossed[:, :, 1], qk[:, :, 0], sin[:, :, 1], ALU.mult
                                            ).then_inc(pool_own[st], 1)
                    nc.gpsimd.tensor_copy(v[:, q, :, 0:DH], qkv[:, q, 2 * P:3 * P].rearrange("p (h c) -> p h c", h=H)
                                          ).then_inc(pool_own[st], 1)
                    pool.wait_ge(pool_own[st], own + ROPE)
                    nc.gpsimd.tensor_tensor(qkv[:, q, 0:2 * P], rot[:, 0, :], rot[:, 1, :], ALU.add
                                            ).then_inc(S[st]["rope"], 1)
                    pool.wait_ge(S[st]["rope"], at(it, b))
                yield
                values_x(st, it, 1, None)
                keys_low(st, it, 1)
                yield
                yield
                for b in range(B2):
                    q = st * B2 + b
                    pool.wait_ge(S[st]["khi"], at(it, b, 2, 3))
                    low_part(kpad[:, q, :, :], qkv[:, q, P:2 * P], P, 2 * DH).then_inc(S[st]["klo"], 1)
                    pool.wait_ge(S[st]["qhi"], at(it, b, 0, 3))
                    low_part(qpad[:, q, :, :], qkv[:, q, 0:P], P, DH).then_inc(S[st]["qlo"], 1)
                yield
                yield
                yield
                yield from attention(st, it, sends)
                yield
                yield
                yield from norm(st, it, 1, "o_x0")
                yield from cross_queries(st, it, 1)
                yield from attention(st, it, sends)
                yield
                yield
                yield from norm(st, it)
                yield

            def layer1(st, it):
                yield from norm(st, it, 2, "o_f")
                yield
                for b in range(B2):
                    q = st * B2 + b
                    pool.wait_ge(S[st]["fqkv"], at(it, b))
                    nc.gpsimd.tensor_tensor(sq[:, q, :], qkv[:, q, 0:2 * P], qkv[:, q, 0:2 * P], ALU.mult
                                            ).then_inc(S[st]["sq"], 1)
                for _ in range(9):
                    yield
                yield from norm(st, it, 3, "o_x1")
                yield from cross_queries(st, it, 2)
                yield from attention(st, it, None)
                for _ in range(10):
                    yield

            turns(pool, layer0, layer1)
            for st in range(2):
                for n in range(B2 * TOPK):
                    send(st, TURNS - 1, n)

            def store_tiles(it, half):
                pool.wait_ge(y_ev, it * TU + 4 * half + 4)
                nc.gpsimd.dma_start(ys_d[bass.ds(it * TU + 4 * half, 4)].rearrange("t p f -> p t f"),
                                    y[:, 4 * half:4 * half + 4, :]).then_inc(y_out[half], 16)

            with pool.Fori(0, NT // TU) as it:
                for half in range(2):
                    store_tiles(it, half)
            y_rows = ys_d.rearrange("t p f -> (t p) f")
            pool.wait_ge(moving, 5 * (NT // TU))
            for u in range(2):
                pool.wait_ge(y_out[u], 16 * (NT // TU))

            def gather(it):
                for u in range(2):
                    if not opening(it):
                        pool.wait_ge(summed, it * 2 + u - 1)
                        plain(pool)
                    nc.gpsimd.tensor_copy(idx_f[:, u, :], row_all[:, bass.ds(it * 16 + u * 8, 8)]).then_inc(picked, 1)
                    pool.wait_ge(picked, it * 2 + u + 1)
                    plain(pool)
                    for j in range(TOPK):
                        nc.gpsimd.indirect_dma_start(
                            out=got[:, u, j, :], out_offset=None, in_=y_rows,
                            in_offset=bass.IndirectOffsetOnAxis(ap=idx_f[:, u, j:j + 1], axis=0)
                        ).then_inc(gathered[u], 16)

            gather(0)
            with pool.Fori(1, NSEQ // 2) as it:
                gather(it)

        @block.vector
        def _(dve):
            ahead(dve, "dve")
            dve.wait_ge(loads, 16 * N_LOADS)
            dve.wait_ge(setup_pe, 1)
            nc.vector.tensor_copy(identb[:, :], ident)
            nc.vector.tensor_copy(upperb[:, :], const("upper"))
            for j in range(4):
                nc.vector.tensor_copy(causal4[:, j, :], const("causal"))
                nc.vector.tensor_copy(causal4_t[:, j, :], const("causal_t"))
            nc.vector.tensor_scalar(sign_a[:, :], wt("ffn"), 0.0, None, ALU.is_gt)
            nc.vector.tensor_scalar(sign_w[:, :], wt("ffn"), 0.0, None, ALU.is_lt)
            nc.vector.tensor_scalar(maskb[:, :], mask_i[:, :], 0, -1.0e9, ALU.is_equal, ALU.mult)
            nc.vector.tensor_scalar(seen[:, :], mask_i[:, :], 0, None, ALU.not_equal).then_inc(setup, 1)
            dve.wait_ge(setup, 1)
            nc.vector.tensor_tensor(sign_w[:, :], sign_a[:, :], sign_w[:, :], ALU.subtract)
            for j in range(4):
                nc.vector.tensor_copy(mask4[:, j, :], maskb[:, :])
            nc.vector.tensor_reduce(q_scale[:, :], seen[:, :], AX, ALU.max).then_inc(dve_step, 1)
            dve.wait_ge(dve_step, 1)
            nc.vector.tensor_scalar(q_scale[:, :], q_scale[:, :], SCALE, None, ALU.mult)
            nc.vector.tensor_scalar(q_bias1[:, :], bias("q_x1"), SCALE, None, ALU.mult).then_inc(dve_step, 1)
            dve.wait_ge(dve_step, 2)
            nc.vector.tensor_scalar(q_bias0[:, :], bias("q_x0"), q_scale[:, 0:1], None, ALU.mult)
            dve.wait_ge(mask_t, 1)
            for j in range(4):
                cp = nc.vector.tensor_copy(mask4_t[:, j, :], bank[0:SK, 0, 0:P // 2].bitcast(BF16))
            cp.then_inc(setup, 1)
            dve.wait_ge(setup, 2)

            class Chain:

                def __init__(self, st, it, start):
                    self.sem, self.base, self.n = dve_own[st], it * (STEPS0 + STEPS1) + start, 0

                def __call__(self, ins, alone=False):
                    self.n += 1
                    ins.then_inc(self.sem, 1)
                    dve.wait_ge(self.sem, self.base + self.n)
                    if alone:
                        plain(dve)

                def note(self, ins):
                    self.n += 1
                    ins.then_inc(self.sem, 1)

            def statistics(own, st, it, k, src):
                for b in range(B2):
                    q = st * B2 + b
                    if k:
                        dve.wait_ge(S[st]["res"], at(it, b, k - 1, 5))
                    else:
                        dve.wait_ge(x_loaded[st], 16 * it + 16)
                    ins = nc.vector.bn_stats(stats[:, q, :], src[:, q, :])
                    if b < B2 - 1:
                        own.note(ins)
                own(ins, alone=True)
                for b in range(B2):
                    q = st * B2 + b
                    nc.vector.bn_aggr(mv[:, q, :], stats[:, q, :]).then_inc(S[st]["mv"], 1)

            def normalise(st, it, k, src, out):
                dve.wait_ge(rstd_done[st], it * 6 + k + 1)
                dve.wait_ge(S[st]["mv"], at(it, B2 - 1, k, 6))
                if k == 5 and not opening(it):
                    dve.wait_ge(scattered[st], 16 * B2 * TOPK * it)
                    dve.wait_ge(ln_out[st], 16 * it)
                for b in range(B2):
                    q = st * B2 + b
                    nc.vector.tensor_scalar(out[:, q, :], src[:, q, :], mv[:, q, 0:1], rstd[:, q:q + 1], ALU.subtract,
                                            ALU.mult).then_inc(S[st]["ln"], 1)

            def norm(own, st, it, k, src, out):
                statistics(own, st, it, k, src)
                yield
                normalise(st, it, k, src, out)
                yield
                yield

            def heads_out(own, st, it, b, made, n_made):
                q = st * B2 + b
                dve.wait_ge(S[st][made], n_made)
                heads = bank[:, q, 0:H * DA].rearrange("p (h c) -> p h c", h=H)
                if made == "num_mm":
                    own(nc.vector.tensor_scalar(rden[:, q, :], heads[:, :, DH], M * FAV_EPS, None, ALU.add))
                    own(nc.vector.reciprocal(rden[:, q, :], rden[:, q, :]))
                else:
                    own(nc.vector.reciprocal(rden[:, q, :], heads[:, :, DH]))
                nc.vector.tensor_tensor(o[:, q, :].rearrange("p (h c) -> p h c", h=H), heads[:, :, 0:DH],
                                        rden[:, q, :].rearrange("p (h a) -> p h a", a=1).to_broadcast((P, H, DH)),
                                        ALU.mult).then_inc(S[st]["o"], 1)

            def attention(own, st, it, a, sk):
                for b in range(B2):
                    for half in range(2):
                        dve.wait_ge(S[st]["sc_mm"], half_made(it, a, b, half))
                        place = qpad[:, st * B2 + b, :, 3 * DH].rearrange("p (g j) -> p j g", j=4)
                        nc.vector.tensor_reduce(place[:, 2 * half:2 * half + 2, :].bitcast(F32R),
                                                wide[:, st, :, :, 0:sk], AX, ALU.max, negate=True
                                                ).then_inc(S[st]["max"], 1)
                        yield
                yield
                for b in range(B2):
                    yield
                    yield
                    heads_out(own, st, it, b, "pv", at(it, b, a, 3))
                    yield

            def project(st, it, k, n_xb):
                yield
                residual(st, it, k, n_xb)
                yield

            def residual(st, it, k, n_xb):
                for b in range(B2):
                    q = st * B2 + b
                    dve.wait_ge(S[st]["proj"], at(it, b, k, 5))
                    if k == 0 and not opening(it):
                        dve.wait_ge(res_out[st], 16 * it)
                    if n_xb is None:
                        base = x
                    else:
                        base = xb
                        dve.wait_ge(S[st]["xb"], at(it, b, n_xb, 4))
                    nc.vector.tensor_tensor(x[:, q, :], base[:, q, :], bank[:, q, 0:P], ALU.add
                                            ).then_inc(S[st]["res"], 1)

            def cross_queries(st, it, k, n_raw, scale, bias_tile):
                for b in range(B2):
                    q = st * B2 + b
                    dve.wait_ge(S[st]["qkv_mm"], at(it, b, k, 4))
                    nc.vector.scalar_tensor_tensor(qkv[:, q, 0:P], bank[:, q, 0:P], scale, bias_tile, ALU.mult, ALU.add
                                                   ).then_inc(S[st]["qkv"], 1)
                yield
                yield
                yield

            def layer0(st, it):
                own = Chain(st, it, 0)
                statistics(own, st, it, 0, x_in)
                yield
                for b in range(B2):
                    q = st * B2 + b
                    dve.wait_ge(S[st]["ctx_mm"], at(it, b))
                    nc.vector.tensor_tensor(ckv[:, q, :, :].rearrange("p a c -> p (a c)"), bank[0:SK, q, :],
                                            bias("ctx")[0:SK, :], ALU.add).then_inc(S[st]["ckv"], 1)
                yield
                normalise(st, it, 0, x_in, ln)
                yield
                yield
                for b in range(B2):
                    q = st * B2 + b
                    dve.wait_ge(S[st]["qkv_mm"], at(it, b, 0, 4))
                    nc.vector.tensor_tensor(qkv[:, q, :], bank[:, q, 0:3 * P], bias("qkv0"), ALU.add
                                            ).then_inc(S[st]["qkv"], 1)
                for _ in range(7):
                    yield
                yield from attention(own, st, it, 0, P)
                yield from project(st, it, 0, 0)
                yield from norm(own, st, it, 1, x, ln)
                yield from cross_queries(st, it, 1, 0, q_scale[:, 0:1], q_bias0[:, :])
                yield from attention(own, st, it, 1, SK)
                yield from project(st, it, 1, 1)
                yield from norm(own, st, it, 2, x, ln)
                residual(st, it, 2, None)
                assert own.n == STEPS0, own.n
                yield

            def layer1(st, it):
                own = Chain(st, it, STEPS0)
                yield from norm(own, st, it, 3, x, ln)
                yield
                for b in range(B2):
                    q = st * B2 + b
                    dve.wait_ge(S[st]["sq"], at(it, b))
                    nc.vector.tensor_reduce(norm2[:, q, :], sq[:, q, :].rearrange("p (h c) -> p h c", c=DH), AX, ALU.add
                                            ).then_inc(S[st]["norm2"], 1)
                yield
                for i in range(2):
                    for b in range(B2):
                        q = st * B2 + b
                        dve.wait_ge(S[st]["xw"], at(it, b, i, 2))
                        feats = bank[:, q, :].rearrange("p (h m) -> p h m", h=H)
                        cut = fmax[:, q, i * H:(i + 1) * H]
                        own(nc.vector.tensor_reduce(cut, feats, AX, ALU.max))
                        dve.wait_ge(S[st]["norm2"], at(it, b))
                        own(nc.vector.scalar_tensor_tensor(cut, norm2[:, q, i * H:(i + 1) * H], 0.5, cut, ALU.mult,
                                                           ALU.add))
                        nc.vector.tensor_tensor(phi[:, q, i, :].rearrange("p (h m) -> p h m", h=H), feats,
                                                cut.rearrange("p (h a) -> p h a", a=1).to_broadcast((P, H, M)),
                                                ALU.subtract).then_inc(S[st]["fsub"], 1)
                    yield
                for i in range(2):
                    for b in range(B2):
                        q = st * B2 + b
                        dve.wait_ge(S[st]["fexp"], at(it, b, i, 2))
                        nc.vector.tensor_scalar(phi[:, q, i, :], phi[:, q, i, :], FAV_EPS, None, ALU.add
                                                ).then_inc(S[st]["fphi"], 1)
                    yield
                for b in range(B2):
                    q = st * B2 + b
                    dve.wait_ge(S[st]["kv_mm"], at(it, b))
                    nc.vector.tensor_tensor(kvb[:, q, :], bank[:, q, 0:H * DA], const("blocks"), ALU.mult
                                            ).then_inc(S[st]["kvb"], 1)
                yield
                for b in range(B2):
                    heads_out(own, st, it, b, "num_mm", at(it, b))
                yield
                yield from project(st, it, 3, 2)
                yield from norm(own, st, it, 4, x, ln)
                yield from cross_queries(st, it, 3, 1, SCALE, q_bias1[:, :])
                yield from attention(own, st, it, 2, SK)
                yield from project(st, it, 4, 3)
                yield from norm(own, st, it, 5, x, ln_r)
                yield
                yield from router(own, st, it)

            def router(own, st, it):
                two = slice(st * B2, st * B2 + B2)
                seqs = range(st * B2, st * B2 + B2)
                dve.wait_ge(gate_exp[st], it + 1)
                own(nc.vector.tensor_scalar(sc[:, two, :], sc[:, two, :], 1.0, None, ALU.add))
                own(nc.vector.reciprocal(sc[:, two, :], sc[:, two, :]))
                for q in seqs:
                    ins = nc.vector.tensor_tensor(sfc[:, q, :], sc[:, q, :], bias("gate"), ALU.add)
                own(ins, alone=True)
                for q in seqs:
                    for g in range(NG):
                        ins = nc.vector.max(top8[:, q, g, :], sfc[:, q, g * 8:(g + 1) * 8])
                own(ins)
                own(nc.vector.tensor_tensor(gsum[:, two, :], top8[:, two, :, 0], top8[:, two, :, 1], ALU.add))
                yield
                for q in seqs:
                    mine = gsum[:, q, :].rearrange("p (g a) -> p g a", a=1).to_broadcast((P, NG, NG))
                    theirs = gsum[:, q, :].rearrange("p (a g) -> p a g", a=1).to_broadcast((P, NG, NG))
                    nc.vector.tensor_tensor(more[:, q, :, :], theirs, mine, ALU.is_gt)
                    ins = nc.vector.tensor_tensor(least[:, q, :, :], theirs, mine, ALU.is_ge)
                own(ins)
                for q in seqs:
                    ins = nc.vector.tensor_tensor(least[:, q, :, :].rearrange("p a g -> p (a g)"),
                                                  least[:, q, :, :].rearrange("p a g -> p (a g)"), const("before"),
                                                  ALU.mult)
                own(ins)
                flat = "p b a g -> p (b a g)"
                own(nc.vector.tensor_tensor(more[:, two, :, :].rearrange(flat), more[:, two, :, :].rearrange(flat),
                                            least[:, two, :, :].rearrange(flat), ALU.max))
                own(nc.vector.tensor_reduce(glead[:, two, :], more[:, two, :, :], AX, ALU.add))
                own(nc.vector.tensor_scalar(glead[:, two, :], glead[:, two, :], TOPG - 0.5, None, ALU.is_lt))
                own(nc.vector.tensor_tensor(
                    masked[:, two, :].rearrange("p b (g c) -> p (b g) c", c=8),
                    sfc[:, two, :].rearrange("p b (g c) -> p (b g) c", c=8),
                    glead[:, two, :].rearrange("p b g -> p (b g)").rearrange("p (n a) -> p n a", a=1
                                                                             ).to_broadcast((P, B2 * NG, 8)), ALU.mult),
                    alone=True)
                for q in seqs:
                    ins = nc.vector.max(best[:, q, :], masked[:, q, :])
                own(ins, alone=True)
                for q in seqs:
                    ins = nc.vector.match_replace(taken[:, q, :], best[:, q, :], masked[:, q, :], GONE)
                own(ins)
                nc.vector.tensor_scalar(chosenb[:, two, :], taken[:, two, :], GONE / 2, None, ALU.is_lt)
                own(nc.vector.tensor_scalar(chosen[:, two, :], taken[:, two, :], GONE / 2, None, ALU.is_lt))
                dve.sem_inc(routed[st], 1)
                yield
                own(nc.vector.tensor_tensor(gw[:, two, :], chosen[:, two, :], sc[:, two, :], ALU.mult))
                own(nc.vector.tensor_reduce(wsum[:, two], gw[:, two, :], AX, ALU.add))
                own(nc.vector.tensor_scalar(wsum[:, two], wsum[:, two], 1e-20, None, ALU.add))
                own(nc.vector.reciprocal(wsum[:, two], wsum[:, two]))
                own(nc.vector.tensor_scalar(wsum[:, two], wsum[:, two], ROUTED, None, ALU.mult))
                own(nc.vector.tensor_tensor(gw[:, two, :], gw[:, two, :],
                                            wsum[:, two].rearrange("p (b a) -> p b a", a=1).to_broadcast((P, B2, E)),
                                            ALU.mult))
                yield
                dve.wait_ge(route_mm[st], 2 * it + 2)
                for q in seqs:
                    b = q - st * B2
                    ins = nc.vector.tensor_tensor(slot[:, q, :], bank[:, st * B2 + 1, b * E:(b + 1) * E],
                                                  const("first_slot"), ALU.add)
                own(ins)
                dve.sem_inc(routed[st], 1)
                for q in seqs:
                    own(nc.vector.tensor_tensor(total[:, :], total[:, :], chosen[:, q, :], ALU.add))
                nc.vector.tensor_copy(totalb[:, :], total[:, :])
                own(nc.vector.tensor_tensor(slot[:, two, :], slot[:, two, :], chosen[:, two, :], ALU.mult), alone=True)
                for q in seqs:
                    ins = nc.vector.max(slot8[:, q, :], slot[:, q, :])
                own(ins)
                own(nc.vector.tensor_scalar(idx[:, two, :], slot8[:, two, :], -1.0, None, ALU.add))
                for q in seqs:
                    for j in range(TOPK):
                        ins = nc.vector.scalar_tensor_tensor(picks_of[st][:, j, :], slot[:, q, :], slot8[:, q, j:j + 1],
                                                             gw[:, q, :], ALU.is_equal, ALU.mult,
                                                             accum_out=w8[:, q, j:j + 1])
                    own(ins)
                at_turn = bass.ds(it * (G * 8) + st * (B2 * 8), B2 * 8)
                nc.vector.tensor_copy(idx_all[:, at_turn], idx[:, two, :].rearrange("p b j -> p (b j)"))
                own(nc.vector.tensor_copy(w_all[:, at_turn], w8[:, two, :].rearrange("p b j -> p (b j)")))
                dve.sem_inc(routed[st], 1)
                assert own.n == STEPS1, own.n
                yield

            turns(dve, layer0, layer1)

            done = 2

            def late(ins):
                nonlocal done
                done += 1
                ins.then_inc(dve_step, 1)
                dve.wait_ge(dve_step, done)

            dve.wait_ge(counted, 1)
            late(nc.vector.tensor_scalar(room[:, :], bank[:, 0, 0:E], float(LAST), None, ALU.is_le))
            late(nc.vector.tensor_tensor(empty[:, :], room[:, :], const("last_tile"), ALU.mult))
            late(nc.vector.tensor_reduce(spare[:, :], empty[:, :], AX, ALU.max))
            late(nc.vector.tensor_tensor(tail_f[:, :], bank[:, 0, 0:E], const("first_slot"), ALU.add))
            late(nc.vector.tensor_scalar(tail_f[:, :], tail_f[:, :], -1.0, spare[:, 0:1], ALU.add, ALU.subtract))
            late(nc.vector.tensor_tensor(tail_f[:, :], tail_f[:, :], room[:, :], ALU.mult))
            nc.vector.tensor_scalar(tail_i[:, :], tail_f[:, :], spare[:, 0:1], None, ALU.add).then_inc(tables, 1)
            late(nc.vector.tensor_scalar(n_int[:, :], bank[:, 0, 0:E], float(P - 1), None, ALU.add))
            late(nc.vector.tensor_scalar(n_int[:, :], n_int[:, :], 7, None, ALU.arith_shift_right))
            late(nc.vector.tensor_copy(n_tiles[:, :], n_int[:, :]))
            late(nc.vector.tensor_tensor_scan(upto[:, :], ones_e[:, :], n_tiles[:, :], 0.0, ALU.mult, ALU.add))
            for c in range(TCOLS):
                tile_no = const("tile_no")[:, c:c + 1]
                late(nc.vector.scalar_tensor_tensor(past[:, :], upto[:, :], tile_no, ones_e[:, :], ALU.is_le, ALU.mult,
                                                    accum_out=which[:, c:c + 1]))
                late(nc.vector.scalar_tensor_tensor(past[:, :], upto[:, :], tile_no, n_tiles[:, :], ALU.is_le, ALU.mult,
                                                    accum_out=skipped[:, c:c + 1]))
            late(nc.vector.tensor_tensor(skipped[:, :], const("tile_no"), skipped[:, :], ALU.subtract))
            late(nc.vector.tensor_scalar(skipped[:, :], skipped[:, :], float(P), None, ALU.mult))
            late(nc.vector.scalar_tensor_tensor(skipped[:, :], which[:, :], float(REGION), skipped[:, :], ALU.mult,
                                                ALU.add))
            late(nc.vector.tensor_scalar(skipped[:, :], skipped[:, :], spare[:, 0:1], None, ALU.subtract))
            late(nc.vector.scalar_tensor_tensor(skipped[:, :], which[:, :], E - 0.5, skipped[:, :], ALU.is_lt,
                                                ALU.mult))
            late(nc.vector.tensor_scalar(rowf[:, 0:TCOLS], skipped[:, :], spare[:, 0:1], None, ALU.add))
            late(nc.vector.tensor_scalar(rowf[:, TCOLS:], which[:, :], float(E - 1), None, ALU.min))
            nc.vector.tensor_copy(rowi[:, :], rowf[:, :]).then_inc(tables, 1)
            late(nc.vector.tensor_tensor(shift[:, :], upto[:, :], n_tiles[:, :], ALU.subtract))
            late(nc.vector.tensor_scalar(shift[:, :], shift[:, :], float(P), 1.0, ALU.mult, ALU.add))
            late(nc.vector.tensor_tensor(shift[:, :], shift[:, :], const("first_slot"), ALU.subtract))
            late(nc.vector.tensor_scalar(of_all[:, :], idx_all[:, :], REGION.bit_length() - 1, None,
                                         ALU.arith_shift_right))

            def moves(it):
                def own(ins, n):
                    ins.then_inc(moving, 1)
                    dve.wait_ge(moving, it * 5 + n)

                seq = bass.ds(it * 8, 8)
                own(nc.vector.tensor_copy(of[:, :], of_all[:, seq]), 1)
                mine = of[:, :].rearrange("p (j a) -> p j a", a=1).to_broadcast((P, TOPK, E))
                every = const("expert").rearrange("p (a e) -> p a e", a=1).to_broadcast((P, TOPK, E))
                by = shift[:, :].rearrange("p (a e) -> p a e", a=1).to_broadcast((P, TOPK, E))
                own(nc.vector.tensor_tensor(same[:, :, :], every, mine, ALU.is_equal), 2)
                own(nc.vector.tensor_tensor(same[:, :, :], same[:, :, :], by, ALU.mult), 3)
                nc.vector.tensor_reduce(moved[:, :], same[:, :, :], AX, ALU.add).then_inc(moving, 1)

            def experts_turn(it, first, last):
                for u in range(TU):
                    t = it * TU + u
                    if not (first and u < 2) and not (last and u >= 2):
                        dve.wait_ge(g_act, t - 1)
                        if not (first and u < 6):
                            dve.wait_ge(ht_mm, t - 5)
                        nc.vector.tensor_tensor(hid[:, (u - 2) % 4, :], act_g[:, (u - 2) % 4, :],
                                                bank8[2 + u % 2][:, I:2 * I], ALU.mult).then_inc(h_done, 1)
                    if not (first and u < 4) and not (last and u >= 4):
                        dve.wait_ge(ht_mm, t - 3)
                        nc.vector.tensor_copy(hid_t[:, (u - 4) % 4, :], bank8[4 + u % 2][0:I, 0:P]).then_inc(ht_ev, 1)
                    if not last and u == 3:
                        moves(it)
                    if not last and u == 5:
                        dve.wait_ge(moving, it * 5 + 4)
                        seq = bass.ds(it * 8, 8)
                        nc.vector.tensor_tensor(row_all[:, seq], moved[:, :], idx_all[:, seq], ALU.add
                                                ).then_inc(moving, 1)

            dve.wait_ge(table_in, 32)
            experts_turn(0, True, False)
            with dve.Fori(1, NT // TU) as it:
                experts_turn(it, False, False)
            experts_turn(NT // TU, False, True)

            def sums(it):
                for u in range(2):
                    dve.wait_ge(g_act, NT + it * 2 + u + 1)
                    nc.vector.tensor_tensor(s_hid[:, u, :], s_act[:, u, :], bank8[2 + u][:, 2 * I:4 * I], ALU.mult
                                            ).then_inc(h_done, 1)
                for u in range(2):
                    t = it * 2 + u
                    dve.wait_ge(y_mm, NT + t + 1)
                    dve.wait_ge(tok_in[2 + u], FETCHES + 16 * it + 16)
                    if not opening(it):
                        dve.wait_ge(tok_in[4 + u], FETCHES + 16 * it)
                    nc.vector.tensor_tensor(acc[:, u, :], res[:, u, :], bank8[4 + u][:, 0:P], ALU.add
                                            ).then_inc(acc_step, 1)
                    dve.wait_ge(gathered[u], 16 * TOPK * (it + 1))
                    for j in range(TOPK):
                        dve.wait_ge(acc_step, t * TOPK + j + 1)
                        ins = nc.vector.scalar_tensor_tensor(
                            acc[:, u, :], got[:, u, j, :], w_all[:, bass.ds(it * 16 + u * 8 + j, 1)], acc[:, u, :],
                            ALU.mult, ALU.add)
                        ins.then_inc(acc_step if j < TOPK - 1 else summed, 1)

            sums(0)
            with dve.Fori(1, NSEQ // 2) as it:
                sums(it)


BEATS0, BEATS1 = 47, 40
STEPS0, STEPS1 = 10, 49




def shape_tables():
    at, n = columns(CONSTS)
    c = np.zeros((P, n), np.float32)

    def put(name, value):
        c[:, at[name][0]:at[name][1]] = value

    i = np.arange(P)
    put("ident", np.eye(P))
    put("causal", np.where(i[None, :] > i[:, None], -1e10, 0.0))
    put("causal_t", np.where(i[:, None] > i[None, :], -1e10, 0.0))
    put("upper", i[:, None] < i[None, :])
    theta = 1.0 / 10000.0 ** (2.0 * np.arange(DH // 2, dtype=np.float32) / DH)
    ang = (i[:, None].astype(np.float32) * theta[None, :].astype(np.float32)).astype(np.float32)
    cos = np.repeat(np.cos(ang)[:, None, :, None], 2, 3).reshape(P, 1, DH)
    sin = np.stack([-np.sin(ang), np.sin(ang)], -1).reshape(P, 1, DH)
    both = np.repeat(np.array([SCALE, 1.0]), H)[None, :, None]
    put("rope_c", (both * cos).reshape(P, -1))
    put("rope_s", (both * sin).reshape(P, -1))
    put("blocks", np.tile(np.repeat(i[:, None] // M == np.arange(4)[None, :], DA, 1), (1, 4)))
    put("first_slot", np.arange(E)[None, :] * REGION + 1)
    put("last_tile", np.arange(E)[None, :] * REGION + LAST)
    put("tile_no", i[:, None] + P * np.arange(TCOLS)[None, :])
    put("expert", np.arange(E)[None, :])
    g = np.arange(NG)
    put("before", (g[None, :] < g[:, None]).reshape(1, -1))
    return c


def kernel(**inputs):
    import concourse.bacc as bacc
    from concourse.bass_utils import run_bass_kernel_spmd

    a = {k: np.asarray(v) for k, v in inputs.items()}
    t = lambda name: a[name].T
    c0, c1, f = "L0_xattn_", "L1_xattn_", "L1_attn_"
    proj = np.zeros((H, DH, H, M), np.float32)
    proj[np.arange(H), :, np.arange(H), :] = a["L1_attn_proj"].transpose(0, 2, 1)
    shared_gu = np.concatenate([t("L1_ffn_Sg"), t("L1_ffn_Su")], 1)
    weight = np.concatenate([
        t("L0_attn_wq"), t("L0_attn_wk"), t("L0_attn_wv"), t("L0_attn_wp"), t(c0 + "Wq"),
        t(c0 + "Wk"), t(c0 + "Wv"), a[c1 + "Wk"], a[c1 + "Wv"], t(c0 + "Wo"), t("L0_ffn_weight"),
        t(f + "Wq"), t(f + "Wk"), t(f + "Wv"), proj.reshape(P, H * M), t(f + "Wo"), a[c1 + "Wq"], a[c1 + "Wo"],
        t("L1_ffn_gate_w"), shared_gu], 1)
    bias = np.concatenate([
        a["L0_attn_bq"], a["L0_attn_bk"], a["L0_attn_bv"], a["L0_attn_bp"], a[c0 + "bq"], a[c0 + "bk"], a[c0 + "bv"],
        a[c1 + "bk"], a[c1 + "bv"], a[c0 + "bo"], a[f + "bo"], a[c1 + "bq"], a[c1 + "bo"], a["L1_ffn_gate_bias"]])
    w_gu = np.stack([a["L1_ffn_Wg"], a["L1_ffn_Wu"]], 1).transpose(3, 0, 1, 2).reshape(P, E * 2 * I)
    arrays = {
        "x_d": a["x"], "ctx_d": a["ctx_1024"], "mask_d": a["mask_1x1xSxS2_ik0"].reshape(P, SK),
        "const_d": shape_tables(), "bias_d": np.broadcast_to(bias[None, :], (P, bias.size)), "weight_d": weight,
        "wgu_d": w_gu, "wdown_d": a["L1_ffn_Wd"].transpose(2, 0, 1).reshape(I, E * P),
        "sdown_d": a["L1_ffn_Sd"].T.reshape(2, I, P).transpose(1, 0, 2).reshape(I, 2 * P)}
    arrays = {k: np.ascontiguousarray(v) for k, v in arrays.items()}
    nc = bacc.Bacc("TRN2", target_bir_lowering=False, num_devices=1)
    args = [nc.dram_tensor(k, v.shape, mybir.dt.from_np(v.dtype), kind="ExternalInput").ap() for k, v in arrays.items()]
    args.append(nc.dram_tensor("out_d", (NSEQ, P, P), F32, kind="ExternalOutput").ap())
    for name, shape, dt in [("xs_d", (ROWS, P), F32), ("ys_d", (NT, P, P), F32), ("ln_d", (NSEQ, P, P), F32),
                            ("res_d", (NSEQ, P, P), F32), ("tab_d", (2 * TCOLS * P,), I32)]:
        args.append(nc.dram_tensor(name, shape, dt).ap())
    build(nc, *args)
    r = run_bass_kernel_spmd(nc, [arrays], core_ids=[0])
    return r.results[0]["out_d"]
```

```python
from contextlib import ExitStack

import concourse.bass as bass
import numpy as np
from concourse import mybir
from concourse.alu_op_type import AluOpType as ALU

ACT = mybir.ActivationFunctionType
F32 = mybir.dt.float32
F32R = mybir.dt.float32r
BF16 = mybir.dt.bfloat16
I32 = mybir.dt.int32
AX = mybir.AxisListType.X

P = 128
NSEQ = 64
SK = 120
H, DH = 16, 8
DA = DH + 1
PAD = 32
VW = 8 * DH
G = 4
B2 = 2
TURNS = NSEQ // G
M = 32
E, I, TOPK, NG, TOPG = 64, 88, 8, 8, 4
REGION = NSEQ * P
NT = NSEQ * P * TOPK // P + E
TCOLS = -(-NT // P)
TU = 8
ROWS = E * REGION
LAST = REGION - P
SCALE = DH ** -0.5
LN_EPS, FAV_EPS = 1e-5, 1e-6
ROUTED = 2.5
GONE = -3.0e38

CONSTS = [("ident", P), ("causal", P), ("causal_t", P), ("upper", P), ("rope_c", 2 * P), ("rope_s", 2 * P),
          ("blocks", H * DA), ("first_slot", E), ("last_tile", E), ("tile_no", TCOLS), ("expert", E), ("before", NG * NG)]
BIASES = [("qkv0", 3 * P), ("o0", P), ("q_x0", P), ("ctx", 4 * P), ("o_x0", P), ("o_f", P), ("q_x1", P), ("o_x1", P),
          ("gate", E)]
WEIGHTS = [("qkv0", 3 * P), ("o0", P), ("q_x0", P), ("ctx", 4 * P), ("o_x0", P), ("ffn", P), ("qkv_f", 3 * P),
           ("proj_f", H * M), ("o_f", P), ("q_x1", P), ("o_x1", P), ("gate", E), ("shared_gu", 4 * I)]


def columns(parts):
    at, n = {}, 0
    for name, w in parts:
        at[name] = (n, n + w)
        n += w
    return at, n


def build(nc, x_d, ctx_d, mask_d, const_d, bias_d, weight_d, wgu_d, wdown_d, sdown_d, out_d,
          xs_d, ys_d, ln_d, res_d, tab_d):
    const_at, n_const = columns(CONSTS)
    bias_at, n_bias = columns(BIASES)
    w_at, n_w = columns(WEIGHTS)
    with ExitStack() as ctx:
        def sb(name, shape, dt=F32):
            return ctx.enter_context(nc.sbuf_tensor(name, shape, dt))

        def sem(name):
            return ctx.enter_context(nc.semaphore(name))

        wide = ctx.enter_context(nc.psum_tensor("wide", [P, 2, 2, 4, P], F32))
        bank = ctx.enter_context(nc.psum_tensor("bank", [P, G, 512], F32))

        consts = sb("consts", [P, n_const])
        biases = sb("biases", [P, n_bias])
        w = sb("w", [P, n_w])
        s_down = sb("s_down", [I, 2 * P])

        def const(name):
            return consts[:, const_at[name][0]:const_at[name][1]]

        def bias(name):
            return biases[:, bias_at[name][0]:bias_at[name][1]]

        def wt(name):
            return w[:, w_at[name][0]:w_at[name][1]]

        ident = const("ident")
        identb = sb("identb", [P, P], BF16)
        upperb = sb("upperb", [P, P], BF16)
        onesb = sb("onesb", [P, P], BF16)
        causal4 = sb("causal4", [P, 4, P], BF16)
        causal4_t = sb("causal4_t", [P, 4, P], BF16)
        mask_i = sb("mask_i", [P, SK], I32)
        maskb = sb("maskb", [P, SK], BF16)
        mask4 = sb("mask4", [P, 4, SK], BF16)
        mask4_t = sb("mask4_t", [SK, 4, P], BF16)
        seen = sb("seen", [P, SK])
        q_scale = sb("q_scale", [P, 1])
        q_bias0 = sb("q_bias0", [P, P])
        q_bias1 = sb("q_bias1", [P, P])
        sign_a = sb("sign_a", [P, P])
        sign_w = sb("sign_w", [P, P])

        idx_all = sb("idx_all", [P, (NT // TU + 1) * 8], I32)
        w_all = sb("w_all", [P, NSEQ * 8])
        ones_e = sb("ones_e", [P, E])
        zeros = sb("zeros", [P, P])
        total = sb("total", [P, E])
        totalb = sb("totalb", [P, E], BF16)
        eps = sb("eps", [P, 1])

        first = ExitStack()

        def sa(name, shape, dt=F32):
            return first.enter_context(nc.sbuf_tensor(name, shape, dt))

        x_in = sa("x_in", [P, G, P])
        ctx_in = sa("ctx_in", [SK, G, P])
        x = sa("x", [P, G, P])
        xb = sa("xb", [P, G, P])
        stats = sa("stats", [P, G, 6])
        mv = sa("mv", [P, G, 2])
        lnv = sa("lnv", [P, G])
        rstd = sa("rstd", [P, G])
        ln = sa("ln", [P, G, P])
        ln_r = sa("ln_r", [P, G, P])
        ln_t = sa("ln_t", [P, G, P])
        ctx_t = ln_t[:, :, 0:SK]
        kt_x = [sa(f"kt_x{i}", [P, G, 4, SK], F32R) for i in range(2)]
        v_x = [sa(f"v_x{i}", [SK, G, P]) for i in range(2)]
        v_pad = sa("v_pad", [P, G, H * VW + 3 * DH])
        sums = sa("sums", [P, 2, 4 * P])
        den_t, rden_t = sums[:, :, 0:P], sums[:, :, P:2 * P]
        kvb = sums[:, :, :].rearrange("p s (b c) -> p (s b) c", b=2)[:, :, 0:H * DA]
        qkv = sa("qkv", [P, G, 3 * P])
        rot = sa("rot", [P, 2, 2 * P])
        kpad = sa("kpad", [P, G, H, PAD])
        kt = sa("kt", [P, G, 4, P], F32R)
        v = sa("v", [P, G, H, DA])
        qpad = sa("qpad", [P, G, H, PAD])
        qt = sa("qt", [P, G, 4, 4, P], F32R)
        pt = sa("pt", [P, 2, H, P])
        pt_flat = pt[:, :, :, :].rearrange("p a h c -> p (a h c)")
        phi = pt_flat.rearrange("p (b i c) -> p b i c", b=G, i=2)
        ckv = phi[0:SK, :, 0, :].rearrange("p b (a c) -> p b a c", a=4)
        pq_t = phi[:, :, 0, :]
        fqk_t = phi[:, :, 1, 0:2 * P]
        sq = phi[:, :, 0, 0:2 * P]
        o = phi[:, :, 1, 0:P]
        top8 = phi[:, :, 0, 0:E].rearrange("p b (g c) -> p b g c", c=8)
        taken = phi[:, :, 0, E:2 * E]
        rden = sa("rden", [P, G, H])
        o_t = sa("o_t", [P, G, P])
        norm2 = sa("norm2", [P, G, 2 * H])
        fmax = sa("fmax", [P, G, 2 * H])

        sc = sa("sc", [P, G, E])
        sfc = sa("sfc", [P, G, E])
        gsum = sa("gsum", [P, G, NG])
        more = sa("more", [P, G, NG, NG])
        least = sa("least", [P, G, NG, NG])
        glead = sa("glead", [P, G, NG])
        masked = sa("masked", [P, G, E])
        best = sa("best", [P, G, 8])
        chosen = sa("chosen", [P, G, E])
        chosenb = sa("chosenb", [P, G, E], BF16)
        gw = sa("gw", [P, G, E])
        wsum = sa("wsum", [P, G])
        slot = sa("slot", [P, G, E])
        slot8 = sa("slot8", [P, G, 8])
        picks_of = [sa(f"picks_{st}", [P, TOPK, E]) for st in range(2)]
        w8 = sa("w8", [P, G, 8])
        idx = sa("idx", [P, G, 8], I32)

        first.close()
        w_gu = sb("w_gu", [P, E * 2 * I])
        w_down = sb("w_down", [I, E * P])
        tok = sb("tok", [P, TU, P])
        tok_t = sb("tok_t", [P, 4, P])
        gu_of = sb("gu_of", [P, 4, 2 * I])
        down_of = sb("down_of", [I, 4, P])
        act_g = sb("act_g", [I, 4, P])
        hid_t = sb("hid_t", [I, 4, P])
        y = sb("y", [P, TU, P])
        n_tiles = sb("n_tiles", [P, E])
        n_int = sb("n_int", [P, E], I32)
        upto = sb("upto", [P, E])
        past = sb("past", [P, E])
        which = sb("which", [P, TCOLS])
        skipped = sb("skipped", [P, TCOLS])
        rowf = sb("rowf", [P, 2 * TCOLS])
        rowi = sb("rowi", [P, 2 * TCOLS], I32)
        rows = sb("rows", [1, 2 * TCOLS * P], I32)
        tail_f = sb("tail_f", [P, E])
        tail_i = sb("tail_i", [P, E], I32)
        room = sb("room", [P, E])
        empty = sb("empty", [P, E])
        spare = sb("spare", [P, 1])
        of_all = sb("of_all", [P, (NT // TU + 1) * 8], I32)
        row_all = sb("row_all", [P, (NT // TU + 1) * 8], I32)
        of = sb("of", [P, 8])
        same = sb("same", [P, TOPK, E])
        moved = sb("moved", [P, TOPK])
        shift = sb("shift", [P, E])
        idx_f = sb("idx_f", [P, 2, 8], I32)
        own = sb("own", [P, 2, P])
        res = sb("res", [P, 2, P])
        own_t = sb("own_t", [P, 2, P])
        s_act = sb("s_act", [P, 2, 2 * I])
        s_hid = sb("s_hid", [P, 2, 2 * I])
        s_hid_t = sb("s_hid_t", [I, 2, 2 * P])
        got = sb("got", [P, 2, TOPK, P])
        acc = sb("acc", [P, 2, P])

        names = {
            "dve": "mv ln ckv qkv max o res norm2 fsub fphi kvb",
            "act": "ctx_t den khi qhi kt ln_t qt exp o_t fqkv fqk_t fexp pq_t",
            "pool": "xb rope values klo qlo sq",
            "pe": "ctx_mm0 ctx_mm kt_mm lnt_mm qkv_mm qt_mm sc_mm st_mm pv ot_mm proj fqkt_mm xw kv_mm pqt_mm num_mm",
        }
        S = [{n: sem(f"{n}_{st}") for part in names.values() for n in part.split()} for st in range(2)]

        def per_stream(name):
            return [sem(f"{name}_{st}") for st in range(2)]

        loads, setup, setup_pe, mask_t = sem("loads"), sem("setup"), sem("setup_pe"), sem("mask_t")
        cleared, down_in, carried = sem("cleared"), sem("down_in"), sem("carried")
        x_loaded, c_loaded, lnv_done, rstd_done = (per_stream(n) for n in ("x_loaded", "c_loaded", "lnv", "rstd"))
        route_mm, gate_exp, routed = (per_stream(n) for n in ("route_mm", "gate_exp", "routed"))
        res_out, ln_out, scattered = (per_stream(n) for n in ("res_out", "ln_out", "scattered"))
        dve_own, pool_own = per_stream("dve_own"), per_stream("pool_own")
        dve_step, pool_step = sem("dve_step"), sem("pool_step")
        counted, tables, table_in, tails = (sem(n) for n in ("counted", "tables", "table_in", "tails"))
        tok_in = [sem(f"tok_in{u}") for u in range(TU)]
        y_out = [sem(f"y_out{u}") for u in range(2)]
        FETCHES = 16 * (NT // TU)
        xt_mm, xt_ev, gu_mm, g_act, h_done = (sem(n) for n in ("xt_mm", "xt_ev", "gu_mm", "g_act", "h_done"))
        ht_mm, ht_ev, y_mm, y_ev, moving = (sem(n) for n in ("ht_mm", "ht_ev", "y_mm", "y_ev", "moving"))
        gu_ready = sem("gu_ready")
        gathered = [sem(f"gathered{u}") for u in range(2)]
        acc_step, summed, picked = (sem(n) for n in ("acc_step", "summed", "picked"))

        def at(it, b=B2 - 1, k=0, K=1):
            return (it * K + k) * B2 + b + 1 + B2

        def before(it, b, k=0, K=1):
            return (it * K + k) * B2 + b + 1

        def half_at(it, a, b, half):
            return ((it * 3 + a) * B2 + b) * 2 + half + 1 + 2 * B2

        def half_made(it, a, b, half):
            return half_at(it, a, b, half) - B2

        def ahead(eng, part):
            for st in range(2):
                for n in names[part].split():
                    eng.sem_inc(S[st][n], 2 * B2 if n in ("max", "exp") else B2)

        def plain(eng):
            eng.sem_inc(carried, 1)

        def opening(it):
            return isinstance(it, int) and it == 0

        def weave(one, other):
            i = j = 0
            while i < one[1] or j < other[1]:
                if j >= other[1] or (i < one[1] and i * other[1] <= j * one[1]):
                    next(one[0])
                    i += 1
                else:
                    next(other[0])
                    j += 1

        def turns(eng, layer0, layer1):
            def turn(it):
                weave((layer0(0, it), BEATS0), (layer1(1, it - 1), BEATS1))
                weave((layer1(0, it), BEATS1), (layer0(1, it), BEATS0))

            weave((layer0(0, 0), BEATS0), (iter(()), 0))
            weave((layer1(0, 0), BEATS1), (layer0(1, 0), BEATS0))
            turn(1)
            with eng.Fori(2, TURNS) as it:
                turn(it)
            weave((layer1(1, TURNS - 1), BEATS1), (iter(()), 0))

        def entry(n, most, engine):
            return nc.values_load(rows[0:1, bass.ds(n, 1)], engines=[engine], min_val=0, max_val=most,
                                  skip_runtime_bounds_check_because="the table is made with a minimum, and its first "
                                  "rows are those of tiles inside the regions")

        def zero_tails(eng, part):
            eng.wait_ge(tables, 1)
            with eng.Fori(0, E // 8) as n:
                for u in range(4):
                    e = part * (E // 2) + n * 4 + u
                    row = eng.value_load(tail_i[0:1, bass.ds(e, 1)], min_val=0, max_val=ROWS - P)
                    eng.dma_start(xs_d[bass.ds(row, P)], zeros[:, :]).then_inc(tails, 16)

        block = ctx.enter_context(nc.Block())
        bank8 = [wide[:, i // 2, i % 2, :, :].rearrange("p g c -> p (g c)") for i in range(4)] + \
                [bank[:, i, :] for i in range(4)]
        N_LOADS = 5

        @block.sync
        def _(sp):
            def load(st, turn):
                src = bass.ds(turn * G + st * B2, B2)
                dst = slice(st * B2, st * B2 + B2)
                sp.dma_start(x_in[:, dst, :], x_d[src].rearrange("s t f -> t s f")).then_inc(x_loaded[st], 16)
                sp.dma_start(ctx_in[:, dst, :], ctx_d[src].rearrange("s t f -> t s f")).then_inc(c_loaded[st], 16)

            def load_next(st, it):
                sp.wait_ge(S[st]["ln"], at(it, B2 - 1, 0, 6))
                plain(sp)
                sp.wait_ge(S[st]["xb"], at(it, B2 - 1, 0, 4))
                plain(sp)
                sp.wait_ge(S[st]["ctx_t"], at(it))
                plain(sp)
                load(st, it + 1)

            def store(st, it):
                dst = bass.ds(it * G + st * B2, B2)
                src = slice(st * B2, st * B2 + B2)
                sp.wait_ge(S[st]["res"], at(it, B2 - 1, 4, 5))
                plain(sp)
                sp.dma_start(res_d[dst].rearrange("s t f -> t s f"), x[:, src, :]).then_inc(res_out[st], 16)
                sp.wait_ge(S[st]["ln"], at(it, B2 - 1, 5, 6))
                plain(sp)
                sp.dma_start(ln_d[dst].rearrange("s t f -> t s f"), ln_r[:, src, :]).then_inc(ln_out[st], 16)

            sp.dma_start(consts[:, :], const_d).then_inc(loads, 16)
            load(0, 0)
            sp.dma_start(mask_i[:, :], mask_d).then_inc(loads, 16)
            sp.dma_start(w[:, :], weight_d).then_inc(loads, 16)
            sp.dma_start(biases[:, :], bias_d).then_inc(loads, 16)
            load(1, 0)
            sp.dma_start(s_down[:, :], sdown_d).then_inc(loads, 16)
            sp.wait_ge(setup_pe, 1)
            for e in range(E):
                sp.dma_start(xs_d[e * REGION + LAST:(e + 1) * REGION], zeros[:, :]).then_inc(cleared, 16)
            load_next(0, 0)
            load_next(1, 0)
            store(0, 0)
            with sp.Fori(1, TURNS - 1) as it:
                load_next(0, it)
                store(1, it - 1)
                load_next(1, it)
                store(0, it)
            store(1, TURNS - 2)
            store(0, TURNS - 1)
            store(1, TURNS - 1)

            zero_tails(sp, 0)
            sp.wait_ge(tables, 2)
            sp.dma_start(tab_d.rearrange("(c p) -> p c", p=P), rowi[:, :], allow_slow_non_contiguous=True
                         ).then_inc(table_in, 16)
            sp.wait_ge(table_in, 16)
            sp.dma_start(rows[:, :], tab_d.rearrange("(a n) -> a n", a=1)).then_inc(table_in, 16)
            sp.wait_ge(table_in, 32)
            sp.wait_ge(tails, 16 * E)

            for st in range(2):
                sp.wait_ge(scattered[st], 16 * B2 * TOPK * TURNS)
                sp.wait_ge(res_out[st], 16 * TURNS)
                sp.wait_ge(ln_out[st], 16 * TURNS)
            sp.dma_start(w_gu[:, :], wgu_d).then_inc(down_in, 16)
            sp.dma_start(w_down[:, :], wdown_d).then_inc(down_in, 16)

            def fetch(it):
                for u in range(TU):
                    row = entry(it * TU + u, ROWS - P, mybir.EngineType.SP)
                    if not opening(it):
                        sp.wait_ge(xt_mm, it * TU + u + 1 - TU)
                        plain(sp)
                    sp.dma_start(tok[:, u, :], xs_d[bass.ds(row, P)]).then_inc(tok_in[u], 16)

            fetch(0)
            with sp.Fori(1, NT // TU) as it:
                fetch(it)

            def rows_in(it, u):
                if not opening(it):
                    sp.wait_ge(xt_ev, NT + it * 2 + u - 1)
                    plain(sp)
                    sp.wait_ge(acc_step, ((it - 1) * 2 + u) * TOPK + 1)
                    plain(sp)
                sp.dma_start(own[:, u, :], ln_d[it * 2 + u]).then_inc(tok_in[u], 16)
                sp.dma_start(res[:, u, :], res_d[it * 2 + u]).then_inc(tok_in[2 + u], 16)

            def rows_out(it, u):
                sp.wait_ge(summed, it * 2 + u + 1)
                plain(sp)
                sp.dma_start(out_d[it * 2 + u], acc[:, u, :]).then_inc(tok_in[4 + u], 16)

            sp.wait_ge(xt_mm, NT)
            rows_in(0, 0)
            rows_in(0, 1)
            with sp.Fori(1, NSEQ // 2) as it:
                for u in range(2):
                    rows_in(it, u)
                    rows_out(it - 1, u)
            for u in range(2):
                rows_out(NSEQ // 2 - 1, u)
            for u in range(2):
                sp.wait_ge(tok_in[4 + u], FETCHES + 16 * (NSEQ // 2))

        @block.tensor
        def _(pe):
            ahead(pe, "pe")
            pe.wait_ge(setup, 1)
            pe.transpose(bank[0:SK, 0, 0:P // 2].bitcast(BF16), maskb[:, :], identb[:, :]).then_inc(mask_t, 1)
            pe.wait_ge(setup, 2)

            def turn(out, in_, n_in):
                return pe.transpose(out, in_, ident[0:n_in, 0:n_in])

            def norm_t(st, it, k, freed, src=ln):
                for b in range(B2):
                    q = st * B2 + b
                    pe.wait_ge(S[st]["ln"], at(it, b, k, 6))
                    pe.wait_ge(S[st][freed[0]], at(it, b, freed[1], freed[2]))
                    turn(bank[:, q, 0:P], src[:, q, :], P).then_inc(S[st]["lnt_mm"], 1)

            def through(st, it, k, weight, width, name):
                for b in range(B2):
                    q = st * B2 + b
                    pe.wait_ge(S[st]["ln_t"], at(it, b, k, 6))
                    pe.matmul(bank[:, q, 0:width], ln_t[:, q, :], weight, start=True, stop=True).then_inc(S[st][name], 1)

            def keys_t(st, it, k, sk, freed, n_freed):
                for b in range(B2):
                    q = st * B2 + b
                    pe.wait_ge(S[st]["klo"], at(it, b, k, 3))
                    pe.wait_ge(S[st][freed], n_freed(b))
                    for g in range(4):
                        mm = turn(bank[:, q, g * sk:(g + 1) * sk],
                                  kpad[0:sk, q, 4 * g:4 * g + 4, :].rearrange("p h c -> p (h c)"), sk)
                    mm.then_inc(S[st]["kt_mm"], 1)

            def queries_t(st, it, ready, n_ready, free, n_free):
                for b in range(B2):
                    q = st * B2 + b
                    pe.wait_ge(S[st][ready], n_ready(b))
                    pe.wait_ge(S[st][free], n_free(b))
                    for g in range(4):
                        mm = turn(bank[:, q, g * P:(g + 1) * P],
                                  qpad[:, q, 4 * g:4 * g + 4, :].rearrange("p h c -> p (h c)"), P)
                    mm.then_inc(S[st]["qt_mm"], 1)

            def attention(st, it, a, keys, sk, mask, mask_turned):
                sems = S[st]
                for b in range(B2):
                    q = st * B2 + b
                    for half in range(2):
                        if not half:
                            pe.wait_ge(sems["qt"], at(it, b, 2 * a, 6))
                        if b or half:
                            pe.wait_ge(sems["max"], half_at(it, a, b, half) - 1)
                        else:
                            pe.wait_ge(sems["exp"], half_at(it, a, 0, 0) - 1)
                        for c in range(2):
                            if mask is not None:
                                pe.matmul(wide[:, st, c, :, 0:sk], identb[:, :], mask, start=True, stop=False,
                                          skip_group_check=True)
                        for g in range(4):
                            for c in range(2):
                                mm = pe.matmul(wide[:, st, c, g, 0:sk], qt[:, q, g, 2 * half + c, :],
                                               keys[:, q, g, 0:sk], start=mask is None, stop=True,
                                               skip_group_check=True)
                        mm.then_inc(sems["sc_mm"], 1)
                        yield
                queries_t(st, it, "max", lambda b: half_at(it, a, b, 1), "qt", lambda b: at(it, b, 2 * a, 6))
                yield
                for b in range(B2):
                    q = st * B2 + b
                    for half in range(2):
                        if not half:
                            pe.wait_ge(sems["qt"], at(it, b, 2 * a + 1, 6))
                        if b or half:
                            pe.wait_ge(sems["exp"], half_at(it, a, b, half) - 1)
                        else:
                            pe.wait_ge(sems["max"], half_at(it, a, 1, 1))
                        for c in range(2):
                            if mask_turned is not None:
                                pe.matmul(wide[0:sk, st, c, :, :], identb[0:sk, 0:sk], mask_turned, start=True,
                                          stop=False, skip_group_check=True)
                        for c in range(2):
                            mm = pe.matmul(wide[0:sk, st, c, :, :], keys[:, q, 2 * half + c, 0:sk],
                                           qt[:, q, 2 * half + c, :, :], start=mask_turned is None, stop=True,
                                           skip_group_check=True)
                        mm.then_inc(sems["st_mm"], 1)
                        yield
                    pe.wait_ge(sems["values"], at(it, b, a, 3))
                    for g in range(4):
                        if g % 2 == 0:
                            pe.wait_ge(sems["exp"], half_at(it, a, b, g // 2))
                        for j in range(4):
                            at_head = VW * (4 * g + j) + (3 - j) * DH
                            mm = pe.matmul(bank[0:2 * 4 * DH, q, g * P:(g + 1) * P],
                                           v_pad[0:sk, q, at_head:at_head + 2 * 4 * DH], pt[0:sk, st, 4 * g + j, :],
                                           start=j == 0, stop=j == 3)
                    mm.then_inc(sems["pv"], 1)
                    yield

            def project(st, it, k, weight):
                if k == 2:
                    for b in range(B2):
                        q = st * B2 + b
                        pe.wait_ge(S[st]["o"], at(it, b, k, 4))
                        turn(bank[:, q, 0:P], o[:, q, :], P).then_inc(S[st]["ot_mm"], 1)
                    yield
                for b in range(B2):
                    q = st * B2 + b
                    if k == 2:
                        pe.wait_ge(S[st]["o_t"], at(it, b))
                    else:
                        pe.wait_ge(S[st]["o"], at(it, b, k, 4))
                    pe.matmul(bank[:, q, 0:P], o_t[:, q, :], weight, start=True, stop=True).then_inc(S[st]["proj"], 1)
                yield

            def layer0(st, it):
                sems = S[st]
                if not opening(it):
                    pe.wait_ge(routed[st], 3 * it - 1)
                for b in range(B2):
                    q = st * B2 + b
                    pe.wait_ge(c_loaded[st], 16 * it + 16)
                    turn(bank[:, q, 0:SK], ctx_in[:, q, :], SK).then_inc(sems["ctx_mm0"], 1)
                yield
                for b in range(B2):
                    q = st * B2 + b
                    pe.wait_ge(sems["ctx_t"], at(it, b))
                    pe.matmul(bank[0:SK, q, :], ctx_t[:, q, :], wt("ctx"), start=True, stop=True
                              ).then_inc(sems["ctx_mm"], 1)
                yield
                yield
                norm_t(st, it, 0, ("ckv", 0, 1))
                yield
                through(st, it, 0, wt("qkv0"), 3 * P, "qkv_mm")
                yield
                keys_t(st, it, 0, SK, "qkv", lambda b: at(it, b, 0, 3))
                yield
                yield
                keys_t(st, it, 1, SK, "kt", lambda b: at(it, b, 0, 3))
                yield
                yield
                keys_t(st, it, 2, P, "kt", lambda b: at(it, b, 1, 3))
                yield
                queries_t(st, it, "qlo", lambda b: at(it, b, 0, 3), "kt", lambda b: at(it, b, 2, 3))
                yield
                yield from attention(st, it, 0, kt, P, causal4[:, :, :], causal4_t[:, :, :])
                yield from project(st, it, 0, wt("o0"))
                yield
                yield
                norm_t(st, it, 1, ("res", 0, 5))
                yield
                through(st, it, 1, wt("q_x0"), P, "qkv_mm")
                yield
                yield
                queries_t(st, it, "qlo", lambda b: at(it, b, 1, 3), "qkv", lambda b: at(it, b, 1, 3))
                yield
                yield from attention(st, it, 1, kt_x[0], SK, mask4[:, :, :], mask4_t[:, :, :])
                yield from project(st, it, 1, wt("o_x0"))
                yield
                yield
                norm_t(st, it, 2, ("res", 1, 5))
                yield
                through(st, it, 2, sign_w[:, :], P, "proj")
                yield

            def layer1(st, it):
                sems = S[st]
                yield
                yield
                norm_t(st, it, 3, ("res", 2, 5))
                yield
                through(st, it, 3, wt("qkv_f"), 3 * P, "qkv_mm")
                yield
                for b in range(B2):
                    q = st * B2 + b
                    pe.wait_ge(sems["fqkv"], at(it, b))
                    for i in range(2):
                        mm = turn(bank[:, q, i * P:(i + 1) * P], qkv[:, q, i * P:(i + 1) * P], P)
                    mm.then_inc(sems["fqkt_mm"], 1)
                yield
                for i in range(2):
                    for b in range(B2):
                        q = st * B2 + b
                        if i:
                            pe.wait_ge(sems["fsub"], at(it, b, 0, 2))
                        else:
                            pe.wait_ge(sems["fqk_t"], at(it, b))
                        pe.matmul(bank[:, q, :], fqk_t[:, q, i * P:(i + 1) * P], wt("proj_f"), start=True, stop=True
                                  ).then_inc(sems["xw"], 1)
                    yield
                yield
                for b in range(B2):
                    q = st * B2 + b
                    pe.wait_ge(sems["fphi"], at(it, b, 0, 2))
                    pe.wait_ge(sems["fsub"], at(it, b, 1, 2))
                    for g in range(4):
                        mm = turn(bank[:, q, g * P:(g + 1) * P], phi[:, q, 0, g * P:(g + 1) * P], P)
                    mm.then_inc(sems["pqt_mm"], 1)
                yield
                for b in range(B2):
                    q = st * B2 + b
                    pe.wait_ge(sems["fphi"], at(it, b, 1, 2))
                    pe.wait_ge(sems["pq_t"], at(it, b))
                    for g in range(4):
                        mm = pe.matmul(bank[:, q, g * 4 * DA:(g + 1) * 4 * DA], phi[:, q, 1, g * P:(g + 1) * P],
                                       v[:, q, 4 * g:4 * g + 4, :].rearrange("p h c -> p (h c)"), start=True, stop=True)
                    mm.then_inc(sems["kv_mm"], 1)
                yield
                for b in range(B2):
                    q = st * B2 + b
                    pe.wait_ge(sems["kvb"], at(it, b))
                    for g in range(4):
                        mm = pe.matmul(bank[:, q, g * 4 * DA:(g + 1) * 4 * DA], pq_t[:, q, g * P:(g + 1) * P],
                                       kvb[:, q, g * 4 * DA:(g + 1) * 4 * DA], start=True, stop=True)
                    mm.then_inc(sems["num_mm"], 1)
                yield
                yield from project(st, it, 2, wt("o_f"))
                yield
                yield
                norm_t(st, it, 4, ("res", 3, 5))
                yield
                through(st, it, 4, wt("q_x1"), P, "qkv_mm")
                yield
                yield
                queries_t(st, it, "qlo", lambda b: at(it, b, 2, 3), "qkv", lambda b: at(it, b, 2, 3))
                yield
                yield from attention(st, it, 2, kt_x[1], SK, None, None)
                yield from project(st, it, 3, wt("o_x1"))
                yield
                yield
                norm_t(st, it, 5, ("res", 4, 5), ln_r)
                yield
                for b in range(B2):
                    pe.wait_ge(sems["ln_t"], at(it, b, 5, 6))
                    mm = pe.matmul(bank[:, st * B2, b * E:(b + 1) * E], ln_t[:, st * B2 + b, :], wt("gate"), start=True,
                                   stop=True)
                mm.then_inc(route_mm[st], 1)
                yield
                yield
                yield
                yield
                pe.wait_ge(routed[st], 3 * it + 1)
                ranks = bank[:, st * B2 + 1, 0:B2 * E]
                pe.matmul(ranks.rearrange("p (b e) -> p b e", b=B2), onesb[:, :],
                          totalb[:, :].rearrange("p (a e) -> p a e", a=1).to_broadcast((P, B2, E)), start=True,
                          stop=False, skip_group_check=True)
                for b in range(B2):
                    pe.matmul(ranks[:, b * E:(b + 1) * E], upperb[:, :], chosenb[:, st * B2 + b, :], start=False,
                              stop=False, skip_group_check=True)
                pe.matmul(ranks[:, E:2 * E], onesb[:, :], chosenb[:, st * B2, :], start=False, stop=True,
                          skip_group_check=True).then_inc(route_mm[st], 1)
                yield

            turns(pe, layer0, layer1)

            for st in range(2):
                pe.wait_ge(routed[st], 3 * TURNS)
            pe.matmul(bank[:, 0, 0:E], onesb[:, :], totalb[:, :], start=True, stop=True).then_inc(counted, 1)
            pe.wait_ge(table_in, 32)

            def experts_turn(it, first, last):
                for u in range(TU):
                    t = it * TU + u
                    if not last:
                        pe.wait_ge(tok_in[u], 16 * it + 16)
                        if not (first and u < 2):
                            pe.wait_ge(xt_ev, t - 1)
                        turn(bank8[u % 2][:, 0:P], tok[:, u, :], P).then_inc(xt_mm, 1)
                    if not (first and u < 2) and not (last and u >= 2):
                        pe.wait_ge(xt_ev, t - 1)
                        pe.wait_ge(gu_ready, t - 1)
                        if not (first and u < 4):
                            pe.wait_ge(h_done, t - 3)
                        for c in range(2):
                            mm = pe.matmul(bank8[2 + u % 2][0:I, c * P:(c + 1) * P],
                                           gu_of[:, (u - 2) % 4, c * I:(c + 1) * I], tok_t[:, (u - 2) % 4, :],
                                           start=True, stop=True)
                        mm.then_inc(gu_mm, 1)
                    if not (first and u < 4) and not (last and u >= 4):
                        pe.wait_ge(h_done, t - 3)
                        if not (first and u < 6):
                            pe.wait_ge(y_ev, t - 5)
                        pe.matmul(bank8[6 + u % 2][:, 0:P], hid_t[:, u % 4, :], down_of[:, u % 4, :], start=True,
                                  stop=True).then_inc(y_mm, 1)

            experts_turn(0, True, False)
            with pe.Fori(1, NT // TU) as it:
                experts_turn(it, False, False)
            experts_turn(NT // TU, False, True)

            pe.wait_ge(y_ev, NT)

            def shared_turn(it):
                for u in range(2):
                    pe.wait_ge(tok_in[u], FETCHES + 16 * it + 16)
                    if not opening(it):
                        pe.wait_ge(ht_ev, it * 2 + u - 1)
                    turn(bank8[u][:, 0:P], own[:, u, :], P).then_inc(xt_mm, 1)
                for u in range(2):
                    pe.wait_ge(xt_ev, NT + it * 2 + u + 1)
                    pe.matmul(bank8[2 + u][:, 0:4 * I], own_t[:, u, :], wt("shared_gu"), start=True, stop=True
                              ).then_inc(gu_mm, 1)
                for u in range(2):
                    pe.wait_ge(h_done, NT + it * 2 + u + 1)
                    for c in range(2):
                        mm = turn(bank8[u][0:I, (1 + c) * P:(2 + c) * P], s_hid[:, u, c * I:(c + 1) * I], P)
                    mm.then_inc(ht_mm, 1)
                for u in range(2):
                    pe.wait_ge(ht_ev, it * 2 + u + 1)
                    if not opening(it):
                        pe.wait_ge(acc_step, ((it - 1) * 2 + u) * TOPK + 1)
                    for c in range(2):
                        mm = pe.matmul(bank8[4 + u][:, 0:P], s_hid_t[:, u, c * P:(c + 1) * P],
                                       s_down[:, c * P:(c + 1) * P], start=c == 0, stop=c == 1)
                    mm.then_inc(y_mm, 1)

            shared_turn(0)
            with pe.Fori(1, NSEQ // 2) as it:
                shared_turn(it)

        @block.scalar
        def _(act):
            ahead(act, "act")
            nc.scalar.preload_act_table_set("natural_log_exp_and_others")
            act.wait_ge(setup, 2)

            def rstd_of(st, it, k):
                two = slice(st * B2, st * B2 + B2)
                act.wait_ge(S[st]["mv"], at(it, B2 - 1, k, 6))
                nc.scalar.activation(lnv[:, two], mv[:, two, 1], ACT.Ln, bias=eps[:, 0:1]).then_inc(lnv_done[st], 1)
                act.wait_ge(lnv_done[st], it * 6 + k + 1)
                nc.scalar.activation(rstd[:, two], lnv[:, two], ACT.Exp, scale=-0.5).then_inc(rstd_done[st], 1)

            def copies(st, made, n_made, name, out, in_):
                for b in range(B2):
                    act.wait_ge(S[st][made], n_made(b))
                    nc.scalar.copy(out(st * B2 + b), in_(st * B2 + b)).then_inc(S[st][name], 1)

            def norm_t(st, it, k):
                copies(st, "lnt_mm", lambda b: at(it, b, k, 6), "ln_t", lambda q: ln_t[:, q, :], lambda q: bank[:, q, 0:P])

            def keys_t(st, it, k, out, sk):
                copies(st, "kt_mm", lambda b: at(it, b, k, 3), "kt", lambda q: out[:, q, :, :],
                       lambda q: bank[:, q, 0:4 * sk].rearrange("p (g c) -> p g c", g=4))

            def queries_t(st, it, k):
                for b in range(B2):
                    q = st * B2 + b
                    act.wait_ge(S[st]["qt_mm"], at(it, b, k, 6))
                    for j in range(4):
                        rows_j = slice(j * PAD, (j + 1) * PAD)
                        ins = nc.scalar.copy(qt[rows_j, q, :, j, :],
                                             bank[rows_j, q, :].rearrange("p (g c) -> p g c", g=4))
                    ins.then_inc(S[st]["qt"], 1)

            def high_parts(dst, src, sk, step):
                out = dst[0:sk, :, 0:2 * step].rearrange("p h (c e) -> p h c e", c=2)[:, :, :, 0:DH].bitcast(F32R)
                heads = src.rearrange("p (h a c) -> p h a c", h=H, a=1)
                return nc.scalar.copy(out, heads.to_broadcast((sk, H, 2, DH)))

            def attention(st, it, a, sk):
                for _ in range(4):
                    yield
                queries_t(st, it, 2 * a + 1)
                yield
                for b in range(B2):
                    for half in range(2):
                        act.wait_ge(S[st]["st_mm"], half_made(it, a, b, half))
                        if not half:
                            act.wait_ge(S[st]["pv"], at(it, b, a, 3) - 1)
                        nc.scalar.activation(pt[0:sk, st, 8 * half:8 * half + 8, :],
                                             wide[0:sk, st, :, :, :].rearrange("p j g c -> p (j g) c"), ACT.Exp
                                             ).then_inc(S[st]["exp"], 1)
                        yield
                    q = st * B2 + b
                    act.wait_ge(S[st]["pv"], at(it, b, a, 3))
                    act.wait_ge(S[st]["o"], before(it, b, {0: 0, 1: 1, 2: 3}[a], 4) + 1)
                    for g in range(4):
                        ins = nc.scalar.copy(den_t[4 * DH * g:4 * DH * (g + 1), st, :],
                                             bank[4 * DH:8 * DH, q, g * P:(g + 1) * P])
                    ins.then_inc(S[st]["den"], 1)
                    yield

            def project(st, it, k):
                if k == 2:
                    copies(st, "ot_mm", lambda b: at(it, b), "o_t", lambda q: o_t[:, q, :], lambda q: bank[:, q, 0:P])
                    yield
                yield

            def norm(st, it, k):
                rstd_of(st, it, k)
                yield
                yield
                norm_t(st, it, k)
                yield

            def cross_queries(st, it, k):
                yield
                for b in range(B2):
                    act.wait_ge(S[st]["qkv"], at(it, b, k, 3))
                    high_parts(qpad[:, st * B2 + b, :, :], qkv[:, st * B2 + b, 0:P], P, 16).then_inc(S[st]["qhi"], 1)
                yield
                queries_t(st, it, 2 * k)
                yield

            def layer0(st, it):
                copies(st, "ctx_mm0", lambda b: at(it, b), "ctx_t", lambda q: ctx_t[:, q, :], lambda q: bank[:, q, 0:SK])
                yield
                rstd_of(st, it, 0)
                yield
                for b in range(B2):
                    act.wait_ge(S[st]["ckv"], at(it, b))
                    high_parts(kpad[:, st * B2 + b, :, :], ckv[:, st * B2 + b, 0, :], SK, DH).then_inc(S[st]["khi"], 1)
                yield
                norm_t(st, it, 0)
                yield
                yield
                keys_t(st, it, 0, kt_x[0], SK)
                yield
                for b in range(B2):
                    high_parts(kpad[:, st * B2 + b, :, :], ckv[:, st * B2 + b, 2, :], SK, DH).then_inc(S[st]["khi"], 1)
                yield
                keys_t(st, it, 1, kt_x[1], SK)
                yield
                for b in range(B2):
                    q = st * B2 + b
                    act.wait_ge(S[st]["rope"], at(it, b))
                    high_parts(kpad[:, q, :, :], qkv[:, q, P:2 * P], P, DH).then_inc(S[st]["khi"], 1)
                    high_parts(qpad[:, q, :, :], qkv[:, q, 0:P], P, 16).then_inc(S[st]["qhi"], 1)
                yield
                keys_t(st, it, 2, kt, P)
                yield
                queries_t(st, it, 0)
                yield
                yield from attention(st, it, 0, P)
                yield from project(st, it, 0)
                yield from norm(st, it, 1)
                yield from cross_queries(st, it, 1)
                yield from attention(st, it, 1, SK)
                yield from project(st, it, 1)
                yield from norm(st, it, 2)
                yield

            def layer1(st, it):
                yield from norm(st, it, 3)
                for b in range(B2):
                    q = st * B2 + b
                    act.wait_ge(S[st]["qkv_mm"], at(it, b, 2, 4))
                    nc.scalar.mul(qkv[:, q, 0:2 * P], bank[:, q, 0:2 * P], SCALE)
                    nc.scalar.copy(v[:, q, :, 0:DH], bank[:, q, 2 * P:3 * P].rearrange("p (h c) -> p h c", h=H)
                                   ).then_inc(S[st]["fqkv"], 1)
                yield
                copies(st, "fqkt_mm", lambda b: at(it, b), "fqk_t", lambda q: fqk_t[:, q, :],
                       lambda q: bank[:, q, 0:2 * P])
                yield
                yield
                for i in range(2):
                    for b in range(B2):
                        q = st * B2 + b
                        act.wait_ge(S[st]["fsub"], at(it, b, i, 2))
                        nc.scalar.activation(phi[:, q, i, :], phi[:, q, i, :], ACT.Exp).then_inc(S[st]["fexp"], 1)
                    yield
                copies(st, "pqt_mm", lambda b: at(it, b), "pq_t", lambda q: pq_t[:, q, :], lambda q: bank[:, q, :])
                yield
                yield
                yield
                yield from project(st, it, 2)
                yield from norm(st, it, 4)
                yield from cross_queries(st, it, 2)
                yield from attention(st, it, 2, SK)
                yield from project(st, it, 3)
                yield from norm(st, it, 5)
                act.wait_ge(route_mm[st], 2 * it + 1)
                nc.scalar.activation(sc[:, st * B2:st * B2 + B2, :],
                                     bank[:, st * B2, 0:B2 * E].rearrange("p (b e) -> p b e", b=B2), ACT.Exp,
                                     scale=-1.0).then_inc(gate_exp[st], 1)
                for _ in range(5):
                    yield

            turns(act, layer0, layer1)
            zero_tails(act, 1)
            act.wait_ge(table_in, 32)

            def experts_turn(it, first, last):
                for u in range(TU):
                    t = it * TU + u
                    if not last:
                        act.wait_ge(xt_mm, t + 1)
                        nc.scalar.copy(tok_t[:, u % 4, :], bank8[u % 2][:, 0:P]).then_inc(xt_ev, 1)
                    if not (first and u < 2) and not (last and u >= 2):
                        act.wait_ge(gu_mm, t - 1)
                        if not (first and u < 6):
                            act.wait_ge(h_done, t - 5)
                        nc.scalar.activation(act_g[:, (u - 2) % 4, :], bank8[2 + u % 2][0:I, 0:P], ACT.Silu
                                             ).then_inc(g_act, 1)
                    if not (first and u < 4) and not (last and u >= 4):
                        act.wait_ge(y_mm, t - 3)
                        lane = (u - 4) % TU
                        if lane == 0 and not first:
                            act.wait_ge(y_out[0], 16 * it)
                        if lane == 4 and not opening(it - 1):
                            act.wait_ge(y_out[1], 16 * (it - 1))
                        nc.scalar.copy(y[:, lane, :], bank8[6 + u % 2][:, 0:P]).then_inc(y_ev, 1)

            experts_turn(0, True, False)
            experts_turn(1, False, False)
            with act.Fori(2, NT // TU) as it:
                experts_turn(it, False, False)
            experts_turn(NT // TU, False, True)

            def shared_turn(it):
                for u in range(2):
                    act.wait_ge(xt_mm, NT + it * 2 + u + 1)
                    nc.scalar.copy(own_t[:, u, :], bank8[u][:, 0:P]).then_inc(xt_ev, 1)
                for u in range(2):
                    act.wait_ge(gu_mm, NT + it * 2 + u + 1)
                    nc.scalar.activation(s_act[:, u, :], bank8[2 + u][:, 0:2 * I], ACT.Silu).then_inc(g_act, 1)
                for u in range(2):
                    act.wait_ge(ht_mm, it * 2 + u + 1)
                    nc.scalar.copy(s_hid_t[:, u, :], bank8[u][0:I, P:3 * P]).then_inc(ht_ev, 1)

            shared_turn(0)
            with act.Fori(1, NSEQ // 2) as it:
                shared_turn(it)

        @block.gpsimd
        def _(pool):
            ahead(pool, "pool")
            for t in [qpad, kpad]:
                nc.gpsimd.memset(t[:, :, :, :], 0.0)
            for q in range(G):
                nc.gpsimd.memset(qt[:, q, :, :, :].rearrange("p g j c -> p (g j c)").bitcast(F32), 0.0)
            nc.gpsimd.memset(v_pad[:, :, :], 0.0)
            nc.gpsimd.memset(zeros[:, :], 0.0)
            nc.gpsimd.memset(onesb[:, :], 1.0)
            nc.gpsimd.memset(totalb[:, :], 0.0)
            nc.gpsimd.memset(total[:, :], 0.0)
            nc.gpsimd.memset(ones_e[:, :], 1.0)
            nc.gpsimd.memset(idx_all[:, :], 0)
            nc.gpsimd.memset(eps[:, :], LN_EPS).then_inc(pool_step, 1)
            pool.wait_ge(pool_step, 1)
            nc.gpsimd.memset(kpad[:, :, :, 3 * DH:3 * DH + 1], 1.0)
            for q in range(G):
                heads = v_pad[:, q, 0:H * VW].rearrange("p (h c) -> p h c", c=VW)
                nc.gpsimd.memset(heads[:, :, VW - DH:VW], 1.0)
            nc.gpsimd.memset(v[:, :, :, DH:DH + 1], 1.0).then_inc(setup_pe, 1)
            pool.wait_ge(setup, 2)
            pool.wait_ge(loads, 16 * N_LOADS)
            ROPE = 2

            def with_bias(st, it, k, name, src):
                for b in range(B2):
                    q = st * B2 + b
                    if k:
                        pool.wait_ge(S[st]["res"], at(it, b, {1: 0, 2: 2, 3: 3}[k], 5))
                    else:
                        pool.wait_ge(S[st]["res"], before(it, b, 0, 5))
                        pool.wait_ge(x_loaded[st], 16 * it + 16)
                    nc.gpsimd.tensor_tensor(xb[:, q, :], src[:, q, :], bias(name), ALU.add).then_inc(S[st]["xb"], 1)

            def low_part(dst, src, sk, place):
                return nc.gpsimd.tensor_tensor(dst[0:sk, :, place:place + DH].bitcast(F32R),
                                               src.rearrange("p (h c) -> p h c", h=H), dst[0:sk, :, 0:DH], ALU.subtract)

            def values_x(st, it, i):
                for b in range(B2):
                    q = st * B2 + b
                    pool.wait_ge(S[st]["ckv"], at(it, b))
                    plain(pool)
                    nc.gpsimd.tensor_copy(v_x[i][:, q, :], ckv[:, q, 2 * i + 1, :])

            def values(st, it, a, b, src, sk):
                q = st * B2 + b
                pool.wait_ge(S[st]["pv"], before(it, b, a, 3))
                plain(pool)
                heads = v_pad[0:sk, q, 0:H * VW].rearrange("p (h c) -> p h c", c=VW)
                nc.gpsimd.tensor_copy(heads[:, :, 3 * DH:4 * DH], src.rearrange("p (h c) -> p h c", h=H)
                                      ).then_inc(S[st]["values"], 1)

            def keys_low(st, it, i):
                for b in range(B2):
                    q = st * B2 + b
                    pool.wait_ge(S[st]["khi"], at(it, b, i, 3))
                    low_part(kpad[:, q, :, :], ckv[:, q, 2 * i, :], SK, 2 * DH).then_inc(S[st]["klo"], 1)

            def send(st, turn, n):
                q, j = st * B2 + n // TOPK, n % TOPK
                if n == 0:
                    pool.wait_ge(routed[st], 3 * turn + 3)
                    plain(pool)
                    if isinstance(turn, int) and turn == 0:
                        pool.wait_ge(cleared, 16 * E)
                nc.gpsimd.indirect_dma_start(
                    out=xs_d, out_offset=bass.IndirectOffsetOnAxis(ap=idx[:, q, j:j + 1], axis=0),
                    in_=ln_r[:, q, :], in_offset=None).then_inc(scattered[st], 16)

            def attention(st, it, sends, start=0):
                for step in range(11):
                    if step >= start and sends and sends[0] < B2 * TOPK:
                        send(st, it - 1, sends[0])
                        sends[0] += 1
                    yield

            def norm(st, it, k=None, name=None):
                yield
                if k:
                    with_bias(st, it, k, name, x)
                yield
                yield

            def cross_queries(st, it, k):
                yield
                for b in range(B2):
                    q = st * B2 + b
                    pool.wait_ge(S[st]["qhi"], at(it, b, k, 3))
                    low_part(qpad[:, q, :, :], qkv[:, q, 0:P], P, DH)
                    nc.gpsimd.memset(qpad[:, q, :, 3 * DH:3 * DH + 1], 0.0).then_inc(S[st]["qlo"], 1)
                yield
                for b in range(B2):
                    values(st, it, k, b, v_x[k - 1][:, st * B2 + b, :], SK)
                yield

            def layer0(st, it):
                sends = None if opening(it) else [0]
                with_bias(st, it, 0, "o0", x_in)
                yield
                yield
                values_x(st, it, 0)
                yield
                keys_low(st, it, 0)
                yield
                yield
                for b in range(B2):
                    q = st * B2 + b
                    own = it * (B2 * ROPE) + b * ROPE
                    pool.wait_ge(S[st]["qkv"], at(it, b, 0, 3))
                    qk = qkv[:, q, 0:2 * P].rearrange("p (n c) -> p n c", c=2)
                    sin = const("rope_s").rearrange("p (n c) -> p n c", c=2)
                    crossed = rot[:, 1, :].rearrange("p (n c) -> p n c", c=2)
                    nc.gpsimd.tensor_tensor(rot[:, 0, :], qkv[:, q, 0:2 * P], const("rope_c"), ALU.mult)
                    nc.gpsimd.tensor_tensor(crossed[:, :, 0], qk[:, :, 1], sin[:, :, 0], ALU.mult
                                            ).then_inc(pool_own[st], 1)
                    nc.gpsimd.tensor_tensor(crossed[:, :, 1], qk[:, :, 0], sin[:, :, 1], ALU.mult
                                            ).then_inc(pool_own[st], 1)
                    values(st, it, 0, b, qkv[:, q, 2 * P:3 * P], P)
                    pool.wait_ge(pool_own[st], own + ROPE)
                    nc.gpsimd.tensor_tensor(qkv[:, q, 0:2 * P], rot[:, 0, :], rot[:, 1, :], ALU.add
                                            ).then_inc(S[st]["rope"], 1)
                    pool.wait_ge(S[st]["rope"], at(it, b))
                yield
                values_x(st, it, 1)
                keys_low(st, it, 1)
                yield
                yield
                for b in range(B2):
                    q = st * B2 + b
                    pool.wait_ge(S[st]["khi"], at(it, b, 2, 3))
                    low_part(kpad[:, q, :, :], qkv[:, q, P:2 * P], P, 2 * DH).then_inc(S[st]["klo"], 1)
                    pool.wait_ge(S[st]["qhi"], at(it, b, 0, 3))
                    low_part(qpad[:, q, :, :], qkv[:, q, 0:P], P, DH)
                    nc.gpsimd.memset(qpad[:, q, :, 3 * DH:3 * DH + 1], 0.0).then_inc(S[st]["qlo"], 1)
                yield
                yield
                yield
                yield from attention(st, it, sends, 6)
                yield
                yield from norm(st, it, 1, "o_x0")
                yield from cross_queries(st, it, 1)
                yield from attention(st, it, sends)
                yield
                yield from norm(st, it)
                yield

            def layer1(st, it):
                yield from norm(st, it, 2, "o_f")
                yield
                for b in range(B2):
                    q = st * B2 + b
                    pool.wait_ge(S[st]["fqkv"], at(it, b))
                    nc.gpsimd.tensor_tensor(sq[:, q, :], qkv[:, q, 0:2 * P], qkv[:, q, 0:2 * P], ALU.mult
                                            ).then_inc(S[st]["sq"], 1)
                for _ in range(9):
                    yield
                yield from norm(st, it, 3, "o_x1")
                yield from cross_queries(st, it, 2)
                yield from attention(st, it, None)
                for _ in range(9):
                    yield

            turns(pool, layer0, layer1)
            for st in range(2):
                for n in range(B2 * TOPK):
                    send(st, TURNS - 1, n)

            def store_tiles(it, half):
                pool.wait_ge(y_ev, it * TU + 4 * half + 4)
                nc.gpsimd.dma_start(ys_d[bass.ds(it * TU + 4 * half, 4)].rearrange("t p f -> p t f"),
                                    y[:, 4 * half:4 * half + 4, :]).then_inc(y_out[half], 16)

            def weights_turn(it):
                for u in range(TU):
                    t = it * TU + u
                    e = entry(t + TCOLS * P, E - 1, mybir.EngineType.Pool)
                    if not (opening(it) and u < 4):
                        pool.wait_ge(gu_mm, t - 3)
                        plain(pool)
                    nc.gpsimd.tensor_copy(gu_of[:, u % 4, :], w_gu[:, bass.ds(e * (2 * I), 2 * I)]
                                          ).then_inc(gu_ready, 1)
                    if not opening(it) and u in (1, 5):
                        store_tiles(it - 1, u // 4)

            pool.wait_ge(table_in, 32)
            pool.wait_ge(down_in, 32)
            weights_turn(0)
            with pool.Fori(1, NT // TU) as it:
                weights_turn(it)
            for half in range(2):
                store_tiles(NT // TU - 1, half)
            y_rows = ys_d.rearrange("t p f -> (t p) f")
            pool.wait_ge(moving, 5 * (NT // TU))
            for u in range(2):
                pool.wait_ge(y_out[u], 16 * (NT // TU))

            def gather(it):
                for u in range(2):
                    if not opening(it):
                        pool.wait_ge(summed, it * 2 + u - 1)
                        plain(pool)
                    nc.gpsimd.tensor_copy(idx_f[:, u, :], row_all[:, bass.ds(it * 16 + u * 8, 8)]).then_inc(picked, 1)
                    pool.wait_ge(picked, it * 2 + u + 1)
                    plain(pool)
                    for j in range(TOPK):
                        nc.gpsimd.indirect_dma_start(
                            out=got[:, u, j, :], out_offset=None, in_=y_rows,
                            in_offset=bass.IndirectOffsetOnAxis(ap=idx_f[:, u, j:j + 1], axis=0)
                        ).then_inc(gathered[u], 16)

            gather(0)
            with pool.Fori(1, NSEQ // 2) as it:
                gather(it)

        @block.vector
        def _(dve):
            ahead(dve, "dve")
            OWN_START = 2048
            dve.sem_inc(dve_own[1], OWN_START)
            dve.wait_ge(loads, 16 * N_LOADS)
            dve.wait_ge(setup_pe, 1)
            nc.vector.tensor_copy(identb[:, :], ident)
            nc.vector.tensor_copy(upperb[:, :], const("upper"))
            for j in range(4):
                nc.vector.tensor_copy(causal4[:, j, :], const("causal"))
                nc.vector.tensor_copy(causal4_t[:, j, :], const("causal_t"))
            nc.vector.tensor_scalar(sign_a[:, :], wt("ffn"), 0.0, None, ALU.is_gt)
            nc.vector.tensor_scalar(sign_w[:, :], wt("ffn"), 0.0, None, ALU.is_lt)
            nc.vector.tensor_scalar(maskb[:, :], mask_i[:, :], 0, -1.0e9, ALU.is_equal, ALU.mult)
            nc.vector.tensor_scalar(seen[:, :], mask_i[:, :], 0, None, ALU.not_equal).then_inc(setup, 1)
            dve.wait_ge(setup, 1)
            nc.vector.tensor_tensor(sign_w[:, :], sign_a[:, :], sign_w[:, :], ALU.subtract)
            for j in range(4):
                nc.vector.tensor_copy(mask4[:, j, :], maskb[:, :])
            nc.vector.tensor_reduce(q_scale[:, :], seen[:, :], AX, ALU.max).then_inc(dve_step, 1)
            dve.wait_ge(dve_step, 1)
            nc.vector.tensor_scalar(q_scale[:, :], q_scale[:, :], SCALE, None, ALU.mult)
            nc.vector.tensor_scalar(q_bias1[:, :], bias("q_x1"), SCALE, None, ALU.mult).then_inc(dve_step, 1)
            dve.wait_ge(dve_step, 2)
            nc.vector.tensor_scalar(q_bias0[:, :], bias("q_x0"), q_scale[:, 0:1], None, ALU.mult)
            dve.wait_ge(mask_t, 1)
            for j in range(4):
                cp = nc.vector.tensor_copy(mask4_t[:, j, :], bank[0:SK, 0, 0:P // 2].bitcast(BF16))
            cp.then_inc(setup, 1)
            dve.wait_ge(setup, 2)

            class Chain:

                def __init__(self, st, it, start):
                    self.sem, self.n = dve_own[st], 0
                    self.base = it * (STEPS0 + STEPS_P + STEPS1) + start + st * OWN_START

                def __call__(self, ins, alone=False):
                    self.n += 1
                    ins.then_inc(self.sem, 1)
                    dve.wait_ge(self.sem, self.base + self.n)
                    if alone:
                        plain(dve)

                def note(self, ins):
                    self.n += 1
                    ins.then_inc(self.sem, 1)

            def statistics(own, st, it, k, src):
                for b in range(B2):
                    q = st * B2 + b
                    if k:
                        dve.wait_ge(S[st]["res"], at(it, b, k - 1, 5))
                    else:
                        dve.wait_ge(x_loaded[st], 16 * it + 16)
                    ins = nc.vector.bn_stats(stats[:, q, :], src[:, q, :])
                    if b < B2 - 1:
                        own.note(ins)
                own(ins, alone=True)
                for b in range(B2):
                    q = st * B2 + b
                    nc.vector.bn_aggr(mv[:, q, :], stats[:, q, :]).then_inc(S[st]["mv"], 1)

            def normalise(st, it, k, src, out):
                dve.wait_ge(rstd_done[st], it * 6 + k + 1)
                dve.wait_ge(S[st]["mv"], at(it, B2 - 1, k, 6))
                if k == 5 and not opening(it):
                    dve.wait_ge(scattered[st], 16 * B2 * TOPK * it)
                    dve.wait_ge(ln_out[st], 16 * it)
                for b in range(B2):
                    q = st * B2 + b
                    nc.vector.tensor_scalar(out[:, q, :], src[:, q, :], mv[:, q, 0:1], rstd[:, q:q + 1], ALU.subtract,
                                            ALU.mult).then_inc(S[st]["ln"], 1)

            def norm(own, st, it, k, src, out):
                statistics(own, st, it, k, src)
                yield
                normalise(st, it, k, src, out)
                yield
                yield

            def heads_out_t(own, st, it, a, b):
                q = st * B2 + b
                dve.wait_ge(S[st]["den"], at(it, b, a, 3))
                dve.wait_ge(S[st]["o"], before(it, b, {0: 0, 1: 1, 2: 3}[a], 4) + 1)
                own(nc.vector.reciprocal(rden_t[:, st, :], den_t[:, st, :]))
                for g in range(4):
                    rows_g = slice(4 * DH * g, 4 * DH * (g + 1))
                    ins = nc.vector.tensor_tensor(o_t[rows_g, q, :], bank[0:4 * DH, q, g * P:(g + 1) * P],
                                                  rden_t[rows_g, st, :], ALU.mult)
                ins.then_inc(S[st]["o"], 1)

            def heads_out(own, st, it, b):
                q = st * B2 + b
                dve.wait_ge(S[st]["num_mm"], at(it, b))
                heads = bank[:, q, 0:H * DA].rearrange("p (h c) -> p h c", h=H)
                own(nc.vector.tensor_scalar(rden[:, q, :], heads[:, :, DH], M * FAV_EPS, None, ALU.add))
                own(nc.vector.reciprocal(rden[:, q, :], rden[:, q, :]))
                nc.vector.tensor_tensor(o[:, q, :].rearrange("p (h c) -> p h c", h=H), heads[:, :, 0:DH],
                                        rden[:, q, :].rearrange("p (h a) -> p h a", a=1).to_broadcast((P, H, DH)),
                                        ALU.mult).then_inc(S[st]["o"], 1)

            def attention(own, st, it, a, sk, between=iter(())):
                for b in range(B2):
                    for half in range(2):
                        dve.wait_ge(S[st]["sc_mm"], half_made(it, a, b, half))
                        place = qpad[:, st * B2 + b, :, 3 * DH].rearrange("p (g j) -> p j g", j=4)
                        nc.vector.tensor_reduce(place[:, 2 * half:2 * half + 2, :].bitcast(F32R),
                                                wide[:, st, :, :, 0:sk], AX, ALU.max, negate=True
                                                ).then_inc(S[st]["max"], 1)
                        yield
                next(between, None)
                yield
                for b in range(B2):
                    for _ in range(2):
                        next(between, None)
                        yield
                    heads_out_t(own, st, it, a, b)
                    yield

            def project(st, it, k, n_xb):
                if k == 3:
                    yield
                residual(st, it, k, n_xb)
                yield

            def residual(st, it, k, n_xb):
                for b in range(B2):
                    q = st * B2 + b
                    dve.wait_ge(S[st]["proj"], at(it, b, k, 5))
                    if k == 0 and not opening(it):
                        dve.wait_ge(res_out[st], 16 * it)
                    if n_xb is None:
                        base = x
                    else:
                        base = xb
                        dve.wait_ge(S[st]["xb"], at(it, b, n_xb, 4))
                    nc.vector.tensor_tensor(x[:, q, :], base[:, q, :], bank[:, q, 0:P], ALU.add
                                            ).then_inc(S[st]["res"], 1)

            def cross_queries(st, it, k, n_raw, scale, bias_tile):
                for b in range(B2):
                    q = st * B2 + b
                    dve.wait_ge(S[st]["qkv_mm"], at(it, b, k, 4))
                    nc.vector.scalar_tensor_tensor(qkv[:, q, 0:P], bank[:, q, 0:P], scale, bias_tile, ALU.mult, ALU.add
                                                   ).then_inc(S[st]["qkv"], 1)
                yield
                yield
                yield

            def layer0(st, it):
                own = Chain(st, it, 0 if opening(it) else -STEPS_P)
                statistics(own, st, it, 0, x_in)
                yield
                for b in range(B2):
                    q = st * B2 + b
                    dve.wait_ge(S[st]["ctx_mm"], at(it, b))
                    nc.vector.tensor_tensor(ckv[:, q, :, :].rearrange("p a c -> p (a c)"), bank[0:SK, q, :],
                                            bias("ctx")[0:SK, :], ALU.add).then_inc(S[st]["ckv"], 1)
                yield
                normalise(st, it, 0, x_in, ln)
                yield
                yield
                for b in range(B2):
                    q = st * B2 + b
                    dve.wait_ge(S[st]["qkv_mm"], at(it, b, 0, 4))
                    nc.vector.tensor_tensor(qkv[:, q, :], bank[:, q, 0:3 * P], bias("qkv0"), ALU.add
                                            ).then_inc(S[st]["qkv"], 1)
                for _ in range(7):
                    yield
                yield from attention(own, st, it, 0, P, iter(()) if opening(it) else places(own, st, it - 1))
                yield from project(st, it, 0, 0)
                yield from norm(own, st, it, 1, x, ln)
                yield from cross_queries(st, it, 1, 0, q_scale[:, 0:1], q_bias0[:, :])
                yield from attention(own, st, it, 1, SK)
                yield from project(st, it, 1, 1)
                yield from norm(own, st, it, 2, x, ln)
                residual(st, it, 2, None)
                assert own.n == STEPS0 + (0 if opening(it) else STEPS_P), own.n
                yield

            def layer1(st, it):
                own = Chain(st, it, STEPS0)
                yield from norm(own, st, it, 3, x, ln)
                yield
                for b in range(B2):
                    q = st * B2 + b
                    dve.wait_ge(S[st]["sq"], at(it, b))
                    nc.vector.tensor_reduce(norm2[:, q, :], sq[:, q, :].rearrange("p (h c) -> p h c", c=DH), AX, ALU.add
                                            ).then_inc(S[st]["norm2"], 1)
                yield
                for i in range(2):
                    for b in range(B2):
                        q = st * B2 + b
                        dve.wait_ge(S[st]["xw"], at(it, b, i, 2))
                        feats = bank[:, q, :].rearrange("p (h m) -> p h m", h=H)
                        cut = fmax[:, q, i * H:(i + 1) * H]
                        own(nc.vector.tensor_reduce(cut, feats, AX, ALU.max))
                        dve.wait_ge(S[st]["norm2"], at(it, b))
                        own(nc.vector.scalar_tensor_tensor(cut, norm2[:, q, i * H:(i + 1) * H], 0.5, cut, ALU.mult,
                                                           ALU.add))
                        nc.vector.tensor_tensor(phi[:, q, i, :].rearrange("p (h m) -> p h m", h=H), feats,
                                                cut.rearrange("p (h a) -> p h a", a=1).to_broadcast((P, H, M)),
                                                ALU.subtract).then_inc(S[st]["fsub"], 1)
                    yield
                for i in range(2):
                    for b in range(B2):
                        q = st * B2 + b
                        dve.wait_ge(S[st]["fexp"], at(it, b, i, 2))
                        nc.vector.tensor_scalar(phi[:, q, i, :], phi[:, q, i, :], FAV_EPS, None, ALU.add
                                                ).then_inc(S[st]["fphi"], 1)
                    yield
                for b in range(B2):
                    q = st * B2 + b
                    dve.wait_ge(S[st]["kv_mm"], at(it, b))
                    dve.wait_ge(S[st]["o"], at(it, B2 - 1, 1, 4))
                    nc.vector.tensor_tensor(kvb[:, q, :], bank[:, q, 0:H * DA], const("blocks"), ALU.mult
                                            ).then_inc(S[st]["kvb"], 1)
                yield
                for b in range(B2):
                    heads_out(own, st, it, b)
                yield
                yield from project(st, it, 3, 2)
                yield from norm(own, st, it, 4, x, ln)
                yield from cross_queries(st, it, 3, 1, SCALE, q_bias1[:, :])
                yield from attention(own, st, it, 2, SK)
                yield from project(st, it, 4, 3)
                yield from norm(own, st, it, 5, x, ln_r)
                yield
                yield from router(own, st, it)

            def router(own, st, it):
                two = slice(st * B2, st * B2 + B2)
                seqs = range(st * B2, st * B2 + B2)
                dve.wait_ge(gate_exp[st], it + 1)
                own(nc.vector.tensor_scalar(sc[:, two, :], sc[:, two, :], 1.0, None, ALU.add))
                own(nc.vector.reciprocal(sc[:, two, :], sc[:, two, :]))
                for q in seqs:
                    ins = nc.vector.tensor_tensor(sfc[:, q, :], sc[:, q, :], bias("gate"), ALU.add)
                own(ins, alone=True)
                for q in seqs:
                    for g in range(NG):
                        ins = nc.vector.max(top8[:, q, g, :], sfc[:, q, g * 8:(g + 1) * 8])
                own(ins)
                own(nc.vector.tensor_tensor(gsum[:, two, :], top8[:, two, :, 0], top8[:, two, :, 1], ALU.add))
                yield
                for q in seqs:
                    mine = gsum[:, q, :].rearrange("p (g a) -> p g a", a=1).to_broadcast((P, NG, NG))
                    theirs = gsum[:, q, :].rearrange("p (a g) -> p a g", a=1).to_broadcast((P, NG, NG))
                    nc.vector.tensor_tensor(more[:, q, :, :], theirs, mine, ALU.is_gt)
                    ins = nc.vector.tensor_tensor(least[:, q, :, :], theirs, mine, ALU.is_ge)
                own(ins)
                for q in seqs:
                    ins = nc.vector.tensor_tensor(least[:, q, :, :].rearrange("p a g -> p (a g)"),
                                                  least[:, q, :, :].rearrange("p a g -> p (a g)"), const("before"),
                                                  ALU.mult)
                own(ins)
                flat = "p b a g -> p (b a g)"
                own(nc.vector.tensor_tensor(more[:, two, :, :].rearrange(flat), more[:, two, :, :].rearrange(flat),
                                            least[:, two, :, :].rearrange(flat), ALU.max))
                own(nc.vector.tensor_reduce(glead[:, two, :], more[:, two, :, :], AX, ALU.add))
                own(nc.vector.tensor_scalar(glead[:, two, :], glead[:, two, :], TOPG - 0.5, None, ALU.is_lt))
                own(nc.vector.tensor_tensor(
                    masked[:, two, :].rearrange("p b (g c) -> p (b g) c", c=8),
                    sfc[:, two, :].rearrange("p b (g c) -> p (b g) c", c=8),
                    glead[:, two, :].rearrange("p b g -> p (b g)").rearrange("p (n a) -> p n a", a=1
                                                                             ).to_broadcast((P, B2 * NG, 8)), ALU.mult),
                    alone=True)
                for q in seqs:
                    ins = nc.vector.max(best[:, q, :], masked[:, q, :])
                own(ins, alone=True)
                for q in seqs:
                    ins = nc.vector.match_replace(taken[:, q, :], best[:, q, :], masked[:, q, :], GONE)
                own(ins)
                nc.vector.tensor_scalar(chosenb[:, two, :], taken[:, two, :], GONE / 2, None, ALU.is_lt)
                own(nc.vector.tensor_scalar(chosen[:, two, :], taken[:, two, :], GONE / 2, None, ALU.is_lt))
                dve.sem_inc(routed[st], 1)
                yield
                yield
                dve.wait_ge(route_mm[st], 2 * it + 2)
                for q in seqs:
                    b = q - st * B2
                    ins = nc.vector.tensor_tensor(slot[:, q, :], bank[:, st * B2 + 1, b * E:(b + 1) * E],
                                                  const("first_slot"), ALU.add)
                own(ins)
                dve.sem_inc(routed[st], 1)
                for q in seqs:
                    own(nc.vector.tensor_tensor(total[:, :], total[:, :], chosen[:, q, :], ALU.add))
                own(nc.vector.tensor_copy(totalb[:, :], total[:, :]))
                assert own.n == STEPS1, own.n
                yield

            def places(own, st, it):
                two = slice(st * B2, st * B2 + B2)
                seqs = range(st * B2, st * B2 + B2)
                own(nc.vector.tensor_tensor(gw[:, two, :], chosen[:, two, :], sc[:, two, :], ALU.mult))
                own(nc.vector.tensor_reduce(wsum[:, two], gw[:, two, :], AX, ALU.add))
                own(nc.vector.tensor_scalar(wsum[:, two], wsum[:, two], 1e-20, None, ALU.add))
                own(nc.vector.reciprocal(wsum[:, two], wsum[:, two]))
                own(nc.vector.tensor_scalar(wsum[:, two], wsum[:, two], ROUTED, None, ALU.mult))
                own(nc.vector.tensor_tensor(gw[:, two, :], gw[:, two, :],
                                            wsum[:, two].rearrange("p (b a) -> p b a", a=1).to_broadcast((P, B2, E)),
                                            ALU.mult))
                yield
                own(nc.vector.tensor_tensor(slot[:, two, :], slot[:, two, :], chosen[:, two, :], ALU.mult), alone=True)
                for q in seqs:
                    ins = nc.vector.max(slot8[:, q, :], slot[:, q, :])
                own(ins)
                own(nc.vector.tensor_scalar(idx[:, two, :], slot8[:, two, :], -1.0, None, ALU.add))
                for q in seqs:
                    for j in range(TOPK):
                        ins = nc.vector.scalar_tensor_tensor(picks_of[st][:, j, :], slot[:, q, :], slot8[:, q, j:j + 1],
                                                             gw[:, q, :], ALU.is_equal, ALU.mult,
                                                             accum_out=w8[:, q, j:j + 1])
                    own(ins)
                    if q == seqs[0]:
                        yield
                at_turn = bass.ds(it * (G * 8) + st * (B2 * 8), B2 * 8)
                nc.vector.tensor_copy(idx_all[:, at_turn], idx[:, two, :].rearrange("p b j -> p (b j)"))
                own(nc.vector.tensor_copy(w_all[:, at_turn], w8[:, two, :].rearrange("p b j -> p (b j)")))
                dve.sem_inc(routed[st], 1)
                yield

            turns(dve, layer0, layer1)
            for st in range(2):
                for _ in places(Chain(st, TURNS, -STEPS_P), st, TURNS - 1):
                    pass

            done = 2

            def late(ins):
                nonlocal done
                done += 1
                ins.then_inc(dve_step, 1)
                dve.wait_ge(dve_step, done)

            dve.wait_ge(counted, 1)
            late(nc.vector.tensor_scalar(room[:, :], bank[:, 0, 0:E], float(LAST), None, ALU.is_le))
            late(nc.vector.tensor_tensor(empty[:, :], room[:, :], const("last_tile"), ALU.mult))
            late(nc.vector.tensor_reduce(spare[:, :], empty[:, :], AX, ALU.max))
            late(nc.vector.tensor_tensor(tail_f[:, :], bank[:, 0, 0:E], const("first_slot"), ALU.add))
            late(nc.vector.tensor_scalar(tail_f[:, :], tail_f[:, :], -1.0, spare[:, 0:1], ALU.add, ALU.subtract))
            late(nc.vector.tensor_tensor(tail_f[:, :], tail_f[:, :], room[:, :], ALU.mult))
            nc.vector.tensor_scalar(tail_i[:, :], tail_f[:, :], spare[:, 0:1], None, ALU.add).then_inc(tables, 1)
            late(nc.vector.tensor_scalar(n_int[:, :], bank[:, 0, 0:E], float(P - 1), None, ALU.add))
            late(nc.vector.tensor_scalar(n_int[:, :], n_int[:, :], 7, None, ALU.arith_shift_right))
            late(nc.vector.tensor_copy(n_tiles[:, :], n_int[:, :]))
            late(nc.vector.tensor_tensor_scan(upto[:, :], ones_e[:, :], n_tiles[:, :], 0.0, ALU.mult, ALU.add))
            for c in range(TCOLS):
                tile_no = const("tile_no")[:, c:c + 1]
                late(nc.vector.scalar_tensor_tensor(past[:, :], upto[:, :], tile_no, ones_e[:, :], ALU.is_le, ALU.mult,
                                                    accum_out=which[:, c:c + 1]))
                late(nc.vector.scalar_tensor_tensor(past[:, :], upto[:, :], tile_no, n_tiles[:, :], ALU.is_le, ALU.mult,
                                                    accum_out=skipped[:, c:c + 1]))
            late(nc.vector.tensor_tensor(skipped[:, :], const("tile_no"), skipped[:, :], ALU.subtract))
            late(nc.vector.tensor_scalar(skipped[:, :], skipped[:, :], float(P), None, ALU.mult))
            late(nc.vector.scalar_tensor_tensor(skipped[:, :], which[:, :], float(REGION), skipped[:, :], ALU.mult,
                                                ALU.add))
            late(nc.vector.tensor_scalar(skipped[:, :], skipped[:, :], spare[:, 0:1], None, ALU.subtract))
            late(nc.vector.scalar_tensor_tensor(skipped[:, :], which[:, :], E - 0.5, skipped[:, :], ALU.is_lt,
                                                ALU.mult))
            late(nc.vector.tensor_scalar(rowf[:, 0:TCOLS], skipped[:, :], spare[:, 0:1], None, ALU.add))
            late(nc.vector.tensor_scalar(rowf[:, TCOLS:], which[:, :], float(E - 1), None, ALU.min))
            nc.vector.tensor_copy(rowi[:, :], rowf[:, :]).then_inc(tables, 1)
            late(nc.vector.tensor_tensor(shift[:, :], upto[:, :], n_tiles[:, :], ALU.subtract))
            late(nc.vector.tensor_scalar(shift[:, :], shift[:, :], float(P), 1.0, ALU.mult, ALU.add))
            late(nc.vector.tensor_tensor(shift[:, :], shift[:, :], const("first_slot"), ALU.subtract))
            late(nc.vector.tensor_scalar(of_all[:, :], idx_all[:, :], REGION.bit_length() - 1, None,
                                         ALU.arith_shift_right))

            def moves(it, step):
                seq = bass.ds(it * 8, 8)
                mine = of[:, :].rearrange("p (j a) -> p j a", a=1).to_broadcast((P, TOPK, E))
                every = const("expert").rearrange("p (a e) -> p a e", a=1).to_broadcast((P, TOPK, E))
                by = shift[:, :].rearrange("p (a e) -> p a e", a=1).to_broadcast((P, TOPK, E))
                if step:
                    dve.wait_ge(moving, it * 5 + step)
                if step == 0:
                    ins = nc.vector.tensor_copy(of[:, :], of_all[:, seq])
                elif step == 1:
                    ins = nc.vector.tensor_tensor(same[:, :, :], every, mine, ALU.is_equal)
                elif step == 2:
                    ins = nc.vector.tensor_tensor(same[:, :, :], same[:, :, :], by, ALU.mult)
                elif step == 3:
                    ins = nc.vector.tensor_reduce(moved[:, :], same[:, :, :], AX, ALU.add)
                else:
                    ins = nc.vector.tensor_tensor(row_all[:, seq], moved[:, :], idx_all[:, seq], ALU.add)
                ins.then_inc(moving, 1)

            def experts_turn(it, first, last):
                for u in range(TU):
                    t = it * TU + u
                    if not (first and u < 2) and not (last and u >= 2):
                        e = entry(t - 2 + TCOLS * P, E - 1, mybir.EngineType.DVE)
                        if not (first and u < 6):
                            dve.wait_ge(y_mm, t - 5)
                        nc.vector.tensor_copy(down_of[:, (u - 2) % 4, :], w_down[:, bass.ds(e * P, P)])
                        dve.wait_ge(g_act, t - 1)
                        nc.vector.tensor_tensor(hid_t[:, (u - 2) % 4, :], act_g[:, (u - 2) % 4, :],
                                                bank8[2 + u % 2][0:I, P:2 * P], ALU.mult).then_inc(h_done, 1)
                    if not last and 2 <= u < 7:
                        moves(it, u - 2)

            dve.wait_ge(table_in, 32)
            dve.wait_ge(down_in, 32)
            experts_turn(0, True, False)
            with dve.Fori(1, NT // TU) as it:
                experts_turn(it, False, False)
            experts_turn(NT // TU, False, True)

            def sums(it):
                for u in range(2):
                    dve.wait_ge(g_act, NT + it * 2 + u + 1)
                    nc.vector.tensor_tensor(s_hid[:, u, :], s_act[:, u, :], bank8[2 + u][:, 2 * I:4 * I], ALU.mult
                                            ).then_inc(h_done, 1)
                for u in range(2):
                    t = it * 2 + u
                    dve.wait_ge(y_mm, NT + t + 1)
                    dve.wait_ge(tok_in[2 + u], FETCHES + 16 * it + 16)
                    if not opening(it):
                        dve.wait_ge(tok_in[4 + u], FETCHES + 16 * it)
                    nc.vector.tensor_tensor(acc[:, u, :], res[:, u, :], bank8[4 + u][:, 0:P], ALU.add
                                            ).then_inc(acc_step, 1)
                    dve.wait_ge(gathered[u], 16 * TOPK * (it + 1))
                    for j in range(TOPK):
                        dve.wait_ge(acc_step, t * TOPK + j + 1)
                        ins = nc.vector.scalar_tensor_tensor(
                            acc[:, u, :], got[:, u, j, :], w_all[:, bass.ds(it * 16 + u * 8 + j, 1)], acc[:, u, :],
                            ALU.mult, ALU.add)
                        ins.then_inc(acc_step if j < TOPK - 1 else summed, 1)

            sums(0)
            with dve.Fori(1, NSEQ // 2) as it:
                sums(it)


BEATS0, BEATS1 = 45, 39
STEPS0, STEPS_P, STEPS1 = 10, 12, 38




def shape_tables():
    at, n = columns(CONSTS)
    c = np.zeros((P, n), np.float32)

    def put(name, value):
        c[:, at[name][0]:at[name][1]] = value

    i = np.arange(P)
    put("ident", np.eye(P))
    put("causal", np.where(i[None, :] > i[:, None], -1e10, 0.0))
    put("causal_t", np.where(i[:, None] > i[None, :], -1e10, 0.0))
    put("upper", i[:, None] < i[None, :])
    theta = 1.0 / 10000.0 ** (2.0 * np.arange(DH // 2, dtype=np.float32) / DH)
    ang = (i[:, None].astype(np.float32) * theta[None, :].astype(np.float32)).astype(np.float32)
    cos = np.repeat(np.cos(ang)[:, None, :, None], 2, 3).reshape(P, 1, DH)
    sin = np.stack([-np.sin(ang), np.sin(ang)], -1).reshape(P, 1, DH)
    both = np.repeat(np.array([SCALE, 1.0]), H)[None, :, None]
    put("rope_c", (both * cos).reshape(P, -1))
    put("rope_s", (both * sin).reshape(P, -1))
    put("blocks", np.tile(np.repeat(i[:, None] // M == np.arange(4)[None, :], DA, 1), (1, 4)))
    put("first_slot", np.arange(E)[None, :] * REGION + 1)
    put("last_tile", np.arange(E)[None, :] * REGION + LAST)
    put("tile_no", i[:, None] + P * np.arange(TCOLS)[None, :])
    put("expert", np.arange(E)[None, :])
    g = np.arange(NG)
    put("before", (g[None, :] < g[:, None]).reshape(1, -1))
    return c


def kernel(**inputs):
    import concourse.bacc as bacc
    from concourse.bass_utils import run_bass_kernel_spmd

    a = {k: np.asarray(v) for k, v in inputs.items()}
    t = lambda name: a[name].T
    c0, c1, f = "L0_xattn_", "L1_xattn_", "L1_attn_"
    proj = np.zeros((H, DH, H, M), np.float32)
    proj[np.arange(H), :, np.arange(H), :] = a["L1_attn_proj"].transpose(0, 2, 1)
    shared_gu = np.concatenate([t("L1_ffn_Sg"), t("L1_ffn_Su")], 1)
    weight = np.concatenate([
        t("L0_attn_wq"), t("L0_attn_wk"), t("L0_attn_wv"), t("L0_attn_wp"), t(c0 + "Wq"),
        t(c0 + "Wk"), t(c0 + "Wv"), a[c1 + "Wk"], a[c1 + "Wv"], t(c0 + "Wo"), t("L0_ffn_weight"),
        t(f + "Wq"), t(f + "Wk"), t(f + "Wv"), proj.reshape(P, H * M), t(f + "Wo"), a[c1 + "Wq"], a[c1 + "Wo"],
        t("L1_ffn_gate_w"), shared_gu], 1)
    bias = np.concatenate([
        a["L0_attn_bq"], a["L0_attn_bk"], a["L0_attn_bv"], a["L0_attn_bp"], a[c0 + "bq"], a[c0 + "bk"], a[c0 + "bv"],
        a[c1 + "bk"], a[c1 + "bv"], a[c0 + "bo"], a[f + "bo"], a[c1 + "bq"], a[c1 + "bo"], a["L1_ffn_gate_bias"]])
    w_gu = np.stack([a["L1_ffn_Wg"], a["L1_ffn_Wu"]], 1).transpose(3, 0, 1, 2).reshape(P, E * 2 * I)
    arrays = {
        "x_d": a["x"], "ctx_d": a["ctx_1024"], "mask_d": a["mask_1x1xSxS2_ik0"].reshape(P, SK),
        "const_d": shape_tables(), "bias_d": np.broadcast_to(bias[None, :], (P, bias.size)), "weight_d": weight,
        "wgu_d": w_gu, "wdown_d": a["L1_ffn_Wd"].transpose(2, 0, 1).reshape(I, E * P),
        "sdown_d": a["L1_ffn_Sd"].T.reshape(2, I, P).transpose(1, 0, 2).reshape(I, 2 * P)}
    arrays = {k: np.ascontiguousarray(v) for k, v in arrays.items()}
    nc = bacc.Bacc("TRN2", target_bir_lowering=False, num_devices=1)
    args = [nc.dram_tensor(k, v.shape, mybir.dt.from_np(v.dtype), kind="ExternalInput").ap() for k, v in arrays.items()]
    args.append(nc.dram_tensor("out_d", (NSEQ, P, P), F32, kind="ExternalOutput").ap())
    for name, shape, dt in [("xs_d", (ROWS, P), F32), ("ys_d", (NT, P, P), F32), ("ln_d", (NSEQ, P, P), F32),
                            ("res_d", (NSEQ, P, P), F32), ("tab_d", (2 * TCOLS * P,), I32)]:
        args.append(nc.dram_tensor(name, shape, dt).ap())
    build(nc, *args)
    r = run_bass_kernel_spmd(nc, [arrays], core_ids=[0])
    return r.results[0]["out_d"]
```
